# Optimizing a Trainium2 kernel written in Bass

```python
import numpy as np
import jax
import jax.numpy as jnp

def _softmax(x, axis=-1):
    return jax.nn.softmax(x, axis=axis)

def _gelu(x):
    return jax.nn.gelu(x, approximate=True)

def _silu(x):
    return jax.nn.silu(x)

def _sigmoid(x):
    return jax.nn.sigmoid(x)

def _layernorm(x, axis=-1, eps=1e-05):
    m = jnp.mean(x, axis=axis, keepdims=True)
    v = jnp.var(x, axis=axis, keepdims=True)
    return (x - m) / jnp.sqrt(v + eps)

def _scatter_add(tgt, idx, src, axis=0):
    return tgt.at[idx].add(src)

def _segment_sum(src, seg, n):
    return jax.ops.segment_sum(src, seg, n)
kernel_name = 'mk_macaron_d2_jaxref_r8_e85d33'

def setup_inputs(seed: int=0):
    np.random.seed(seed)
    _w = jnp.asarray

    def _L0_attn_setup():
        import jax, jax.numpy as jnp
        import numpy as np
        H = 16
        EPS_DEN = 1e-06

        def _decay_scan(x, decay, init):
            xT = jnp.moveaxis(x, 2, 0)

            def step(s, xt):
                s = decay * s + xt
                return (s, s)
            _, ys = jax.lax.scan(step, init, xT)
            return jnp.moveaxis(ys, 0, 2)

        def _phi(z):
            return jax.nn.elu(z) + 1.0

        def _reference_tuple_inner(x, w_qkv, w_out, decay_param):
            B, T, Hid = x.shape
            D = Hid // H
            qkv = x @ w_qkv
            q, k, v = jnp.split(qkv, 3, axis=-1)

            def to_bhtd(t):
                return t.reshape(B, T, H, D).transpose(0, 2, 1, 3)
            q = _phi(to_bhtd(q))
            k = _phi(to_bhtd(k))
            v = to_bhtd(v)
            decay = jax.nn.sigmoid(decay_param).reshape(1, H, 1)
            init = jnp.zeros((B, H, D), dtype=x.dtype)
            running_kv = _decay_scan(k * v, decay, init)
            running_ksum = _decay_scan(k, decay, init)
            den = jnp.clip(jnp.sum(q * running_ksum, axis=-1, keepdims=True), EPS_DEN, None)
            out = q * running_kv / den
            out = out.transpose(0, 2, 1, 3).reshape(B, T, Hid) @ w_out
            new_kv = running_kv[:, :, -1, :]
            new_ksum = running_ksum[:, :, -1, :]
            return (out, new_kv, new_ksum)
        key = jax.random.key(seed)
        k1, k2, k3 = jax.random.split(key, 3)
        x = jax.random.normal(k1, (2, 512, 256), dtype=jnp.float32)
        w_qkv = jax.random.normal(k2, (256, 768), dtype=jnp.float32) * 0.02
        w_out = jax.random.normal(k3, (256, 256), dtype=jnp.float32) * 0.02
        decay_param = jnp.full((H,), 0.95, dtype=jnp.float32)
        return {'x': x, 'w_qkv': w_qkv, 'w_out': w_out, 'decay_param': decay_param}
    _L0_attn_in = _L0_attn_setup()

    def _L0_ffn_setup():
        import jax, jax.numpy as jnp
        import numpy as np
        B, S, D_IN, D_OUT, E = (4, 128, 256, 256, 32)
        MASK_DENSITY = 0.3
        THRESH = 0.5
        key = jax.random.key(seed)
        k_x, k_w, k_m, k_r = jax.random.split(key, 4)
        x = jax.random.normal(k_x, (B, S, D_IN), dtype=jnp.float32)
        bound = np.sqrt(1.0 / D_IN) * np.sqrt(3.0)
        weight = jax.random.uniform(k_w, (D_OUT, D_IN), minval=-bound, maxval=bound, dtype=jnp.float32)
        scale = jnp.ones((D_OUT,), dtype=jnp.float32)
        expert_masks = (jax.random.uniform(k_m, (E, D_OUT, D_IN)) < MASK_DENSITY).astype(jnp.float32)
        router_w = 0.01 * jax.random.normal(k_r, (E, D_IN), dtype=jnp.float32)
        return {'x': x, 'weight': weight, 'scale': scale, 'expert_masks': expert_masks, 'router_w': router_w}
    _L0_ffn_in = _L0_ffn_setup()

    def _L1_attn_setup():
        import jax, jax.numpy as jnp
        import numpy as np
        EMBED_DIM = 256
        NUM_HEADS = 16
        HEAD_DIM = EMBED_DIM // NUM_HEADS
        key = jax.random.key(seed)
        ks = jax.random.split(key, 9)
        B, S, D = (2, 256, EMBED_DIM)
        scale = 1.0 / np.sqrt(D)
        inp = {'x': jax.random.normal(ks[0], (B, S, D), dtype=jnp.float32), 'wq': jax.random.normal(ks[1], (D, D), dtype=jnp.float32) * scale, 'bq': jnp.zeros((D,), dtype=jnp.float32), 'wk': jax.random.normal(ks[2], (D, D), dtype=jnp.float32) * scale, 'bk': jnp.zeros((D,), dtype=jnp.float32), 'wv': jax.random.normal(ks[3], (D, D), dtype=jnp.float32) * scale, 'bv': jnp.zeros((D,), dtype=jnp.float32), 'wo': jax.random.normal(ks[4], (D, D), dtype=jnp.float32) * scale, 'bo': jnp.zeros((D,), dtype=jnp.float32)}
        return inp
    _L1_attn_in = _L1_attn_setup()

    def _L1_ffn_setup():
        import jax, jax.numpy as jnp
        import numpy as np
        N_HEAD = 16
        N_EMBD = 256
        R = 8
        HEAD_DIM = N_EMBD // N_HEAD
        D_STD = HEAD_DIM - R
        THRESHOLD = 0.1
        B, T = (4, 128)
        key = jax.random.key(seed)
        k1, k2, k3, k4, k5 = jax.random.split(key, 5)
        fused_dim = 2 * N_HEAD * D_STD + N_EMBD + 2 * N_HEAD * R
        x = jax.random.normal(k1, (B, T, N_EMBD), dtype=jnp.float32)
        Wa = jax.random.normal(k2, (N_EMBD, fused_dim), dtype=jnp.float32) * 0.02
        Wp = jax.random.normal(k3, (N_EMBD, N_EMBD), dtype=jnp.float32) * 0.02
        w_std = jax.random.uniform(k4, (N_HEAD,), dtype=jnp.float32, minval=0.3, maxval=0.7)
        w_rec = jax.random.uniform(k5, (N_HEAD,), dtype=jnp.float32)
        return {'x': x, 'Wa': Wa, 'Wp': Wp, 'w_std': w_std, 'w_rec': w_rec}
    _L1_ffn_in = _L1_ffn_setup()
    _d = {'L0_attn_x': _L0_attn_in['x'], 'L0_attn_w_qkv': _L0_attn_in['w_qkv'], 'L0_attn_w_out': _L0_attn_in['w_out'], 'L0_attn_decay_param': _L0_attn_in['decay_param'], 'L0_ffn_weight': _L0_ffn_in['weight'], 'L0_ffn_scale': _L0_ffn_in['scale'], 'L0_ffn_expert_masks': _L0_ffn_in['expert_masks'], 'L0_ffn_router_w': _L0_ffn_in['router_w'], 'L1_attn_wq': _L1_attn_in['wq'], 'L1_attn_bq': _L1_attn_in['bq'], 'L1_attn_wk': _L1_attn_in['wk'], 'L1_attn_bk': _L1_attn_in['bk'], 'L1_attn_wv': _L1_attn_in['wv'], 'L1_attn_bv': _L1_attn_in['bv'], 'L1_attn_wo': _L1_attn_in['wo'], 'L1_attn_bo': _L1_attn_in['bo'], 'L1_ffn_Wa': _L1_ffn_in['Wa'], 'L1_ffn_Wp': _L1_ffn_in['Wp'], 'L1_ffn_w_std': _L1_ffn_in['w_std'], 'L1_ffn_w_rec': _L1_ffn_in['w_rec']}
    _x0 = _d['L0_attn_x']
    _d['L0_attn_x'] = jax.random.normal(jax.random.fold_in(jax.random.key(seed), 1), (8, 512, 256), dtype=_x0.dtype)
    del _x0
    return _d

def reference(L0_attn_x, L0_attn_w_qkv, L0_attn_w_out, L0_attn_decay_param, L0_ffn_weight, L0_ffn_scale, L0_ffn_expert_masks, L0_ffn_router_w, L1_attn_wq, L1_attn_bq, L1_attn_wk, L1_attn_bk, L1_attn_wv, L1_attn_bv, L1_attn_wo, L1_attn_bo, L1_ffn_Wa, L1_ffn_Wp, L1_ffn_w_std, L1_ffn_w_rec):

    def _L0_attn_ref(x, w_qkv, w_out, decay_param):
        import jax, jax.numpy as jnp
        import numpy as np
        H = 16
        EPS_DEN = 1e-06

        def _decay_scan(x, decay, init):
            xT = jnp.moveaxis(x, 2, 0)

            def step(s, xt):
                s = decay * s + xt
                return (s, s)
            _, ys = jax.lax.scan(step, init, xT)
            return jnp.moveaxis(ys, 0, 2)

        def _phi(z):
            return jax.nn.elu(z) + 1.0

        def _reference_tuple_inner(x, w_qkv, w_out, decay_param):
            B, T, Hid = x.shape
            D = Hid // H
            qkv = x @ w_qkv
            q, k, v = jnp.split(qkv, 3, axis=-1)

            def to_bhtd(t):
                return t.reshape(B, T, H, D).transpose(0, 2, 1, 3)
            q = _phi(to_bhtd(q))
            k = _phi(to_bhtd(k))
            v = to_bhtd(v)
            decay = jax.nn.sigmoid(decay_param).reshape(1, H, 1)
            init = jnp.zeros((B, H, D), dtype=x.dtype)
            running_kv = _decay_scan(k * v, decay, init)
            running_ksum = _decay_scan(k, decay, init)
            den = jnp.clip(jnp.sum(q * running_ksum, axis=-1, keepdims=True), EPS_DEN, None)
            out = q * running_kv / den
            out = out.transpose(0, 2, 1, 3).reshape(B, T, Hid) @ w_out
            new_kv = running_kv[:, :, -1, :]
            new_ksum = running_ksum[:, :, -1, :]
            return (out, new_kv, new_ksum)
        return _reference_tuple_inner(x, w_qkv, w_out, decay_param)[0]

    def _L0_ffn_ref(x, weight, scale, expert_masks, router_w):
        import jax, jax.numpy as jnp
        import numpy as np
        B, S, D_IN, D_OUT, E = (4, 128, 256, 256, 32)
        MASK_DENSITY = 0.3
        THRESH = 0.5
        logits = jnp.einsum('bsd,ed->bse', x, router_w)
        probs = jax.nn.softmax(logits, axis=-1)
        top1_w = jnp.max(probs, axis=-1)
        top1_idx = jnp.argmax(probs, axis=-1)
        w_q = jnp.clip(jnp.round(weight / THRESH), -1.0, 1.0)
        w_scaled = w_q * scale[:, None]
        out0 = jnp.zeros((x.shape[0], x.shape[1], weight.shape[0]), dtype=x.dtype)

        def body(out, inputs):
            e_idx, mask_e = inputs
            y = jnp.einsum('bsi,oi->bso', x, w_scaled * mask_e)
            sel = (top1_idx == e_idx)[..., None]
            out = jnp.where(sel, y * top1_w[..., None], out)
            return (out, None)
        out, _ = jax.lax.scan(body, out0, (jnp.arange(E), expert_masks))
        return out

    def _L1_attn_ref(x, wq, bq, wk, bk, wv, bv, wo, bo):
        import jax, jax.numpy as jnp
        import numpy as np
        EMBED_DIM = 256
        NUM_HEADS = 16
        HEAD_DIM = EMBED_DIM // NUM_HEADS
        B, S, D = x.shape
        H, Hd = (NUM_HEADS, HEAD_DIM)
        q = (x @ wq.T + bq).reshape(B, S, H, Hd).transpose(0, 2, 1, 3)
        k = (x @ wk.T + bk).reshape(B, S, H, Hd).transpose(0, 2, 1, 3)
        v = (x @ wv.T + bv).reshape(B, S, H, Hd).transpose(0, 2, 1, 3)
        scores = jnp.einsum('bhqd,bhkd->bhqk', q, k) / jnp.sqrt(jnp.asarray(Hd, x.dtype))
        weights = jax.nn.softmax(scores, axis=-1)
        out = jnp.einsum('bhqk,bhkd->bhqd', weights, v)
        out = out.transpose(0, 2, 1, 3).reshape(B, S, D)
        return out @ wo.T + bo

    def _L1_ffn_ref(x, Wa, Wp, w_std, w_rec):
        import jax, jax.numpy as jnp
        import numpy as np
        N_HEAD = 16
        N_EMBD = 256
        R = 8
        HEAD_DIM = N_EMBD // N_HEAD
        D_STD = HEAD_DIM - R
        THRESHOLD = 0.1
        B, T = (4, 128)
        Bx, Tx, C = x.shape
        H, D, Ds, r = (N_HEAD, HEAD_DIM, D_STD, R)
        s_std = jnp.sqrt(jnp.clip(w_std, 1e-08, None))
        s_rec = jnp.sqrt(jnp.clip(w_rec, 1e-08, None))
        col_scale = jnp.concatenate([jnp.repeat(s_std, Ds), jnp.repeat(s_std, Ds), jnp.ones((C,), dtype=x.dtype), jnp.repeat(s_rec, r), jnp.repeat(s_rec, r)])
        Wb = Wa * col_scale[None, :]
        fused = x @ Wb
        q_std_end = H * Ds
        k_std_end = q_std_end + H * Ds
        v_end = k_std_end + C
        q_low_end = v_end + H * r

        def heads(t, d):
            return t.reshape(Bx, Tx, H, d).transpose(0, 2, 1, 3)
        Q_std = heads(fused[..., :q_std_end], Ds)
        K_std = heads(fused[..., q_std_end:k_std_end], Ds)
        V = heads(fused[..., k_std_end:v_end], D)
        Q_low = heads(fused[..., v_end:q_low_end], r)
        K_low = heads(fused[..., q_low_end:], r)
        use_ra = (w_rec > THRESHOLD)[None, :, None, None]
        q_tail = jnp.where(use_ra, K_low, Q_low)
        k_tail = jnp.where(use_ra, Q_low, K_low)
        Qf = jnp.concatenate([Q_std, q_tail], axis=-1)
        Kf = jnp.concatenate([K_std, k_tail], axis=-1)
        scale = 1.0 / jnp.sqrt(jnp.asarray(D, dtype=x.dtype))
        scores = jnp.einsum('bhtd,bhsd->bhts', Qf, Kf) * scale
        causal = jnp.tril(jnp.ones((Tx, Tx), dtype=bool))
        scores = jnp.where(causal[None, None], scores, jnp.finfo(scores.dtype).min)
        attn = jax.nn.softmax(scores, axis=-1)
        out = jnp.einsum('bhts,bhsd->bhtd', attn, V)
        y = out.transpose(0, 2, 1, 3).reshape(Bx, Tx, C)
        return y @ Wp
    x = L0_attn_x
    x = x + 0.5 * _L0_ffn_ref(_layernorm(x, axis=-1), L0_ffn_weight, L0_ffn_scale, L0_ffn_expert_masks, L0_ffn_router_w)
    x = x + _L0_attn_ref(_layernorm(x, axis=-1), L0_attn_w_qkv, L0_attn_w_out, L0_attn_decay_param)
    x = x + 0.5 * _L0_ffn_ref(_layernorm(x, axis=-1), L0_ffn_weight, L0_ffn_scale, L0_ffn_expert_masks, L0_ffn_router_w)
    x = x + 0.5 * _L1_ffn_ref(_layernorm(x, axis=-1), L1_ffn_Wa, L1_ffn_Wp, L1_ffn_w_std, L1_ffn_w_rec)
    x = x + _L1_attn_ref(_layernorm(x, axis=-1), L1_attn_wq, L1_attn_bq, L1_attn_wk, L1_attn_bk, L1_attn_wv, L1_attn_bv, L1_attn_wo, L1_attn_bo)
    x = x + 0.5 * _L1_ffn_ref(_layernorm(x, axis=-1), L1_ffn_Wa, L1_ffn_Wp, L1_ffn_w_std, L1_ffn_w_rec)
    return x

_drawn_inputs = setup_inputs


def setup_inputs(seed=0):
    import zlib

    import numpy as np

    out = dict(_drawn_inputs(seed))
    spreads = {'L0_attn_decay_param': (0.949999988079071, 0.6),
     'L0_ffn_scale': (1.0, 0.2),
     'L1_attn_bq': (0.0, 0.762),
     'L1_attn_bk': (0.0, 0.8),
     'L1_attn_bv': (0.0, 0.1),
     'L1_attn_bo': (0.0, 0.1)}
    factors = {'L0_attn_w_qkv': 8.0,
     'L0_attn_w_out': 8.0,
     'L1_ffn_Wa': 4.046,
     'L1_ffn_Wp': 4.037,
     'L1_ffn_w_std': 8.0,
     'L1_ffn_w_rec': 8.0}
    for name, (base, spread) in spreads.items():
        noise = np.random.default_rng([zlib.crc32(name.encode()), seed]).standard_normal(out[name].shape)
        drawn = base * np.exp(spread * noise) if base else spread * noise
        out[name] = jnp.asarray(drawn.astype(out[name].dtype))
    for name, factor in factors.items():
        out[name] = (out[name] * factor).astype(out[name].dtype)
    return out
```

```python
from contextlib import ExitStack

import concourse.bass as bass
from concourse import mybir

F32 = mybir.dt.float32
BF16 = mybir.dt.bfloat16
I32 = mybir.dt.int32
ALU = mybir.AluOpType
ACT = mybir.ActivationFunctionType
AX_X = mybir.AxisListType.X

P = 128
NBATCH, T, C = 8, 512, 256
TPB = T // P
NT = NBATCH * TPB
KC = C // P
H, HD = 16, 16
E = 32
NSLOT = 64
EPS = 1e-5
G = 4
NG = H // G
SLOT = 32
MASKED = -1.0e30
ROWS = 98
PARTS_Q = (0, 1, 2, 0, 1, 0)
PARTS_K = (0, 0, 0, 1, 1, 2)


def macaron_kernel(nc, x_in, dec_wqkv, dec_wout, dec_param, ffn_w, ffn_scale, ffn_masks, ffn_router,
                   full_wq, full_wk, full_wv, full_wo, full_bq, full_bk, full_bv, full_bo,
                   cau_wq, cau_wk, cau_wv, cau_wo, cau_std, cau_rec, out, layers):
    ctx = ExitStack()
    with ctx:
        def sb(name, shape, dt=F32):
            return ctx.enter_context(nc.sbuf_tensor(name, shape, dt))

        pb = ctx.enter_context(nc.psum_tensor("pb", [P, 8, 512], F32))

        xn_dram = nc.dram_tensor("xn_dram", [NT * P, C], F32).ap()
        slots_dram = nc.dram_tensor("slots_dram", [NSLOT * P, C], F32).ap()

        x_sb = sb("x_sb", [P, NT, C])
        xn = sb("xn", [P, TPB, C])
        xnT = sb("xnT", [P, KC, T])
        stats = sb("stats", [P, TPB, 6])
        mv = sb("mv", [P, TPB, 2])
        rstd = sb("rstd", [P, TPB])
        var_eps = sb("var_eps", [P, TPB])
        powers = sb("powers", [P, 64])
        ident = sb("ident", [P, P])
        ident_bf = sb("ident_bf", [P, P], BF16)
        mask_ts = sb("mask_ts", [P, P], BF16)
        mask_st = sb("mask_st", [P, P], BF16)
        arena = sb("arena", [P, E * KC * C])
        w_exp = arena[:, :].rearrange("p (e n) -> p e n", e=E)
        qst = arena[:, 0:4096].bitcast(BF16)
        kst = arena[:, 4096:8192].bitcast(BF16)
        qst_h = qst.rearrange("p (h t) -> p h t", h=H)
        kst_h = kst.rearrange("p (h t) -> p h t", h=H)
        probs = arena[:, 8192:16384].rearrange("p (r g n) -> p r g n", r=2, g=G)
        wdec = sb("wdec", [P, KC, 3 * C])
        wdec_out = sb("wdec_out", [P, KC, C])
        router = sb("router", [P, KC, E])
        scale_b = sb("scale_b", [P, C])
        wfull = sb("wfull", [P, KC, 3, C])
        wfull_out = sb("wfull_out", [P, NG, C])
        wcau = sb("wcau", [P, KC, 3, C])
        wcau_out = sb("wcau_out", [P, NG, C])
        bias_qk = sb("bias_qk", [P, 2, KC])
        bias_v = sb("bias_v", [P, C])
        bias_o = sb("bias_o", [P, C])
        work = sb("work", [P, 12800])

        def carver():
            at = [0]

            def carve(words, dt=F32):
                piece = work[:, at[0]:at[0] + words]
                at[0] += words
                assert at[0] <= 12800
                return piece if dt == F32 else piece.bitcast(dt)
            return carve

        class Semaphores:

            def __init__(self, name):
                self.name, self.held = name, []

            def __call__(self, n):
                self.held.append(nc.alloc_semaphore(f"{self.name}_{n}"))
                return self.held[-1]

            def __enter__(self):
                return self

            def __exit__(self, *_):
                nc.clear_and_free_semaphores(self.held)
                nc.all_engine_barrier(sem_only=True)

        def norm_stats(dve, i, mv_ready, rstd_ready):
            for t in range(TPB):
                dve.bn_stats(stats[:, t, :], x_sb[:, bass.ds(i * TPB + t, 1), :])
            dve.drain()
            for t in range(TPB):
                dve.bn_aggr(mv[:, t, :], stats[:, t, :])
            dve.drain()
            dve.tensor_scalar(var_eps[:, :], mv[:, :, 1], EPS, None, ALU.add).then_inc(mv_ready, 1)
            dve.wait_ge(rstd_ready, i + 1)

        def norm_rstd(pool, i, mv_ready, rstd_ready):
            pool.wait_ge(mv_ready, i + 1)
            pool.tensor_tensor(rstd[:, :], var_eps[:, :], powers[:, 0:TPB], ALU.pow).then_inc(rstd_ready, 1)

        def norm_apply(dve, i, xn_ready):
            for t in range(TPB):
                dve.tensor_scalar(xn[:, t, :], x_sb[:, bass.ds(i * TPB + t, 1), :].rearrange("p a c -> p (a c)"),
                                  mv[:, t, 0:1], rstd[:, t:t + 1],
                                  ALU.subtract, ALU.mult).then_inc(xn_ready, 1)

        def transpose_tokens(pe, i, xn_ready, xnT_psum):
            for t in range(TPB):
                pe.wait_ge(xn_ready, i * TPB + (t + 1))
                for k in range(KC):
                    last = pe.transpose(pb[:, k, t * P:(t + 1) * P], xn[:, t, k * P:(k + 1) * P], ident[:, :])
            last.then_inc(xnT_psum, 1)

        def prepare(sem, block_ctx):
            carve = carver()
            wq_f = carve(KC * C)
            colscale = carve(2 * H)
            usev = carve(2 * H)
            raw = carve(KC * 2 * C).rearrange("p (k a n) -> p k a n", k=KC, a=2)
            tmp = carve(2 * 64)
            loaded_x = sem("loaded_x")
            loaded_ffn = sem("loaded_ffn")
            loaded_cau = sem("loaded_cau")
            loaded_w = sem("loaded_w")
            loaded_masks = [sem(f"loaded_masks{n}") for n in range(8)]
            consts_zero = sem("consts_zero")
            consts_done = sem("consts_done")
            scales_ready = sem("scales_ready")
            block = block_ctx.enter_context(nc.Block())

            @block.sync
            def _(sp):
                sp.dma_start(wq_f, ffn_w).then_inc(loaded_ffn, 16)
                for n in range(8):
                    sp.dma_start(arena[:, n * 2048:(n + 1) * 2048],
                                 ffn_masks[:, n * 2048:(n + 1) * 2048]).then_inc(loaded_masks[n], 16)
                for b in range(NBATCH):
                    sp.dma_start(x_sb[:, b * TPB:(b + 1) * TPB, :],
                                 x_in[b * T:(b + 1) * T, :].rearrange("(t p) c -> p t c", p=P)).then_inc(loaded_x, 16)
                sp.wait_ge(loaded_x, 16 * NBATCH)
                sp.wait_ge(loaded_w, 16 * 14)

            @block.scalar
            def _(act):
                act.dma_start(colscale, cau_std).then_inc(loaded_cau, 16)
                act.dma_start(usev, cau_rec).then_inc(loaded_cau, 16)
                act.dma_start(raw[:, :, 0, :], cau_wq).then_inc(loaded_cau, 16)
                act.dma_start(raw[:, :, 1, :], cau_wk).then_inc(loaded_cau, 16)
                for dst, src in ((wcau[:, :, 2, :], cau_wv), (wcau_out[:, :, :], cau_wo), (wdec[:, :, :], dec_wqkv),
                                 (wdec_out[:, :, :], dec_wout), (router[:, :, :], ffn_router),
                                 (scale_b[:, :], ffn_scale), (wfull[:, :, 0, :], full_wq),
                                 (wfull[:, :, 1, :], full_wk), (wfull[:, :, 2, :], full_wv),
                                 (wfull_out[:, :, :], full_wo), (bias_qk[:, 0, :], full_bq),
                                 (bias_qk[:, 1, :], full_bk), (bias_v[:, :], full_bv), (bias_o[:, :], full_bo)):
                    act.dma_start(dst, src).then_inc(loaded_w, 16)

            @block.gpsimd
            def _(pool):
                pool.memset(powers[:, 0:32], -0.5)
                pool.memset(powers[:, 32:64], 0.5)
                pool.wait_ge(loaded_cau, 64)
                pool.tensor_scalar(colscale[:, H:2 * H], usev[:, 0:H], 1e-8, None, ALU.max)
                pool.tensor_scalar(colscale[:, 0:H], colscale[:, 0:H], 1e-8, None, ALU.max)
                pool.drain()
                pool.tensor_tensor(colscale, colscale, powers[:, 32:64], ALU.pow).then_inc(scales_ready, 1)
                pool.memset(ident[:, :], 0.0).then_inc(consts_zero, 1)
                pool.memset(ident_bf[:, :], 0.0).then_inc(consts_zero, 1)
                pool.memset(mask_ts[:, :], 0.0).then_inc(consts_zero, 1)
                pool.memset(mask_st[:, :], 0.0).then_inc(consts_zero, 1)
                pool.wait_ge(consts_zero, 4)
                for m in (ident, ident_bf):
                    pool.affine_select(out=m[:, :], in_=m[:, :], compare_op=ALU.not_equal, fill=1.0, base=0,
                                       pattern=[[-1, P]], channel_multiplier=1).then_inc(consts_done, 1)
                pool.affine_select(out=mask_ts[:, :], in_=mask_ts[:, :], compare_op=ALU.is_ge, fill=MASKED, base=0,
                                   pattern=[[-1, P]], channel_multiplier=1).then_inc(consts_done, 1)
                pool.affine_select(out=mask_st[:, :], in_=mask_st[:, :], compare_op=ALU.is_ge, fill=MASKED, base=0,
                                   pattern=[[1, P]], channel_multiplier=-1).then_inc(consts_done, 1)

            @block.vector
            def _(dve):
                dve.wait_ge(loaded_ffn, 16)
                dve.tensor_scalar(wq_f, wq_f, 2.0, -1.0, ALU.mult, ALU.max)
                dve.drain()
                dve.tensor_scalar(wq_f, wq_f, 1.0, 12582912.0, ALU.min, ALU.add)
                dve.drain()
                dve.tensor_scalar(wq_f, wq_f, 12582912.0, None, ALU.subtract)
                dve.drain()
                dve.wait_ge(loaded_cau, 64)
                s_std, s_rec = colscale[:, 0:H], colscale[:, H:2 * H]
                use, keep = usev[:, 0:H], usev[:, H:2 * H]
                dve.wait_ge(scales_ready, 1)
                dve.tensor_scalar(use, use, 0.1, None, ALU.is_gt)
                dve.drain()
                dve.tensor_scalar(keep, use, -1.0, 1.0, ALU.mult, ALU.add)
                dve.drain()
                t0 = tmp[:, 0:64].rearrange("p (d h) -> p d h", d=8)
                t1 = tmp[:, 64:128].rearrange("p (d h) -> p d h", d=8)
                for k in range(KC):
                    for c in range(KC):
                        def head_vec(v):
                            return v[:, c * 8:(c + 1) * 8].unsqueeze(1).broadcast_to([P, 8, 8])
                        q = raw[:, k, 0, c * P:(c + 1) * P].rearrange("p (d h) -> p d h", d=HD)
                        kk = raw[:, k, 1, c * P:(c + 1) * P].rearrange("p (d h) -> p d h", d=HD)
                        for n, (own, other) in enumerate(((q, kk), (kk, q))):
                            dst = wcau[:, k, n, c * P:(c + 1) * P].rearrange("p (d h) -> p d h", d=HD)
                            dve.tensor_tensor(dst[:, 0:8, :], own[:, 0:8, :], head_vec(s_std), ALU.mult)
                            dve.tensor_tensor(t0, own[:, 8:16, :], head_vec(keep), ALU.mult)
                            dve.tensor_tensor(t1, other[:, 8:16, :], head_vec(use), ALU.mult)
                            dve.drain()
                            dve.tensor_tensor(t0, t0, t1, ALU.add)
                            dve.drain()
                            dve.tensor_tensor(dst[:, 8:16, :], t0, head_vec(s_rec), ALU.mult)
                            dve.drain()
                for n in range(8):
                    dve.wait_ge(loaded_masks[n], 16)
                    piece = arena[:, n * 2048:(n + 1) * 2048].rearrange("p (e n) -> p e n", e=4)
                    dve.tensor_tensor(piece, piece, wq_f.unsqueeze(1).broadcast_to([P, 4, KC * C]), ALU.mult)

        def ffn_route(name):
            with Semaphores(name) as sem, ExitStack() as bc:
                carve = carver()
                logits = carve(NT * E)
                xn_ready, xn_free, xn_stored = sem("xn_ready"), sem("xn_free"), sem("xn_stored")
                xnT_psum, xnT_ready, logits_psum, logits_copied = (sem("xnT_psum"), sem("xnT_ready"),
                                                                   sem("logits_psum"), sem("logits_copied"))
                mv_ready, rstd_ready, xn_kept = sem("mv_ready"), sem("rstd_ready"), sem("xn_kept")
                block = bc.enter_context(nc.Block())

                @block.gpsimd
                def _(pool):
                    with pool.Fori(0, NBATCH) as i:
                        norm_rstd(pool, i, mv_ready, rstd_ready)

                @block.vector
                def _(dve):
                    with dve.Fori(0, NBATCH) as i:
                        norm_stats(dve, i, mv_ready, rstd_ready)
                        dve.wait_ge(xn_free, i + 1)
                        dve.wait_ge(xn_kept, i + 1)
                        norm_apply(dve, i, xn_ready)

                @block.tensor
                def _(pe):
                    pe.sem_inc(xn_free, 1)
                    with pe.Fori(0, NBATCH) as i:
                        transpose_tokens(pe, i, xn_ready, xnT_psum)
                        pe.wait_ge(logits_copied, i + 1)
                        pe.wait_ge(xnT_ready, i + 1)
                        for t in range(TPB):
                            for k in range(KC):
                                last = pe.matmul(pb[:, 2, t * E:(t + 1) * E], xnT[:, k, t * P:(t + 1) * P],
                                                 router[:, k, :], start=(k == 0), stop=(k == KC - 1))
                        last.then_inc(logits_psum, 1)

                @block.scalar
                def _(act):
                    act.sem_inc(logits_copied, 1)
                    with act.Fori(0, NBATCH) as i:
                        act.wait_ge(xnT_psum, i + 1)
                        act.activation(xnT[:, :, :].rearrange("p k t -> p (k t)"),
                                       pb[:, 0:2, :].rearrange("p k t -> p (k t)"), ACT.Copy).then_inc(xnT_ready, 1)
                        act.sem_inc(xn_free, 1)
                        act.wait_ge(logits_psum, i + 1)
                        act.activation(logits[:, bass.ds(i * (TPB * E), TPB * E)], pb[:, 2, 0:TPB * E],
                                       ACT.Copy).then_inc(logits_copied, 1)

                @block.sync
                def _(sp):
                    sp.sem_inc(xn_kept, 1)
                    with sp.Fori(0, NBATCH) as i:
                        sp.wait_ge(xn_ready, i * TPB + TPB)
                        sp.dma_start(xn_dram[bass.ds(i * T, T), :].rearrange("(t p) c -> p t c", p=P),
                                     xn[:, :, :]).then_inc(xn_stored, 16)
                        sp.wait_ge(xn_stored, 16 * i + 16)
                        sp.sem_inc(xn_kept, 1)

        def ffn_experts(name):
            with Semaphores(name) as sem, ExitStack() as bc:
                carve = carver()

                def te(v):
                    return v.rearrange("p (t e) -> p t e", t=NT)

                logits = carve(NT * E)
                shifted = carve(NT * E)
                ex = carve(NT * E)
                cand = carve(NT * E)
                totals = carve(NT * E)
                running = carve(NT * E)
                gate = carve(NT * E)
                onehot = carve(NT * E // 2, BF16)
                lo_hot = carve(NT * P // 2, BF16).rearrange("p (t n) -> p t n", t=NT)
                hi_hot = ex.bitcast(BF16).rearrange("p (t n) -> p t n", t=NT)
                hi_val = cand.bitcast(BF16).rearrange("p (t n) -> p t n", t=NT)
                hi_pid = totals.bitcast(BF16).rearrange("p (t n) -> p t n", t=NT)
                rev = carve(E)
                iota_p = carve(P)
                tile_no = carve(NT)
                part_no = carve(1)
                tri = carve(P // 2, BF16)
                ones = carve(P // 2, BF16)
                coef = carve(NT)
                best = carve(NT)
                pos = carve(NT)
                pos_i = carve(NT, I32)
                hi_i, lo_i = carve(NT, I32), carve(NT, I32)
                hi_f, lo_f = carve(NT), carve(NT)
                cnt, ntile, tend, base = carve(E), carve(E), carve(E), carve(E)
                cnt_i = carve(E, I32)
                ones_e = carve(E)
                owner_f = carve(NSLOT)
                owner_i = carve(NSLOT, I32)
                src_f, src_z = carve(NSLOT), carve(NSLOT)
                src_i = carve(NSLOT, I32)
                own_cmp = running[:, 0:1]
                cmp = shifted
                gat = sbuf_ring(bc, name, "gat", 4)
                yout = sbuf_ring(bc, name, "yout", 4)
                gatT = bc.enter_context(nc.sbuf_tensor(f"{name}_gatT", [P, 2, KC, P], F32))
                idx_a = bc.enter_context(nc.sbuf_tensor(f"{name}_idx", [P, 4], I32))
                del own_cmp
                consts, shifted_ready, ex_ready, onehot_ready, counts_ready = (
                    sem("consts"), sem("shifted_ready"), sem("ex_ready"), sem("onehot_ready"), sem("counts_ready"))
                hots_ready, slots_ready, owner_ready = sem("hots_ready"), sem("slots_ready"), sem("owner_ready")
                gathered, gat_free = [sem(f"gathered{n}") for n in range(4)], sem("gat_free")
                idx_ready = sem("idx_ready")
                gatT_psum, gatT_ready, y_psum, y_ready, y_stored = (sem("gatT_psum"), sem("gatT_ready"), sem("y_psum"),
                                                                    sem("y_ready"), [sem(f"y_stored{n}") for n in range(4)])
                back, back_free = [sem(f"back{n}") for n in range(4)], sem("back_free")
                y_all = sem("y_all")
                gather_turn = sem("gather_turn")
                block = bc.enter_context(nc.Block())

                @block.gpsimd
                def _(pool):
                    pool.iota(iota_p, [[1, P]], base=0, channel_multiplier=0, allow_small_or_imprecise_dtypes=True)
                    pool.iota(rev, [[-1, E]], base=E, channel_multiplier=0, allow_small_or_imprecise_dtypes=True)
                    pool.iota(tile_no, [[1, NT]], base=1, channel_multiplier=0, allow_small_or_imprecise_dtypes=True)
                    pool.iota(part_no, [[0, 1]], base=0, channel_multiplier=1, allow_small_or_imprecise_dtypes=True)
                    pool.memset(ones, 1.0)
                    pool.memset(ones_e, 1.0)
                    pool.memset(gate, 1.0)
                    pool.memset(gat[:, :, :], 0.0)
                    pool.drain()
                    pool.memset(gate.rearrange("p (e t) -> p e t", e=E)[:, :, 0:1], 0.0)
                    pool.affine_select(out=tri, in_=ones, compare_op=ALU.is_ge, fill=0.0, base=-1,
                                       pattern=[[1, P]], channel_multiplier=-1)
                    pool.drain().then_inc(consts, 1)
                    last_token = pool.to_reg(NT * P - 1)
                    last_slot = pool.to_reg(NSLOT * P - 1)
                    with pool.Fori(0, NSLOT // 4) as r:
                        pool.wait_ge(idx_ready, r + 1)
                        for n in range(4):
                            pool.wait_ge(gat_free, r * 4 + (n + 1))
                            pool.sem_inc(gather_turn, 1)
                            pool.indirect_dma_start(gat[:, n, :], None, xn_dram,
                                                    bass.IndirectOffsetOnAxis(ap=idx_a[:, n:n + 1], axis=0),
                                                    bounds_check=last_token, oob_is_err=False).then_inc(gathered[n], 16)
                    pool.wait_ge(y_all, 1)
                    with pool.Fori(0, NT // 4) as r:
                        pool.wait_ge(idx_ready, r + (NSLOT // 4 + 1))
                        for n in range(4):
                            pool.wait_ge(back_free, r * 4 + (n + 1))
                            pool.sem_inc(gather_turn, 1)
                            pool.indirect_dma_start(gat[:, n, :], None, slots_dram,
                                                    bass.IndirectOffsetOnAxis(ap=idx_a[:, n:n + 1], axis=0),
                                                    bounds_check=last_slot, oob_is_err=False).then_inc(back[n], 16)

                @block.vector
                def _(dve):
                    dve.wait_ge(consts, 1)
                    lg = te(logits)
                    dve.tensor_reduce(best, lg, AX_X, ALU.max)
                    dve.drain()
                    dve.tensor_tensor(te(shifted), lg, best.unsqueeze(2).broadcast_to([P, NT, E]),
                                      ALU.subtract).then_inc(shifted_ready, 1)
                    dve.drain()
                    rev_b = rev.unsqueeze(1).broadcast_to([P, NT, E])
                    dve.tensor_scalar(shifted_eq(cand), shifted, 0.0, None, ALU.is_ge)
                    dve.drain()
                    dve.tensor_tensor(te(cand), te(cand), rev_b, ALU.mult)
                    dve.drain()
                    dve.tensor_reduce(best, te(cand), AX_X, ALU.max)
                    dve.drain()
                    dve.tensor_tensor(te(onehot), rev_b, best.unsqueeze(2).broadcast_to([P, NT, E]),
                                      ALU.is_equal).then_inc(onehot_ready, 1)
                    dve.wait_ge(ex_ready, 1)
                    dve.tensor_reduce(pos, te(ex), AX_X, ALU.add)
                    dve.drain()
                    dve.reciprocal(coef, pos)
                    dve.drain()
                    dve.tensor_scalar(coef, coef, 0.5, None, ALU.mult)
                    dve.wait_ge(counts_ready, 1)
                    for half in range(2):
                        dve.tensor_copy(totals.rearrange("p (e t) -> p t e", e=E)[:, half * 16:(half + 1) * 16, :],
                                        pb[:, 2 + half, :].rearrange("p (t e) -> p t e", t=16))
                    dve.drain()
                    dve.tensor_tensor_scan(running, gate, totals, 0.0, ALU.mult, ALU.add)
                    dve.drain()
                    run_et = running.rearrange("p (e t) -> p e t", e=E)
                    dve.tensor_scalar(cnt_i, run_et[:, :, NT - 1], float(P - 1), None, ALU.add)
                    dve.drain()
                    dve.tensor_scalar(cnt_i, cnt_i, 7, None, ALU.arith_shift_right)
                    dve.drain()
                    dve.tensor_copy(ntile, cnt_i)
                    dve.drain()
                    dve.tensor_tensor_scan(tend, ones_e, ntile, 0.0, ALU.mult, ALU.add)
                    dve.drain()
                    dve.tensor_tensor(base, tend, ntile, ALU.subtract)
                    dve.drain()
                    dve.tensor_scalar(base, base, float(P), None, ALU.mult)
                    dve.tensor_tensor(running, running, totals, ALU.subtract)
                    dve.drain()
                    dve.tensor_tensor(run_et, run_et, base.unsqueeze(2).broadcast_to([P, E, NT]), ALU.add)
                    dve.drain()
                    run_te = running.rearrange("p (e t) -> p t e", e=E)
                    for half in range(2):
                        dve.tensor_tensor(te(cand)[:, half * 16:(half + 1) * 16, :],
                                          pb[:, half, :].rearrange("p (t e) -> p t e", t=16),
                                          run_te[:, half * 16:(half + 1) * 16, :], ALU.add)
                    dve.drain()
                    dve.tensor_tensor(cand, cand, onehot, ALU.mult)
                    dve.drain()
                    dve.tensor_reduce(pos, te(cand), AX_X, ALU.add)
                    dve.drain()
                    dve.tensor_copy(pos_i, pos)
                    dve.drain()
                    dve.tensor_scalar(hi_i, pos_i, 7, None, ALU.arith_shift_right)
                    dve.tensor_scalar(lo_i, pos_i, P - 1, None, ALU.bitwise_and)
                    dve.drain()
                    dve.tensor_copy(hi_f, hi_i)
                    dve.tensor_copy(lo_f, lo_i)
                    dve.drain()
                    dve.tensor_tensor(lo_hot, iota_p.unsqueeze(1).broadcast_to([P, NT, P]),
                                      lo_f.unsqueeze(2).broadcast_to([P, NT, P]), ALU.is_equal)
                    dve.tensor_tensor(hi_hot, iota_p[:, 0:NSLOT].unsqueeze(1).broadcast_to([P, NT, NSLOT]),
                                      hi_f.unsqueeze(2).broadcast_to([P, NT, NSLOT]), ALU.is_equal)
                    dve.drain()
                    dve.tensor_tensor(hi_val, hi_hot, tile_no.unsqueeze(2).broadcast_to([P, NT, NSLOT]), ALU.mult)
                    dve.tensor_scalar(hi_pid, hi_hot, part_no, None, ALU.mult)
                    dve.drain().then_inc(hots_ready, 1)
                    for half in range(2):
                        dve.tensor_tensor(te(cmp), iota_p[:, half * 32:(half + 1) * 32].unsqueeze(2).broadcast_to([P, 32, E]),
                                          tend.unsqueeze(1).broadcast_to([P, 32, E]), ALU.is_ge)
                        dve.drain()
                        dve.tensor_reduce(owner_f[:, half * 32:(half + 1) * 32], te(cmp), AX_X, ALU.add)
                        dve.drain()
                    dve.tensor_scalar(owner_f, owner_f, float(E - 1), float(KC * C), ALU.min, ALU.mult)
                    dve.drain()
                    dve.tensor_copy(owner_i, owner_f)
                    dve.drain().then_inc(owner_ready, 1)
                    dve.wait_ge(slots_ready, 1)
                    dve.tensor_scalar(src_f, pb[:, 4, 0:NSLOT], float(P), -float(P), ALU.mult, ALU.add)
                    dve.tensor_scalar(src_z, pb[:, 4, 0:NSLOT], 0.0, 8192.0, ALU.is_equal, ALU.mult)
                    dve.drain()
                    dve.tensor_tensor(src_f, pb[:, 4, NSLOT:2 * NSLOT], src_f, ALU.add)
                    dve.drain()
                    dve.tensor_tensor(src_f, src_f, src_z, ALU.add)
                    dve.drain()
                    dve.tensor_copy(src_i, src_f)
                    dve.drain()
                    def scale_round(r, first=False):
                        if not first:
                            dve.wait_ge(gat_free, r * 4 + 4)
                        dve.tensor_copy(idx_a[:, :], src_i[:, bass.ds(r * 4, 4)]).then_inc(idx_ready, 1)
                        for n in range(4):
                            dve.wait_ge(y_psum, r * 4 + (n + 1))
                            if not first:
                                dve.wait_ge(y_stored[n], r * 16)
                            dve.tensor_tensor(yout[:, n, :], pb[:, 6 + n % 2, 0:C], scale_b[:, :],
                                              ALU.mult).then_inc(y_ready, 1)

                    scale_round(0, first=True)
                    with dve.Fori(1, NSLOT // 4) as r:
                        scale_round(r)
                    with dve.Fori(0, NT // 4) as r:
                        dve.tensor_copy(idx_a[:, :], pos_i[:, bass.ds(r * 4, 4)]).then_inc(idx_ready, 1)
                        for n in range(4):
                            dve.wait_ge(back[n], 16 * r + 16)
                            dve.scalar_tensor_tensor(x_sb[:, bass.ds(r * 4 + n, 1), :].rearrange("p a c -> p (a c)"),
                                                     gat[:, n, :], coef[:, bass.ds(r * 4 + n, 1)],
                                                     x_sb[:, bass.ds(r * 4 + n, 1), :].rearrange("p a c -> p (a c)"),
                                                     ALU.mult, ALU.add).then_inc(back_free, 1)

                @block.scalar
                def _(act):
                    act.wait_ge(shifted_ready, 1)
                    act.activation(ex, shifted, ACT.Exp).then_inc(ex_ready, 1)
                    with act.Fori(0, NSLOT // 2) as r:
                        for n in range(2):
                            act.wait_ge(gatT_psum, r * 2 + (n + 1))
                            act.activation(gatT[:, n, :, :].rearrange("p k t -> p (k t)"), pb[:, 4 + n, 0:C],
                                           ACT.Copy).then_inc(gatT_ready, 1)

                @block.tensor
                def _(pe):
                    pe.sem_inc(gat_free, 4)
                    pe.wait_ge(onehot_ready, 1)
                    pe.wait_ge(consts, 1)
                    for half in range(2):
                        oh = onehot[:, half * 512:(half + 1) * 512]
                        pe.matmul(pb[:, half, :], tri, oh, start=True, stop=True)
                        last = pe.matmul(pb[:, 2 + half, :], ones, oh, start=True, stop=True)
                    last.then_inc(counts_ready, 1)
                    pe.wait_ge(hots_ready, 1)
                    for t in range(NT):
                        pe.matmul(pb[:, 4, 0:NSLOT], lo_hot[:, t, :], hi_val[:, t, :], start=(t == 0), stop=(t == NT - 1))
                    for t in range(NT):
                        last = pe.matmul(pb[:, 4, NSLOT:2 * NSLOT], lo_hot[:, t, :], hi_pid[:, t, :],
                                         start=(t == 0), stop=(t == NT - 1))
                    last.then_inc(slots_ready, 1)
                    pe.wait_ge(owner_ready, 1)
                    with pe.Fori(0, NSLOT // 4) as r:
                        for n in range(4):
                            w0 = pe.value_load(owner_i[0:1, bass.ds(r * 4 + n, 1)], min_val=0, max_val=(E - 1) * KC * C)
                            pe.wait_ge(gathered[n], 16 * r + 16)
                            for k in range(KC):
                                last = pe.transpose(pb[:, 4 + n % 2, k * P:(k + 1) * P], gat[:, n, k * P:(k + 1) * P],
                                                    ident[:, :])
                            last.then_inc(gatT_psum, 1)
                            pe.wait_ge(gatT_ready, r * 4 + (n + 1))
                            pe.sem_inc(gat_free, 1)
                            pe.wait_ge(y_ready, r * 4 + (n + 1))
                            for k in range(KC):
                                last = pe.matmul(pb[:, 6 + n % 2, 0:C], gatT[:, n % 2, k, :],
                                                 arena[:, bass.ds(w0 + k * C, C)],
                                                 start=(k == 0), stop=(k == KC - 1))
                            last.then_inc(y_psum, 1)

                @block.sync
                def _(sp):
                    sp.sem_inc(back_free, 4)
                    sp.sem_inc(y_ready, 2)
                    with sp.Fori(0, NSLOT // 4) as r:
                        for n in range(4):
                            sp.wait_ge(y_ready, r * 4 + (n + 3))
                            sp.dma_start(slots_dram[bass.ds((r * 4 + n) * P, P), :], yout[:, n, :])\
                              .then_inc(y_stored[n], 16)
                    for n in range(4):
                        sp.wait_ge(y_stored[n], 16 * (NSLOT // 4))
                    sp.sem_inc(y_all, 1)

        def decay_attention(name):
            with Semaphores(name) as sem, ExitStack() as bc:
                carve = carver()
                F = KC * T

                def kt(v):
                    return v.rearrange("p (k t) -> p k t", k=KC)

                decay = carve(F)
                block_ones = carve(P)
                rate = carve(KC)
                relu_q, exp_q, relu_k, exp_k = carve(F), carve(F), carve(F), carve(F)
                kv, run_kv, run_k, mixed = carve(F), carve(F), carve(F), carve(F)
                param_loaded, rate_exp, rate_ready, consts = (sem("param_loaded"), sem("rate_exp"), sem("rate_ready"),
                                                              sem("consts"))
                mv_ready, rstd_ready, xn_ready, xn_free = (sem("mv_ready"), sem("rstd_ready"), sem("xn_ready"),
                                                           sem("xn_free"))
                xnT_psum, xnT_ready, q_psum, k_psum, v_psum = (sem("xnT_psum"), sem("xnT_ready"), sem("q_psum"),
                                                               sem("k_psum"), sem("v_psum"))
                q_read, k_read, v_read, phi_ready = sem("q_read"), sem("k_read"), sem("v_read"), sem("phi_ready")
                dots_ready, den_psum, mixed_ready, o_psum, x_added, run_ready, qkv_ready = (
                    sem("dots_ready"), sem("den_psum"), sem("mixed_ready"), sem("o_psum"), sem("x_added"),
                    sem("run_ready"), sem("qkv_ready"))
                block = bc.enter_context(nc.Block())

                @block.sync
                def _(sp):
                    sp.dma_start(rate, dec_param).then_inc(param_loaded, 16)

                @block.gpsimd
                def _(pool):
                    pool.memset(block_ones, 1.0)
                    pool.drain()
                    b3 = block_ones.rearrange("p (h d) -> p h d", d=HD)
                    pool.affine_select(out=b3, in_=b3, compare_op=ALU.is_ge, fill=0.0, base=0,
                                       pattern=[[-HD, P // HD], [0, HD]], channel_multiplier=1)
                    pool.drain()
                    pool.affine_select(out=b3, in_=b3, compare_op=ALU.is_ge, fill=0.0, base=HD - 1,
                                       pattern=[[HD, P // HD], [0, HD]], channel_multiplier=-1)
                    pool.drain().then_inc(consts, 1)
                    with pool.Fori(0, NBATCH) as i:
                        norm_rstd(pool, i, mv_ready, rstd_ready)
                        pool.wait_ge(run_ready, i + 1)
                        pool.tensor_tensor(relu_q, relu_q, run_kv, ALU.mult).then_inc(qkv_ready, 1)

                @block.scalar
                def _(act):
                    act.wait_ge(param_loaded, 16)
                    act.activation(rate, rate, ACT.Exp, scale=-1.0).then_inc(rate_exp, 1)
                    act.sem_inc(mixed_ready, 1)
                    with act.Fori(0, NBATCH) as i:
                        act.wait_ge(xnT_psum, i + 1)
                        act.activation(xnT[:, :, :].rearrange("p k t -> p (k t)"),
                                       pb[:, 0:2, :].rearrange("p k t -> p (k t)"), ACT.Copy).then_inc(xnT_ready, 1)
                        act.sem_inc(xn_free, 1)
                        act.wait_ge(mixed_ready, i + 1)
                        for bank, got, rel, ex, read in ((2, q_psum, relu_q, exp_q, q_read),
                                                         (4, k_psum, relu_k, exp_k, k_read)):
                            src = pb[:, bank:bank + 2, :].rearrange("p k t -> p (k t)")
                            act.wait_ge(got, i + 1)
                            act.activation(rel, src, ACT.Relu)
                            act.activation(ex, src, ACT.Exp).then_inc(read, 1)

                @block.tensor
                def _(pe):
                    pe.sem_inc(xn_free, 1)
                    pe.sem_inc(x_added, 1)
                    pe.sem_inc(v_read, 1)
                    pe.wait_ge(consts, 1)
                    with pe.Fori(0, NBATCH) as i:
                        pe.wait_ge(x_added, i + 1)
                        transpose_tokens(pe, i, xn_ready, xnT_psum)
                        pe.wait_ge(xnT_ready, i + 1)
                        pe.wait_ge(v_read, i + 1)
                        for bank, col, done in ((2, 0, q_psum), (4, C, k_psum), (6, 2 * C, v_psum)):
                            for c in range(KC):
                                for k in range(KC):
                                    last = pe.matmul(pb[:, bank + c, :], wdec[:, k, col + c * P:col + (c + 1) * P],
                                                     xnT[:, k, :], start=(k == 0), stop=(k == KC - 1))
                            last.then_inc(done, 1)
                        pe.wait_ge(q_read, i + 1)
                        pe.wait_ge(dots_ready, i + 1)
                        for c in range(KC):
                            last = pe.matmul(pb[:, 2 + c, :], block_ones, kt(run_k)[:, c, :], start=True, stop=True)
                        last.then_inc(den_psum, 1)
                        pe.wait_ge(mixed_ready, i + 2)
                        for t in range(TPB):
                            for c in range(KC):
                                last = pe.matmul(pb[:, t // 2, (t % 2) * C:(t % 2 + 1) * C],
                                                 kt(mixed)[:, c, t * P:(t + 1) * P], wdec_out[:, c, :],
                                                 start=(c == 0), stop=(c == KC - 1))
                        last.then_inc(o_psum, 1)

                @block.vector
                def _(dve):
                    dve.wait_ge(rate_exp, 1)
                    dve.tensor_scalar(rate, rate, 1.0, None, ALU.add)
                    dve.drain()
                    dve.reciprocal(rate, rate)
                    dve.memset(decay, 1.0)
                    dve.drain()
                    for c in range(KC):
                        dve.tensor_scalar(kt(decay)[:, c, :], kt(decay)[:, c, :], rate[:, c:c + 1], None, ALU.mult)
                    dve.drain()
                    dve.memset(kt(decay)[:, :, 0:1], 0.0)
                    dve.drain()
                    with dve.Fori(0, NBATCH) as i:
                        norm_stats(dve, i, mv_ready, rstd_ready)
                        dve.wait_ge(xn_free, i + 1)
                        norm_apply(dve, i, xn_ready)
                        dve.wait_ge(q_read, i + 1)
                        dve.scalar_tensor_tensor(relu_q, exp_q, 1.0, relu_q, ALU.min, ALU.add)
                        dve.wait_ge(k_read, i + 1)
                        dve.scalar_tensor_tensor(relu_k, exp_k, 1.0, relu_k, ALU.min, ALU.add)
                        dve.drain()
                        dve.wait_ge(v_psum, i + 1)
                        dve.tensor_tensor(kv, pb[:, 6:8, :].rearrange("p k t -> p (k t)"), relu_k,
                                          ALU.mult).then_inc(v_read, 1)
                        dve.tensor_tensor_scan(run_k, decay, relu_k, 0.0, ALU.mult, ALU.add)
                        dve.drain()
                        dve.tensor_tensor(run_k, run_k, relu_q, ALU.mult).then_inc(dots_ready, 1)
                        dve.tensor_tensor_scan(run_kv, decay, kv, 0.0, ALU.mult, ALU.add)
                        dve.drain().then_inc(run_ready, 1)
                        dve.wait_ge(den_psum, i + 1)
                        dve.wait_ge(qkv_ready, i + 1)
                        dve.tensor_scalar(kv, pb[:, 2:4, :].rearrange("p k t -> p (k t)"), 1e-6, None, ALU.max)
                        dve.drain()
                        dve.reciprocal(kv, kv)
                        dve.drain()
                        dve.tensor_tensor(mixed, relu_q, kv, ALU.mult).then_inc(mixed_ready, 1)
                        dve.wait_ge(o_psum, i + 1)
                        xi = x_sb[:, bass.ds(i * TPB, TPB), :].rearrange("p t c -> p (t c)")
                        dve.tensor_tensor(xi, pb[:, 0:2, :].rearrange("p k t -> p (k t)"), xi,
                                          ALU.add).then_inc(x_added, 1)
                        dve.drain()

        def score_columns(causal, half):
            if not causal:
                return [(s * 256, half * 256, 256) for s in range(TPB)]
            if half == 0:
                return [(0, 0, 256), (256, 128, 128)]
            return [(0, 256, 256), (256, 256, 256), (512, 256, 256), (768, 384, 128)]

        def attention(name, causal):
            w, w_out = (wcau, wcau_out) if causal else (wfull, wfull_out)
            with Semaphores(name) as sem, ExitStack() as bc:
                carve = carver()
                NQK = 2 * KC
                parts = [carve(NQK * T // 2, BF16).rearrange("p (n t) -> p n t", n=NQK) for _ in range(3)]
                rest = carve(NQK * T).rearrange("p (n t) -> p n t", n=NQK)
                v_aug = carve(TPB * H * SLOT).rearrange("p (s h d) -> p s h d", s=TPB, h=H)
                o_t = carve(NG * T).rearrange("p (g t) -> p g t", g=NG)
                turned = carve(T)
                den = carve(T // SLOT)
                row_max = carve(NG * 16).rearrange("p (g n) -> p g n", g=NG)
                shift_hi = carve(NG * P // 2, BF16).rearrange("p (g n) -> p g n", g=NG)
                shift_lo = carve(NG * P // 2, BF16).rearrange("p (g n) -> p g n", g=NG)

                mv_ready, rstd_ready, xn_ready, xn_free = (sem("mv_ready"), sem("rstd_ready"), sem("xn_ready"),
                                                           sem("xn_free"))
                xnT_psum, xnT_ready, proj_psum, v_psum = sem("xnT_psum"), sem("xnT_ready"), sem("proj_psum"), sem("v_psum")
                part0, rest_ready, part1, part2 = sem("part0"), sem("rest_ready"), sem("part1"), sem("part2")
                stacked = [sem(f"stacked{c}") for c in range(KC)]
                v_ready, aug_set = sem("v_ready"), sem("aug_set")
                rows_psum, rows_read, maxT_psum, shift_ready = (sem("rows_psum"), sem("rows_read"), sem("maxT_psum"),
                                                                sem("shift_ready"))
                shifted = [sem(f"shifted{g}") for g in range(NG)]
                unit_psum, unit_exp, pv_psum, pv_read = sem("unit_psum"), sem("unit_exp"), sem("pv_psum"), sem("pv_read")
                o_ready = sem("o_ready")
                o_psum, x_added, x_biased, scores_done = sem("o_psum"), sem("x_added"), sem("x_biased"), sem("scores_done")
                block = bc.enter_context(nc.Block())

                NR = H * TPB
                NU = H * 2

                @block.gpsimd
                def _(pool):
                    pool.memset(kst[96:98, :], 1.0)
                    pool.drain()
                    pool.memset(v_aug[:, :, :, HD:SLOT], 1.0)
                    pool.drain().then_inc(aug_set, 1)
                    with pool.Fori(0, NBATCH) as i:
                        norm_rstd(pool, i, mv_ready, rstd_ready)
                        for n in range(NQK):
                            pool.wait_ge(part1, NQK * i + (n + 1))
                            pool.tensor_tensor(parts[2][:, n, :], rest[:, n, :], parts[1][:, n, :],
                                               ALU.subtract).then_inc(part2, 1)
                        if not causal:
                            pool.wait_ge(xn_ready, TPB * i + TPB)
                            xi = x_sb[:, bass.ds(i * TPB, TPB), :]
                            pool.tensor_tensor(xi, xi, bias_o[:, :].unsqueeze(1).broadcast_to([P, TPB, C]),
                                               ALU.add).then_inc(x_biased, 1)

                @block.sync
                def _(sp):
                    with sp.Fori(0, NBATCH) as i:
                        batch_no = sp.snap(i + 1)
                        first_part = sp.snap(NQK * i + 1)
                        sp.wait_ge(scores_done, batch_no)
                        for n in range(NQK):
                            c, is_k = n // 2, n % 2
                            stack, order = (kst, PARTS_K) if is_k else (qst, PARTS_Q)
                            for part, done in ((0, part0), (1, part1), (2, part2)):
                                sp.wait_ge(done, first_part if n == 0 else NQK * i + (n + 1))
                                for slot, p in enumerate(order):
                                    if p == part:
                                        sp.dma_start(stack[slot * HD:(slot + 1) * HD, c * 4096:(c + 1) * 4096],
                                                     parts[part][:, n, :]).then_inc(stacked[c], 16)
                        for g in range(NG):
                            sp.wait_ge(shift_ready, NG * i + (g + 1))
                            for row, src in ((96, shift_hi), (97, shift_lo)):
                                sp.dma_start(qst[row:row + 1, g * 2048:(g + 1) * 2048],
                                             src[0:16, g, :]).then_inc(shifted[g], 16)

                @block.scalar
                def _(act):
                    with act.Fori(0, NBATCH) as i:
                        act.wait_ge(xnT_psum, i + 1)
                        act.activation(xnT[:, :, :].rearrange("p k t -> p (k t)"),
                                       pb[:, 0:2, :].rearrange("p k t -> p (k t)"), ACT.Copy).then_inc(xnT_ready, 1)
                        act.sem_inc(xn_free, 1)
                        for n in range(NQK):
                            act.wait_ge(proj_psum, NQK * i + (n + 1))
                            if causal:
                                act.activation(parts[0][:, n, :], pb[:, 2 + n, :], ACT.Copy).then_inc(part0, 1)
                            else:
                                act.activation(parts[0][:, n, :], pb[:, 2 + n, :], ACT.Identity,
                                               bias=bias_qk[:, n % 2, n // 2:n // 2 + 1]).then_inc(part0, 1)
                            if n:
                                act.wait_ge(rest_ready, NQK * i + n)
                                act.activation(parts[1][:, n - 1, :], rest[:, n - 1, :], ACT.Copy).then_inc(part1, 1)
                        act.wait_ge(rest_ready, NQK * i + NQK)
                        act.activation(parts[1][:, NQK - 1, :], rest[:, NQK - 1, :], ACT.Copy).then_inc(part1, 1)
                        for u in range(NU):
                            half, hh = (u // G) % 2, u % G
                            cols = score_columns(causal, half)
                            width = cols[-1][0] + cols[-1][2]
                            act.wait_ge(unit_psum, NU * i + (u + 1))
                            bank = 2 * (u % 2)
                            act.activation(probs[:, (u // G) % 2, hh, 0:width],
                                           pb[:, bank:bank + 2, :].rearrange("p k t -> p (k t)")[:, 0:width],
                                           ACT.Exp, scale=HD ** -0.5).then_inc(unit_exp, 1)

                @block.tensor
                def _(pe):
                    pe.sem_inc(xn_free, 1)
                    pe.sem_inc(x_added, 1)
                    pe.sem_inc(scores_done, 1)
                    pe.wait_ge(aug_set, 1)

                    def row(i, r):
                        h, t = r // TPB, r % TPB
                        if r % TPB == 0:
                            pe.wait_ge(stacked[h // 8], 192 * i + 192)
                        if r >= 2:
                            pe.wait_ge(rows_read, NR * i + (r - 1))
                        width = P * (t + 1) if causal else T
                        bank = 4 + r % 2
                        last = pe.matmul(pb[:, bank, 0:width], qst_h[0:96, h, t * P:(t + 1) * P],
                                         kst_h[0:96, h, 0:width], start=True, stop=not causal)
                        if causal:
                            last = pe.matmul(pb[:, bank, t * P:(t + 1) * P], ident_bf[:, :], mask_ts[:, :],
                                             start=False, stop=True)
                        last.then_inc(rows_psum, 1)

                    def transpose_max(i, g):
                        pe.wait_ge(rows_read, NR * i + 16 * (g + 1))
                        pe.transpose(pb[0:16, 7, 0:P], row_max[:, g, :], ident[:, :]).then_inc(maxT_psum, 1)

                    def unit(i, u):
                        g, half, hh = u // 8, (u // G) % 2, u % G
                        h = g * G + hh
                        if u % 8 == 0:
                            pe.wait_ge(shifted[g], 32 * i + 32)
                        if u >= 2:
                            pe.wait_ge(unit_exp, NU * i + (u - 1))
                        cols = score_columns(causal, half)
                        flat = pb[:, 2 * (u % 2):2 * (u % 2) + 2, :].rearrange("p k t -> p (k t)")
                        for s, (off, q0, n) in enumerate(cols):
                            diagonal = causal and q0 <= s * P
                            last = pe.matmul(flat[:, off:off + n], kst_h[0:ROWS, h, s * P:(s + 1) * P],
                                             qst_h[0:ROWS, h, q0:q0 + n], start=True, stop=not diagonal)
                            if diagonal:
                                at = off + s * P - q0
                                last = pe.matmul(flat[:, at:at + P], ident_bf[:, :], mask_st[:, :],
                                                 start=False, stop=True)
                        last.then_inc(unit_psum, 1)

                    def values(i, n):
                        g, half = n // 2, n % 2
                        pe.wait_ge(unit_exp, NU * i + G * (n + 1))
                        if half == 0 and g > 0:
                            pe.wait_ge(pv_read, NG * i + g)
                        cols = score_columns(causal, half)
                        for s, (off, q0, m) in enumerate(cols):
                            for hh in range(G):
                                last = pe.matmul(pb[hh * SLOT:(hh + 1) * SLOT, 6, q0:q0 + m],
                                                 v_aug[:, s, g * G + hh, :], probs[:, n % 2, hh, off:off + m],
                                                 start=(s == 0), stop=(s == len(cols) - 1))
                        if half == 1:
                            last.then_inc(pv_psum, 1)

                    with pe.Fori(0, NBATCH) as i:
                        pe.wait_ge(x_added, i + 1)
                        transpose_tokens(pe, i, xn_ready, xnT_psum)
                        pe.wait_ge(xnT_ready, i + 1)
                        for n in range(NQK):
                            c, is_k = n // 2, n % 2
                            for k in range(KC):
                                last = pe.matmul(pb[:, 2 + n, :], w[:, k, is_k, c * P:(c + 1) * P], xnT[:, k, :],
                                                 start=(k == 0), stop=(k == KC - 1))
                            last.then_inc(proj_psum, 1)
                        for t in range(TPB):
                            for k in range(KC):
                                last = pe.matmul(pb[:, 6 + t // 2, (t % 2) * C:(t % 2 + 1) * C],
                                                 xnT[:, k, t * P:(t + 1) * P], w[:, k, 2, :],
                                                 start=(k == 0), stop=(k == KC - 1))
                        last.then_inc(v_psum, 1)
                        pe.wait_ge(rest_ready, NQK * i + NQK)
                        pe.wait_ge(v_ready, i + 1)
                        LEAD = 6
                        emitted = 0
                        done_groups = 0
                        for u in range(NU):
                            target = min(NR, 16 + LEAD + 2 * u)
                            while emitted < target:
                                row(i, emitted)
                                emitted += 1
                                if emitted >= 16 * (done_groups + 1) + 2:
                                    transpose_max(i, done_groups)
                                    done_groups += 1
                            if emitted == NR and done_groups < NG:
                                transpose_max(i, done_groups)
                                done_groups += 1
                            unit(i, u)
                            if u >= 5 and u % 4 == 1:
                                values(i, (u - 5) // 4)
                        pe.sem_inc(scores_done, 1)
                        values(i, 2 * NG - 1)
                        for t in range(TPB):
                            if t == 0:
                                pe.wait_ge(o_ready, NG * i + NG)
                            for g in range(NG):
                                last = pe.matmul(pb[:, t // 2, (t % 2) * C:(t % 2 + 1) * C],
                                                 o_t[:, g, t * P:(t + 1) * P], w_out[:, g, :],
                                                 start=(g == 0), stop=(g == NG - 1))
                        last.then_inc(o_psum, 1)

                @block.vector
                def _(dve):
                    def row_maxima(i, r):
                        t = r % TPB
                        width = P * (t + 1) if causal else T
                        dve.wait_ge(rows_psum, NR * i + (r + 1))
                        dve.tensor_reduce(row_max[:, r // 16, r % 16:r % 16 + 1], pb[:, 4 + r % 2, 0:width],
                                          AX_X, ALU.max).then_inc(rows_read, 1)

                    def shift(i, g):
                        dve.wait_ge(maxT_psum, NG * i + (g + 1))
                        dve.tensor_scalar(shift_hi[0:16, g, :], pb[0:16, 7, 0:P], -1.0, None, ALU.mult)
                        dve.drain()
                        dve.scalar_tensor_tensor(shift_lo[0:16, g, :], pb[0:16, 7, 0:P], -1.0, shift_hi[0:16, g, :],
                                                 ALU.mult, ALU.subtract).then_inc(shift_ready, 1)

                    def divide(i, g):
                        dve.drain()
                        dve.wait_ge(pv_psum, NG * i + (g + 1))
                        dve.transpose(turned, pb[:, 6, :]).then_inc(pv_read, 1)
                        dve.drain()
                        t3 = turned.rearrange("p (b r) -> p b r", r=SLOT)
                        dve.reciprocal(den, t3[:, :, HD])
                        dve.drain()
                        dve.tensor_tensor(t3[:, :, 0:HD], t3[:, :, 0:HD],
                                          den.unsqueeze(2).broadcast_to([P, T // SLOT, HD]), ALU.mult)
                        dve.drain()
                        dve.transpose(o_t[:, g, :], turned).then_inc(o_ready, 1)

                    dve.wait_ge(aug_set, 1)
                    with dve.Fori(0, NBATCH) as i:
                        norm_stats(dve, i, mv_ready, rstd_ready)
                        dve.wait_ge(xn_free, i + 1)
                        norm_apply(dve, i, xn_ready)
                        for n in range(NQK):
                            dve.wait_ge(part0, NQK * i + (n + 1))
                            if causal:
                                dve.tensor_tensor(rest[:, n, :], pb[:, 2 + n, :], parts[0][:, n, :],
                                                  ALU.subtract).then_inc(rest_ready, 1)
                            else:
                                dve.scalar_tensor_tensor(rest[:, n, :], pb[:, 2 + n, :],
                                                         bias_qk[:, n % 2, n // 2:n // 2 + 1], parts[0][:, n, :],
                                                         ALU.add, ALU.subtract).then_inc(rest_ready, 1)
                        dve.wait_ge(v_psum, i + 1)
                        for t in range(TPB):
                            src = pb[:, 6 + t // 2, (t % 2) * C:(t % 2 + 1) * C].rearrange("p (h d) -> p h d", h=H)
                            if causal:
                                last = dve.tensor_copy(v_aug[:, t, :, 0:HD], src)
                            else:
                                last = dve.tensor_tensor(v_aug[:, t, :, 0:HD], src,
                                                         bias_v[:, :].rearrange("p (h d) -> p h d", h=H), ALU.add)
                        last.then_inc(v_ready, 1)
                        g_done = 0
                        for r in range(NR):
                            row_maxima(i, r)
                            if r + 1 >= 16 * (g_done + 1) + 4:
                                shift(i, g_done)
                                g_done += 1
                            if r % 16 == 11 and r > 32:
                                divide(i, r // 16 - 2)
                        shift(i, NG - 1)
                        for g in range(NG - 2, NG):
                            divide(i, g)
                        dve.wait_ge(o_psum, i + 1)
                        if not causal:
                            dve.wait_ge(x_biased, i + 1)
                        xi = x_sb[:, bass.ds(i * TPB, TPB), :].rearrange("p t c -> p (t c)")
                        dve.scalar_tensor_tensor(xi, pb[:, 0:2, :].rearrange("p k t -> p (k t)"),
                                                 0.5 if causal else 1.0, xi, ALU.mult, ALU.add).then_inc(x_added, 1)
                        dve.drain()

        def sbuf_ring(bc, name, what, n):
            return bc.enter_context(nc.sbuf_tensor(f"{name}_{what}", [P, n, C], F32))

        def shifted_eq(v):
            return v

        def store_out():
            with ExitStack() as bc:
                stored = bc.enter_context(nc.semaphore("stored"))
                block = bc.enter_context(nc.Block())

                @block.sync
                def _(sp):
                    for b in range(NBATCH):
                        sp.dma_start(out[b * T:(b + 1) * T, :].rearrange("(t p) c -> p t c", p=P),
                                     x_sb[:, b * TPB:(b + 1) * TPB, :]).then_inc(stored, 16)
                    sp.wait_ge(stored, 16 * NBATCH)

        with Semaphores("prep") as sem, ExitStack() as bc:
            prepare(sem, bc)
        for n, layer in enumerate(layers):
            if layer == "ffn":
                ffn_route(f"r{n}")
                ffn_experts(f"e{n}")
            elif layer == "decay":
                decay_attention(f"d{n}")
            elif layer == "causal":
                attention(f"a{n}", True)
            elif layer == "full":
                attention(f"a{n}", False)
        store_out()


LAYERS = ("ffn", "decay", "ffn", "causal", "full", "causal")


def _laid_out(inp):
    import numpy as np
    H, HD, KC, P, E, C = 16, 16, 2, 128, 32, 256
    a = {k: np.asarray(v) for k, v in inp.items()}

    def chunked(w):
        return w.reshape(KC, P, -1).transpose(1, 0, 2)

    def head_minor(w):
        return w.reshape(C, 2, 8, HD).transpose(0, 1, 3, 2).reshape(C, C)

    def padded_rows(w):
        z = np.zeros((4, 4, 32, C), w.dtype)
        z[:, :, :HD] = w.reshape(4, 4, HD, C)
        return z.reshape(4, P, C).transpose(1, 0, 2)

    def every_partition(v):
        return np.broadcast_to(v.reshape(1, -1), (P, v.size))

    wa = a["L1_ffn_Wa"]
    q_std, k_std, v, q_low, k_low = np.split(wa, [128, 256, 512, 640], axis=1)

    def with_tail(std, low):
        return np.concatenate([std.reshape(C, H, 8), low.reshape(C, H, 8)], axis=2).reshape(C, C)

    def column_bias(b):
        return b.reshape(2, 8, HD).transpose(2, 1, 0).reshape(P, 2)

    laid = {
        "x_in": a["L0_attn_x"].reshape(-1, C),
        "dec_wqkv": chunked(a["L0_attn_w_qkv"]),
        "dec_wout": chunked(a["L0_attn_w_out"]),
        "dec_param": np.repeat(a["L0_attn_decay_param"], HD).reshape(KC, P).T,
        "ffn_w": chunked(a["L0_ffn_weight"].T).reshape(P, KC * C),
        "ffn_scale": every_partition(a["L0_ffn_scale"]),
        "ffn_masks": a["L0_ffn_expert_masks"].transpose(2, 0, 1).reshape(KC, P, E, C).transpose(1, 2, 0, 3).reshape(P, -1),
        "ffn_router": chunked(a["L0_ffn_router_w"].T),
        "full_wq": chunked(head_minor(a["L1_attn_wq"].T)),
        "full_wk": chunked(head_minor(a["L1_attn_wk"].T)),
        "full_wv": chunked(a["L1_attn_wv"].T),
        "full_wo": padded_rows(a["L1_attn_wo"].T),
        "full_bq": column_bias(a["L1_attn_bq"]),
        "full_bk": column_bias(a["L1_attn_bk"]),
        "full_bv": every_partition(a["L1_attn_bv"]),
        "full_bo": every_partition(a["L1_attn_bo"]),
        "cau_wq": chunked(head_minor(with_tail(q_std, q_low))),
        "cau_wk": chunked(head_minor(with_tail(k_std, k_low))),
        "cau_wv": chunked(v),
        "cau_wo": padded_rows(a["L1_ffn_Wp"]),
        "cau_std": every_partition(np.concatenate([a["L1_ffn_w_std"], a["L1_ffn_w_std"]])),
        "cau_rec": every_partition(np.concatenate([a["L1_ffn_w_rec"], a["L1_ffn_w_rec"]])),
    }
    return {k: np.ascontiguousarray(v) for k, v in laid.items()}


def kernel(**inputs):
    import numpy as _np
    import concourse.bacc as _bacc
    from concourse import mybir as _mybir
    from concourse.bass_utils import run_bass_kernel_spmd as _run

    nc = _bacc.Bacc("TRN2", target_bir_lowering=False, num_devices=1)
    arrays, args = {}, []
    for name, a in _laid_out(inputs).items():
        arrays[f"in_{name}"] = a
        args.append(nc.dram_tensor(f"in_{name}", a.shape, _mybir.dt.from_np(a.dtype), kind="ExternalInput").ap())
    out = nc.dram_tensor("out_x", (8 * 512, 256), _mybir.dt.from_np(_np.dtype("float32")), kind="ExternalOutput").ap()
    macaron_kernel(nc, *args, out, LAYERS)
    r = _run(nc, [arrays], core_ids=[0])
    return r.results[0]["out_x"].reshape(8, 512, 256)
```

```python
from contextlib import ExitStack

import concourse.bass as bass
from concourse import mybir

F32 = mybir.dt.float32
BF16 = mybir.dt.bfloat16
I32 = mybir.dt.int32
ALU = mybir.AluOpType
ACT = mybir.ActivationFunctionType
AX_X = mybir.AxisListType.X

P = 128
NBATCH, T, C = 8, 512, 256
TPB = T // P
NT = NBATCH * TPB
KC = C // P
H, HD = 16, 16
E = 32
NSLOT = 64
EPS = 1e-5
G = 4
NG = H // G
SLOT = 32
MASKED = -1.0e30
ROWS = 98
PARTS_Q = (0, 1, 2, 0, 1, 0)
PARTS_K = (0, 0, 0, 1, 1, 2)


def macaron_kernel(nc, x_in, dec_wqkv, dec_wout, dec_param, ffn_w, ffn_scale, ffn_masks, ffn_router,
                   full_wq, full_wk, full_wv, full_wo, full_bq, full_bk, full_bv, full_bo,
                   cau_wq, cau_wk, cau_wv, cau_wo, cau_std, cau_rec, out, layers):
    ctx = ExitStack()
    with ctx:
        def sb(name, shape, dt=F32):
            return ctx.enter_context(nc.sbuf_tensor(name, shape, dt))

        pb = ctx.enter_context(nc.psum_tensor("pb", [P, 8, 512], F32))

        xn_dram = nc.dram_tensor("xn_dram", [NT * P, C], F32).ap()
        slots_dram = nc.dram_tensor("slots_dram", [NSLOT * P, C], F32).ap()

        x_sb = sb("x_sb", [P, NT, C])
        xn = sb("xn", [P, TPB, C])
        xnT = sb("xnT", [P, KC, T])
        stats = sb("stats", [P, TPB, 6])
        mv = sb("mv", [P, TPB, 2])
        rstd = sb("rstd", [P, TPB])
        var_eps = sb("var_eps", [P, TPB])
        powers = sb("powers", [P, 64])
        ident = sb("ident", [P, P])
        ident_bf = sb("ident_bf", [P, P], BF16)
        mask_ts = sb("mask_ts", [P, P], BF16)
        mask_st = sb("mask_st", [P, P], BF16)
        arena = sb("arena", [P, E * KC * C])
        w_exp = arena[:, :].rearrange("p (e n) -> p e n", e=E)
        qst = arena[:, 0:4096].bitcast(BF16)
        kst = arena[:, 4096:8192].bitcast(BF16)
        qst_h = qst.rearrange("p (h t) -> p h t", h=H)
        kst_h = kst.rearrange("p (h t) -> p h t", h=H)
        probs = arena[:, 8192:16384].rearrange("p (r g n) -> p r g n", r=2, g=G)
        wdec = sb("wdec", [P, KC, 3 * C])
        wdec_out = sb("wdec_out", [P, KC, C])
        router = sb("router", [P, KC, E])
        scale_b = sb("scale_b", [P, C])
        wfull = sb("wfull", [P, KC, 3, C])
        wfull_out = sb("wfull_out", [P, NG, C])
        wcau = sb("wcau", [P, KC, 3, C])
        wcau_out = sb("wcau_out", [P, NG, C])
        bias_qk = sb("bias_qk", [P, 2, KC])
        bias_v = sb("bias_v", [P, C])
        bias_o = sb("bias_o", [P, C])
        work = sb("work", [P, 12800])

        def carver():
            at = [0]

            def carve(words, dt=F32):
                piece = work[:, at[0]:at[0] + words]
                at[0] += words
                assert at[0] <= 12800
                return piece if dt == F32 else piece.bitcast(dt)
            return carve

        class Semaphores:

            def __init__(self, name):
                self.name, self.held = name, []

            def __call__(self, n):
                self.held.append(nc.alloc_semaphore(f"{self.name}_{n}"))
                return self.held[-1]

            def __enter__(self):
                return self

            def __exit__(self, *_):
                nc.clear_and_free_semaphores(self.held)
                nc.all_engine_barrier(sem_only=True)

        def norm_stats(dve, i, mv_ready, rstd_ready):
            for t in range(TPB):
                dve.bn_stats(stats[:, t, :], x_sb[:, bass.ds(i * TPB + t, 1), :])
            dve.drain()
            for t in range(TPB):
                dve.bn_aggr(mv[:, t, :], stats[:, t, :])
            dve.drain()
            dve.tensor_scalar(var_eps[:, :], mv[:, :, 1], EPS, None, ALU.add).then_inc(mv_ready, 1)
            dve.wait_ge(rstd_ready, i + 1)

        def norm_rstd(pool, i, mv_ready, rstd_ready):
            pool.wait_ge(mv_ready, i + 1)
            pool.tensor_tensor(rstd[:, :], var_eps[:, :], powers[:, 0:TPB], ALU.pow).then_inc(rstd_ready, 1)

        def norm_apply(dve, i, xn_ready):
            for t in range(TPB):
                dve.tensor_scalar(xn[:, t, :], x_sb[:, bass.ds(i * TPB + t, 1), :].rearrange("p a c -> p (a c)"),
                                  mv[:, t, 0:1], rstd[:, t:t + 1],
                                  ALU.subtract, ALU.mult).then_inc(xn_ready, 1)

        def transpose_tokens(pe, i, xn_ready, xnT_psum):
            for t in range(TPB):
                pe.wait_ge(xn_ready, i * TPB + (t + 1))
                for k in range(KC):
                    last = pe.transpose(pb[:, k, t * P:(t + 1) * P], xn[:, t, k * P:(k + 1) * P], ident[:, :])
            last.then_inc(xnT_psum, 1)

        def prepare(sem, block_ctx):
            carve = carver()
            wq_f = carve(KC * C)
            colscale = carve(2 * H)
            usev = carve(2 * H)
            raw = carve(KC * 2 * C).rearrange("p (k a n) -> p k a n", k=KC, a=2)
            tmp = carve(2 * 64)
            loaded_x = sem("loaded_x")
            loaded_ffn = sem("loaded_ffn")
            loaded_cau = sem("loaded_cau")
            loaded_w = sem("loaded_w")
            loaded_masks = [sem(f"loaded_masks{n}") for n in range(8)]
            consts_zero = sem("consts_zero")
            consts_done = sem("consts_done")
            scales_ready = sem("scales_ready")
            block = block_ctx.enter_context(nc.Block())

            @block.sync
            def _(sp):
                sp.dma_start(wq_f, ffn_w).then_inc(loaded_ffn, 16)
                for n in range(8):
                    sp.dma_start(arena[:, n * 2048:(n + 1) * 2048],
                                 ffn_masks[:, n * 2048:(n + 1) * 2048]).then_inc(loaded_masks[n], 16)
                for b in range(NBATCH):
                    sp.dma_start(x_sb[:, b * TPB:(b + 1) * TPB, :],
                                 x_in[b * T:(b + 1) * T, :].rearrange("(t p) c -> p t c", p=P)).then_inc(loaded_x, 16)
                sp.wait_ge(loaded_x, 16 * NBATCH)
                sp.wait_ge(loaded_w, 16 * 14)

            @block.scalar
            def _(act):
                act.dma_start(colscale, cau_std).then_inc(loaded_cau, 16)
                act.dma_start(usev, cau_rec).then_inc(loaded_cau, 16)
                act.dma_start(raw[:, :, 0, :], cau_wq).then_inc(loaded_cau, 16)
                act.dma_start(raw[:, :, 1, :], cau_wk).then_inc(loaded_cau, 16)
                for dst, src in ((wcau[:, :, 2, :], cau_wv), (wcau_out[:, :, :], cau_wo), (wdec[:, :, :], dec_wqkv),
                                 (wdec_out[:, :, :], dec_wout), (router[:, :, :], ffn_router),
                                 (scale_b[:, :], ffn_scale), (wfull[:, :, 0, :], full_wq),
                                 (wfull[:, :, 1, :], full_wk), (wfull[:, :, 2, :], full_wv),
                                 (wfull_out[:, :, :], full_wo), (bias_qk[:, 0, :], full_bq),
                                 (bias_qk[:, 1, :], full_bk), (bias_v[:, :], full_bv), (bias_o[:, :], full_bo)):
                    act.dma_start(dst, src).then_inc(loaded_w, 16)

            @block.gpsimd
            def _(pool):
                pool.memset(powers[:, 0:32], -0.5)
                pool.memset(powers[:, 32:64], 0.5)
                pool.wait_ge(loaded_cau, 64)
                pool.tensor_scalar(colscale[:, H:2 * H], usev[:, 0:H], 1e-8, None, ALU.max)
                pool.tensor_scalar(colscale[:, 0:H], colscale[:, 0:H], 1e-8, None, ALU.max)
                pool.drain()
                pool.tensor_tensor(colscale, colscale, powers[:, 32:64], ALU.pow).then_inc(scales_ready, 1)
                pool.memset(ident[:, :], 0.0).then_inc(consts_zero, 1)
                pool.memset(ident_bf[:, :], 0.0).then_inc(consts_zero, 1)
                pool.memset(mask_ts[:, :], 0.0).then_inc(consts_zero, 1)
                pool.memset(mask_st[:, :], 0.0).then_inc(consts_zero, 1)
                pool.wait_ge(consts_zero, 4)
                for m in (ident, ident_bf):
                    pool.affine_select(out=m[:, :], in_=m[:, :], compare_op=ALU.not_equal, fill=1.0, base=0,
                                       pattern=[[-1, P]], channel_multiplier=1).then_inc(consts_done, 1)
                pool.affine_select(out=mask_ts[:, :], in_=mask_ts[:, :], compare_op=ALU.is_ge, fill=MASKED, base=0,
                                   pattern=[[-1, P]], channel_multiplier=1).then_inc(consts_done, 1)
                pool.affine_select(out=mask_st[:, :], in_=mask_st[:, :], compare_op=ALU.is_ge, fill=MASKED, base=0,
                                   pattern=[[1, P]], channel_multiplier=-1).then_inc(consts_done, 1)

            @block.vector
            def _(dve):
                dve.wait_ge(loaded_ffn, 16)
                dve.tensor_scalar(wq_f, wq_f, 2.0, -1.0, ALU.mult, ALU.max)
                dve.drain()
                dve.tensor_scalar(wq_f, wq_f, 1.0, 12582912.0, ALU.min, ALU.add)
                dve.drain()
                dve.tensor_scalar(wq_f, wq_f, 12582912.0, None, ALU.subtract)
                dve.drain()
                dve.wait_ge(loaded_cau, 64)
                s_std, s_rec = colscale[:, 0:H], colscale[:, H:2 * H]
                use, keep = usev[:, 0:H], usev[:, H:2 * H]
                dve.wait_ge(scales_ready, 1)
                dve.tensor_scalar(use, use, 0.1, None, ALU.is_gt)
                dve.drain()
                dve.tensor_scalar(keep, use, -1.0, 1.0, ALU.mult, ALU.add)
                dve.drain()
                t0 = tmp[:, 0:64].rearrange("p (d h) -> p d h", d=8)
                t1 = tmp[:, 64:128].rearrange("p (d h) -> p d h", d=8)
                for k in range(KC):
                    for c in range(KC):
                        def head_vec(v):
                            return v[:, c * 8:(c + 1) * 8].unsqueeze(1).broadcast_to([P, 8, 8])
                        q = raw[:, k, 0, c * P:(c + 1) * P].rearrange("p (d h) -> p d h", d=HD)
                        kk = raw[:, k, 1, c * P:(c + 1) * P].rearrange("p (d h) -> p d h", d=HD)
                        for n, (own, other) in enumerate(((q, kk), (kk, q))):
                            dst = wcau[:, k, n, c * P:(c + 1) * P].rearrange("p (d h) -> p d h", d=HD)
                            dve.tensor_tensor(dst[:, 0:8, :], own[:, 0:8, :], head_vec(s_std), ALU.mult)
                            dve.tensor_tensor(t0, own[:, 8:16, :], head_vec(keep), ALU.mult)
                            dve.tensor_tensor(t1, other[:, 8:16, :], head_vec(use), ALU.mult)
                            dve.drain()
                            dve.tensor_tensor(t0, t0, t1, ALU.add)
                            dve.drain()
                            dve.tensor_tensor(dst[:, 8:16, :], t0, head_vec(s_rec), ALU.mult)
                            dve.drain()
                for n in range(8):
                    dve.wait_ge(loaded_masks[n], 16)
                    piece = arena[:, n * 2048:(n + 1) * 2048].rearrange("p (e n) -> p e n", e=4)
                    dve.tensor_tensor(piece, piece, wq_f.unsqueeze(1).broadcast_to([P, 4, KC * C]), ALU.mult)

        def ffn_route(name):
            with Semaphores(name) as sem, ExitStack() as bc:
                carve = carver()
                logits = carve(NT * E)
                xn_ready, xn_free, xn_stored = sem("xn_ready"), sem("xn_free"), sem("xn_stored")
                xnT_psum, xnT_ready, logits_psum, logits_copied = (sem("xnT_psum"), sem("xnT_ready"),
                                                                   sem("logits_psum"), sem("logits_copied"))
                mv_ready, rstd_ready, xn_kept = sem("mv_ready"), sem("rstd_ready"), sem("xn_kept")
                block = bc.enter_context(nc.Block())

                @block.gpsimd
                def _(pool):
                    with pool.Fori(0, NBATCH) as i:
                        norm_rstd(pool, i, mv_ready, rstd_ready)

                @block.vector
                def _(dve):
                    with dve.Fori(0, NBATCH) as i:
                        norm_stats(dve, i, mv_ready, rstd_ready)
                        dve.wait_ge(xn_free, i + 1)
                        dve.wait_ge(xn_kept, i + 1)
                        norm_apply(dve, i, xn_ready)

                @block.tensor
                def _(pe):
                    pe.sem_inc(xn_free, 1)
                    with pe.Fori(0, NBATCH) as i:
                        transpose_tokens(pe, i, xn_ready, xnT_psum)
                        pe.wait_ge(logits_copied, i + 1)
                        pe.wait_ge(xnT_ready, i + 1)
                        for t in range(TPB):
                            for k in range(KC):
                                last = pe.matmul(pb[:, 2, t * E:(t + 1) * E], xnT[:, k, t * P:(t + 1) * P],
                                                 router[:, k, :], start=(k == 0), stop=(k == KC - 1))
                        last.then_inc(logits_psum, 1)

                @block.scalar
                def _(act):
                    act.sem_inc(logits_copied, 1)
                    with act.Fori(0, NBATCH) as i:
                        act.wait_ge(xnT_psum, i + 1)
                        act.activation(xnT[:, :, :].rearrange("p k t -> p (k t)"),
                                       pb[:, 0:2, :].rearrange("p k t -> p (k t)"), ACT.Copy).then_inc(xnT_ready, 1)
                        act.sem_inc(xn_free, 1)
                        act.wait_ge(logits_psum, i + 1)
                        act.activation(logits[:, bass.ds(i * (TPB * E), TPB * E)], pb[:, 2, 0:TPB * E],
                                       ACT.Copy).then_inc(logits_copied, 1)

                @block.sync
                def _(sp):
                    sp.sem_inc(xn_kept, 1)
                    with sp.Fori(0, NBATCH) as i:
                        sp.wait_ge(xn_ready, i * TPB + TPB)
                        sp.dma_start(xn_dram[bass.ds(i * T, T), :].rearrange("(t p) c -> p t c", p=P),
                                     xn[:, :, :]).then_inc(xn_stored, 16)
                        sp.wait_ge(xn_stored, 16 * i + 16)
                        sp.sem_inc(xn_kept, 1)

        def ffn_experts(name):
            with Semaphores(name) as sem, ExitStack() as bc:
                carve = carver()

                def te(v):
                    return v.rearrange("p (t e) -> p t e", t=NT)

                logits = carve(NT * E)
                shifted = carve(NT * E)
                ex = carve(NT * E)
                cand = carve(NT * E)
                totals = carve(NT * E)
                running = carve(NT * E)
                gate = carve(NT * E)
                onehot = carve(NT * E // 2, BF16)
                lo_hot = carve(NT * P // 2, BF16).rearrange("p (t n) -> p t n", t=NT)
                hi_hot = ex.bitcast(BF16).rearrange("p (t n) -> p t n", t=NT)
                hi_val = cand.bitcast(BF16).rearrange("p (t n) -> p t n", t=NT)
                hi_pid = totals.bitcast(BF16).rearrange("p (t n) -> p t n", t=NT)
                rev = carve(E)
                iota_p = carve(P)
                tile_no = carve(NT)
                part_no = carve(1)
                tri = carve(P // 2, BF16)
                ones = carve(P // 2, BF16)
                coef = carve(NT)
                best = carve(NT)
                pos = carve(NT)
                pos_i = carve(NT, I32)
                hi_i, lo_i = carve(NT, I32), carve(NT, I32)
                hi_f, lo_f = carve(NT), carve(NT)
                cnt, ntile, tend, base = carve(E), carve(E), carve(E), carve(E)
                cnt_i = carve(E, I32)
                ones_e = carve(E)
                owner_f = carve(NSLOT)
                owner_i = carve(NSLOT, I32)
                src_f, src_z = carve(NSLOT), carve(NSLOT)
                src_i = carve(NSLOT, I32)
                own_cmp = running[:, 0:1]
                cmp = shifted
                gat = sbuf_ring(bc, name, "gat", 4)
                yout = sbuf_ring(bc, name, "yout", 4)
                gatT = bc.enter_context(nc.sbuf_tensor(f"{name}_gatT", [P, 2, KC, P], F32))
                idx_a = bc.enter_context(nc.sbuf_tensor(f"{name}_idx", [P, 4], I32))
                del own_cmp
                consts, shifted_ready, ex_ready, onehot_ready, counts_ready = (
                    sem("consts"), sem("shifted_ready"), sem("ex_ready"), sem("onehot_ready"), sem("counts_ready"))
                hots_ready, slots_ready, owner_ready = sem("hots_ready"), sem("slots_ready"), sem("owner_ready")
                gathered, gat_free = [sem(f"gathered{n}") for n in range(4)], sem("gat_free")
                idx_ready = sem("idx_ready")
                gatT_psum, gatT_ready, y_psum, y_ready, y_stored = (sem("gatT_psum"), sem("gatT_ready"), sem("y_psum"),
                                                                    sem("y_ready"), [sem(f"y_stored{n}") for n in range(4)])
                back, back_free = [sem(f"back{n}") for n in range(4)], sem("back_free")
                y_all = sem("y_all")
                gather_turn = sem("gather_turn")
                block = bc.enter_context(nc.Block())

                @block.gpsimd
                def _(pool):
                    pool.iota(iota_p, [[1, P]], base=0, channel_multiplier=0, allow_small_or_imprecise_dtypes=True)
                    pool.iota(rev, [[-1, E]], base=E, channel_multiplier=0, allow_small_or_imprecise_dtypes=True)
                    pool.iota(tile_no, [[1, NT]], base=1, channel_multiplier=0, allow_small_or_imprecise_dtypes=True)
                    pool.iota(part_no, [[0, 1]], base=0, channel_multiplier=1, allow_small_or_imprecise_dtypes=True)
                    pool.memset(ones, 1.0)
                    pool.memset(ones_e, 1.0)
                    pool.memset(gate, 1.0)
                    pool.memset(gat[:, :, :], 0.0)
                    pool.drain()
                    pool.memset(gate.rearrange("p (e t) -> p e t", e=E)[:, :, 0:1], 0.0)
                    pool.affine_select(out=tri, in_=ones, compare_op=ALU.is_ge, fill=0.0, base=-1,
                                       pattern=[[1, P]], channel_multiplier=-1)
                    pool.drain().then_inc(consts, 1)
                    last_token = pool.to_reg(NT * P - 1)
                    last_slot = pool.to_reg(NSLOT * P - 1)
                    with pool.Fori(0, NSLOT // 4) as r:
                        pool.wait_ge(idx_ready, r + 1)
                        for n in range(4):
                            pool.wait_ge(gat_free, r * 4 + (n + 1))
                            pool.sem_inc(gather_turn, 1)
                            pool.indirect_dma_start(gat[:, n, :], None, xn_dram,
                                                    bass.IndirectOffsetOnAxis(ap=idx_a[:, n:n + 1], axis=0),
                                                    bounds_check=last_token, oob_is_err=False).then_inc(gathered[n], 16)
                    pool.wait_ge(y_all, 1)
                    with pool.Fori(0, NT // 4) as r:
                        pool.wait_ge(idx_ready, r + (NSLOT // 4 + 1))
                        for n in range(4):
                            pool.wait_ge(back_free, r * 4 + (n + 1))
                            pool.sem_inc(gather_turn, 1)
                            pool.indirect_dma_start(gat[:, n, :], None, slots_dram,
                                                    bass.IndirectOffsetOnAxis(ap=idx_a[:, n:n + 1], axis=0),
                                                    bounds_check=last_slot, oob_is_err=False).then_inc(back[n], 16)

                @block.vector
                def _(dve):
                    dve.wait_ge(consts, 1)
                    lg = te(logits)
                    dve.tensor_reduce(best, lg, AX_X, ALU.max)
                    dve.drain()
                    dve.tensor_tensor(te(shifted), lg, best.unsqueeze(2).broadcast_to([P, NT, E]),
                                      ALU.subtract).then_inc(shifted_ready, 1)
                    dve.drain()
                    rev_b = rev.unsqueeze(1).broadcast_to([P, NT, E])
                    dve.tensor_scalar(shifted_eq(cand), shifted, 0.0, None, ALU.is_ge)
                    dve.drain()
                    dve.tensor_tensor(te(cand), te(cand), rev_b, ALU.mult)
                    dve.drain()
                    dve.tensor_reduce(best, te(cand), AX_X, ALU.max)
                    dve.drain()
                    dve.tensor_tensor(te(onehot), rev_b, best.unsqueeze(2).broadcast_to([P, NT, E]),
                                      ALU.is_equal).then_inc(onehot_ready, 1)
                    dve.wait_ge(ex_ready, 1)
                    dve.tensor_reduce(pos, te(ex), AX_X, ALU.add)
                    dve.drain()
                    dve.reciprocal(coef, pos)
                    dve.drain()
                    dve.tensor_scalar(coef, coef, 0.5, None, ALU.mult)
                    dve.wait_ge(counts_ready, 1)
                    for half in range(2):
                        dve.tensor_copy(totals.rearrange("p (e t) -> p t e", e=E)[:, half * 16:(half + 1) * 16, :],
                                        pb[:, 2 + half, :].rearrange("p (t e) -> p t e", t=16))
                    dve.drain()
                    dve.tensor_tensor_scan(running, gate, totals, 0.0, ALU.mult, ALU.add)
                    dve.drain()
                    run_et = running.rearrange("p (e t) -> p e t", e=E)
                    dve.tensor_scalar(cnt_i, run_et[:, :, NT - 1], float(P - 1), None, ALU.add)
                    dve.drain()
                    dve.tensor_scalar(cnt_i, cnt_i, 7, None, ALU.arith_shift_right)
                    dve.drain()
                    dve.tensor_copy(ntile, cnt_i)
                    dve.drain()
                    dve.tensor_tensor_scan(tend, ones_e, ntile, 0.0, ALU.mult, ALU.add)
                    dve.drain()
                    dve.tensor_tensor(base, tend, ntile, ALU.subtract)
                    dve.drain()
                    dve.tensor_scalar(base, base, float(P), None, ALU.mult)
                    dve.tensor_tensor(running, running, totals, ALU.subtract)
                    dve.drain()
                    dve.tensor_tensor(run_et, run_et, base.unsqueeze(2).broadcast_to([P, E, NT]), ALU.add)
                    dve.drain()
                    run_te = running.rearrange("p (e t) -> p t e", e=E)
                    for half in range(2):
                        dve.tensor_tensor(te(cand)[:, half * 16:(half + 1) * 16, :],
                                          pb[:, half, :].rearrange("p (t e) -> p t e", t=16),
                                          run_te[:, half * 16:(half + 1) * 16, :], ALU.add)
                    dve.drain()
                    dve.tensor_tensor(cand, cand, onehot, ALU.mult)
                    dve.drain()
                    dve.tensor_reduce(pos, te(cand), AX_X, ALU.add)
                    dve.drain()
                    dve.tensor_copy(pos_i, pos)
                    dve.drain()
                    dve.tensor_scalar(hi_i, pos_i, 7, None, ALU.arith_shift_right)
                    dve.tensor_scalar(lo_i, pos_i, P - 1, None, ALU.bitwise_and)
                    dve.drain()
                    dve.tensor_copy(hi_f, hi_i)
                    dve.tensor_copy(lo_f, lo_i)
                    dve.drain()
                    dve.tensor_tensor(lo_hot, iota_p.unsqueeze(1).broadcast_to([P, NT, P]),
                                      lo_f.unsqueeze(2).broadcast_to([P, NT, P]), ALU.is_equal)
                    dve.tensor_tensor(hi_hot, iota_p[:, 0:NSLOT].unsqueeze(1).broadcast_to([P, NT, NSLOT]),
                                      hi_f.unsqueeze(2).broadcast_to([P, NT, NSLOT]), ALU.is_equal)
                    dve.drain()
                    dve.tensor_tensor(hi_val, hi_hot, tile_no.unsqueeze(2).broadcast_to([P, NT, NSLOT]), ALU.mult)
                    dve.tensor_scalar(hi_pid, hi_hot, part_no, None, ALU.mult)
                    dve.drain().then_inc(hots_ready, 1)
                    for half in range(2):
                        dve.tensor_tensor(te(cmp), iota_p[:, half * 32:(half + 1) * 32].unsqueeze(2).broadcast_to([P, 32, E]),
                                          tend.unsqueeze(1).broadcast_to([P, 32, E]), ALU.is_ge)
                        dve.drain()
                        dve.tensor_reduce(owner_f[:, half * 32:(half + 1) * 32], te(cmp), AX_X, ALU.add)
                        dve.drain()
                    dve.tensor_scalar(owner_f, owner_f, float(E - 1), float(KC * C), ALU.min, ALU.mult)
                    dve.drain()
                    dve.tensor_copy(owner_i, owner_f)
                    dve.drain().then_inc(owner_ready, 1)
                    dve.wait_ge(slots_ready, 1)
                    dve.tensor_scalar(src_f, pb[:, 4, 0:NSLOT], float(P), -float(P), ALU.mult, ALU.add)
                    dve.tensor_scalar(src_z, pb[:, 4, 0:NSLOT], 0.0, 8192.0, ALU.is_equal, ALU.mult)
                    dve.drain()
                    dve.tensor_tensor(src_f, pb[:, 4, NSLOT:2 * NSLOT], src_f, ALU.add)
                    dve.drain()
                    dve.tensor_tensor(src_f, src_f, src_z, ALU.add)
                    dve.drain()
                    dve.tensor_copy(src_i, src_f)
                    dve.drain()
                    def scale_round(r, first=False):
                        if not first:
                            dve.wait_ge(gat_free, r * 4 + 4)
                        dve.tensor_copy(idx_a[:, :], src_i[:, bass.ds(r * 4, 4)]).then_inc(idx_ready, 1)
                        for n in range(4):
                            dve.wait_ge(y_psum, r * 4 + (n + 1))
                            if not first:
                                dve.wait_ge(y_stored[n], r * 16)
                            dve.tensor_tensor(yout[:, n, :], pb[:, 6 + n % 2, 0:C], scale_b[:, :],
                                              ALU.mult).then_inc(y_ready, 1)

                    scale_round(0, first=True)
                    with dve.Fori(1, NSLOT // 4) as r:
                        scale_round(r)
                    with dve.Fori(0, NT // 4) as r:
                        dve.tensor_copy(idx_a[:, :], pos_i[:, bass.ds(r * 4, 4)]).then_inc(idx_ready, 1)
                        for n in range(4):
                            dve.wait_ge(back[n], 16 * r + 16)
                            dve.scalar_tensor_tensor(x_sb[:, bass.ds(r * 4 + n, 1), :].rearrange("p a c -> p (a c)"),
                                                     gat[:, n, :], coef[:, bass.ds(r * 4 + n, 1)],
                                                     x_sb[:, bass.ds(r * 4 + n, 1), :].rearrange("p a c -> p (a c)"),
                                                     ALU.mult, ALU.add).then_inc(back_free, 1)

                @block.scalar
                def _(act):
                    act.wait_ge(shifted_ready, 1)
                    act.activation(ex, shifted, ACT.Exp).then_inc(ex_ready, 1)
                    with act.Fori(0, NSLOT // 2) as r:
                        for n in range(2):
                            act.wait_ge(gatT_psum, r * 2 + (n + 1))
                            act.activation(gatT[:, n, :, :].rearrange("p k t -> p (k t)"), pb[:, 4 + n, 0:C],
                                           ACT.Copy).then_inc(gatT_ready, 1)

                @block.tensor
                def _(pe):
                    pe.sem_inc(gat_free, 4)
                    pe.wait_ge(onehot_ready, 1)
                    pe.wait_ge(consts, 1)
                    for half in range(2):
                        oh = onehot[:, half * 512:(half + 1) * 512]
                        pe.matmul(pb[:, half, :], tri, oh, start=True, stop=True)
                        last = pe.matmul(pb[:, 2 + half, :], ones, oh, start=True, stop=True)
                    last.then_inc(counts_ready, 1)
                    pe.wait_ge(hots_ready, 1)
                    for t in range(NT):
                        pe.matmul(pb[:, 4, 0:NSLOT], lo_hot[:, t, :], hi_val[:, t, :], start=(t == 0), stop=(t == NT - 1))
                    for t in range(NT):
                        last = pe.matmul(pb[:, 4, NSLOT:2 * NSLOT], lo_hot[:, t, :], hi_pid[:, t, :],
                                         start=(t == 0), stop=(t == NT - 1))
                    last.then_inc(slots_ready, 1)
                    pe.wait_ge(owner_ready, 1)
                    with pe.Fori(0, NSLOT // 4) as r:
                        for n in range(4):
                            w0 = pe.value_load(owner_i[0:1, bass.ds(r * 4 + n, 1)], min_val=0, max_val=(E - 1) * KC * C)
                            pe.wait_ge(gathered[n], 16 * r + 16)
                            for k in range(KC):
                                last = pe.transpose(pb[:, 4 + n % 2, k * P:(k + 1) * P], gat[:, n, k * P:(k + 1) * P],
                                                    ident[:, :])
                            last.then_inc(gatT_psum, 1)
                            pe.wait_ge(gatT_ready, r * 4 + (n + 1))
                            pe.sem_inc(gat_free, 1)
                            pe.wait_ge(y_ready, r * 4 + (n + 1))
                            for k in range(KC):
                                last = pe.matmul(pb[:, 6 + n % 2, 0:C], gatT[:, n % 2, k, :],
                                                 arena[:, bass.ds(w0 + k * C, C)],
                                                 start=(k == 0), stop=(k == KC - 1))
                            last.then_inc(y_psum, 1)

                @block.sync
                def _(sp):
                    sp.sem_inc(back_free, 4)
                    sp.sem_inc(y_ready, 2)
                    with sp.Fori(0, NSLOT // 4) as r:
                        for n in range(4):
                            sp.wait_ge(y_ready, r * 4 + (n + 3))
                            sp.dma_start(slots_dram[bass.ds((r * 4 + n) * P, P), :], yout[:, n, :])\
                              .then_inc(y_stored[n], 16)
                    for n in range(4):
                        sp.wait_ge(y_stored[n], 16 * (NSLOT // 4))
                    sp.sem_inc(y_all, 1)

        def decay_attention(name):
            with Semaphores(name) as sem, ExitStack() as bc:
                carve = carver()
                F = KC * T

                def kt(v):
                    return v.rearrange("p (k t) -> p k t", k=KC)

                decay = carve(F)
                block_ones = carve(P)
                rate = carve(KC)
                relu_q, exp_q, relu_k, exp_k = carve(F), carve(F), carve(F), carve(F)
                kv, run_kv, run_k, mixed = carve(F), carve(F), carve(F), carve(F)
                param_loaded, rate_exp, rate_ready, consts = (sem("param_loaded"), sem("rate_exp"), sem("rate_ready"),
                                                              sem("consts"))
                mv_ready, rstd_ready, xn_ready, xn_free = (sem("mv_ready"), sem("rstd_ready"), sem("xn_ready"),
                                                           sem("xn_free"))
                xnT_psum, xnT_ready, q_psum, k_psum, v_psum = (sem("xnT_psum"), sem("xnT_ready"), sem("q_psum"),
                                                               sem("k_psum"), sem("v_psum"))
                q_read, k_read, v_read, phi_ready = sem("q_read"), sem("k_read"), sem("v_read"), sem("phi_ready")
                dots_ready, den_psum, mixed_ready, o_psum, x_added, run_ready, qkv_ready = (
                    sem("dots_ready"), sem("den_psum"), sem("mixed_ready"), sem("o_psum"), sem("x_added"),
                    sem("run_ready"), sem("qkv_ready"))
                block = bc.enter_context(nc.Block())

                @block.sync
                def _(sp):
                    sp.dma_start(rate, dec_param).then_inc(param_loaded, 16)

                @block.gpsimd
                def _(pool):
                    pool.memset(block_ones, 1.0)
                    pool.drain()
                    b3 = block_ones.rearrange("p (h d) -> p h d", d=HD)
                    pool.affine_select(out=b3, in_=b3, compare_op=ALU.is_ge, fill=0.0, base=0,
                                       pattern=[[-HD, P // HD], [0, HD]], channel_multiplier=1)
                    pool.drain()
                    pool.affine_select(out=b3, in_=b3, compare_op=ALU.is_ge, fill=0.0, base=HD - 1,
                                       pattern=[[HD, P // HD], [0, HD]], channel_multiplier=-1)
                    pool.drain().then_inc(consts, 1)
                    with pool.Fori(0, NBATCH) as i:
                        norm_rstd(pool, i, mv_ready, rstd_ready)
                        pool.wait_ge(run_ready, i + 1)
                        pool.tensor_tensor(relu_q, relu_q, run_kv, ALU.mult).then_inc(qkv_ready, 1)

                @block.scalar
                def _(act):
                    act.wait_ge(param_loaded, 16)
                    act.activation(rate, rate, ACT.Exp, scale=-1.0).then_inc(rate_exp, 1)
                    act.sem_inc(mixed_ready, 1)
                    with act.Fori(0, NBATCH) as i:
                        act.wait_ge(xnT_psum, i + 1)
                        act.activation(xnT[:, :, :].rearrange("p k t -> p (k t)"),
                                       pb[:, 0:2, :].rearrange("p k t -> p (k t)"), ACT.Copy).then_inc(xnT_ready, 1)
                        act.sem_inc(xn_free, 1)
                        act.wait_ge(mixed_ready, i + 1)
                        for bank, got, rel, ex, read in ((2, q_psum, relu_q, exp_q, q_read),
                                                         (4, k_psum, relu_k, exp_k, k_read)):
                            src = pb[:, bank:bank + 2, :].rearrange("p k t -> p (k t)")
                            act.wait_ge(got, i + 1)
                            act.activation(rel, src, ACT.Relu)
                            act.activation(ex, src, ACT.Exp).then_inc(read, 1)

                @block.tensor
                def _(pe):
                    pe.sem_inc(xn_free, 1)
                    pe.sem_inc(x_added, 1)
                    pe.sem_inc(v_read, 1)
                    pe.wait_ge(consts, 1)
                    with pe.Fori(0, NBATCH) as i:
                        pe.wait_ge(x_added, i + 1)
                        transpose_tokens(pe, i, xn_ready, xnT_psum)
                        pe.wait_ge(xnT_ready, i + 1)
                        pe.wait_ge(v_read, i + 1)
                        for bank, col, done in ((2, 0, q_psum), (4, C, k_psum), (6, 2 * C, v_psum)):
                            for c in range(KC):
                                for k in range(KC):
                                    last = pe.matmul(pb[:, bank + c, :], wdec[:, k, col + c * P:col + (c + 1) * P],
                                                     xnT[:, k, :], start=(k == 0), stop=(k == KC - 1))
                            last.then_inc(done, 1)
                        pe.wait_ge(q_read, i + 1)
                        pe.wait_ge(dots_ready, i + 1)
                        for c in range(KC):
                            last = pe.matmul(pb[:, 2 + c, :], block_ones, kt(run_k)[:, c, :], start=True, stop=True)
                        last.then_inc(den_psum, 1)
                        pe.wait_ge(mixed_ready, i + 2)
                        for t in range(TPB):
                            for c in range(KC):
                                last = pe.matmul(pb[:, t // 2, (t % 2) * C:(t % 2 + 1) * C],
                                                 kt(mixed)[:, c, t * P:(t + 1) * P], wdec_out[:, c, :],
                                                 start=(c == 0), stop=(c == KC - 1))
                        last.then_inc(o_psum, 1)

                @block.vector
                def _(dve):
                    dve.wait_ge(rate_exp, 1)
                    dve.tensor_scalar(rate, rate, 1.0, None, ALU.add)
                    dve.drain()
                    dve.reciprocal(rate, rate)
                    dve.memset(decay, 1.0)
                    dve.drain()
                    for c in range(KC):
                        dve.tensor_scalar(kt(decay)[:, c, :], kt(decay)[:, c, :], rate[:, c:c + 1], None, ALU.mult)
                    dve.drain()
                    dve.memset(kt(decay)[:, :, 0:1], 0.0)
                    dve.drain()
                    with dve.Fori(0, NBATCH) as i:
                        norm_stats(dve, i, mv_ready, rstd_ready)
                        dve.wait_ge(xn_free, i + 1)
                        norm_apply(dve, i, xn_ready)
                        dve.wait_ge(q_read, i + 1)
                        dve.scalar_tensor_tensor(relu_q, exp_q, 1.0, relu_q, ALU.min, ALU.add)
                        dve.wait_ge(k_read, i + 1)
                        dve.scalar_tensor_tensor(relu_k, exp_k, 1.0, relu_k, ALU.min, ALU.add)
                        dve.drain()
                        dve.wait_ge(v_psum, i + 1)
                        dve.tensor_tensor(kv, pb[:, 6:8, :].rearrange("p k t -> p (k t)"), relu_k,
                                          ALU.mult).then_inc(v_read, 1)
                        dve.tensor_tensor_scan(run_k, decay, relu_k, 0.0, ALU.mult, ALU.add)
                        dve.drain()
                        dve.tensor_tensor(run_k, run_k, relu_q, ALU.mult).then_inc(dots_ready, 1)
                        dve.tensor_tensor_scan(run_kv, decay, kv, 0.0, ALU.mult, ALU.add)
                        dve.drain().then_inc(run_ready, 1)
                        dve.wait_ge(den_psum, i + 1)
                        dve.wait_ge(qkv_ready, i + 1)
                        dve.tensor_scalar(kv, pb[:, 2:4, :].rearrange("p k t -> p (k t)"), 1e-6, None, ALU.max)
                        dve.drain()
                        dve.reciprocal(kv, kv)
                        dve.drain()
                        dve.tensor_tensor(mixed, relu_q, kv, ALU.mult).then_inc(mixed_ready, 1)
                        dve.wait_ge(o_psum, i + 1)
                        xi = x_sb[:, bass.ds(i * TPB, TPB), :].rearrange("p t c -> p (t c)")
                        dve.tensor_tensor(xi, pb[:, 0:2, :].rearrange("p k t -> p (k t)"), xi,
                                          ALU.add).then_inc(x_added, 1)
                        dve.drain()

        def score_columns(causal, half):
            if not causal:
                return [(s * 256, half * 256, 256) for s in range(TPB)]
            if half == 0:
                return [(0, 0, 256), (256, 128, 128)]
            return [(0, 256, 256), (256, 256, 256), (512, 256, 256), (768, 384, 128)]

        def attention_plan(causal):
            pv_cost, row_cost = (0.3, 0.2) if causal else (0.5, 0.22)

            def items(rows, offset):
                out = []
                for r in rows:
                    out.append(("row", offset, r))
                    if r % 16 == 1 and r > 16:
                        out.append(("turn_max", offset, r // 16 - 1))
                    if r == NROWS - 1:
                        out.append(("turn_max", offset, NG - 1))
                return out

            prologue = [("norm", 0)] + [("turn_x", 0, k) for k in range(KC)]
            for n in range(NQK):
                prologue.append(("project", 0, n))
                if n:
                    prologue.append(("second", 0, n - 1))
            prologue += [("second", 0, NQK - 1), ("value", 0, 0), ("value", 0, 1)] + items(range(EARLY), 0)

            def body(last):
                base = []

                def pv(slot):
                    n, s = divmod(slot - 5, 4)
                    if slot >= 5 and s < len(score_columns(causal, n % 2)):
                        base.append(("pv", n, s))
                        if n % 2 and s == 3:
                            base.append(("divide", n // 2))
                for u in range(NUNITS):
                    pv(u)
                    base.append(("unit", u))
                    if not last:
                        if u == 2:
                            base.append(("norm", 1))
                        if u in (6, 7):
                            base.append(("turn_x", 1, u - 6))
                        if u in (9, 11, 13, 15):
                            base.append(("project", 1, (u - 9) // 2))
                        if u in (11, 13, 15, 17):
                            base.append(("second", 1, (u - 11) // 2))
                for slot in range(NUNITS, NUNITS + 5):
                    pv(slot)
                if not last:
                    base += [("value", 1, 0), ("value", 1, 1)]
                base += [("out", 0, 0), ("out", 0, 1)]
                cost = {"unit": 0.43, "pv": pv_cost, "turn_x": 0.43, "project": 1.7, "value": 1.7, "out": 3.4}
                rows = items(range(EARLY, NROWS), 0) + ([] if last else items(range(EARLY), 1))
                until = sum(cost.get(s[0], 0) for s in base)
                if last:
                    until *= 0.42
                plan, spent, put = [], 0.0, 0
                for step in base:
                    while put < len(rows) and put <= len(rows) * spent / until:
                        plan.append(rows[put])
                        put += 1
                    plan.append(step)
                    spent += cost.get(step[0], 0)
                plan += rows[put:]
                for g in range(1, NG):
                    assert plan.index(("turn_max", 0, g)) < plan.index(("unit", 8 * g)), "shifts come too late"
                return plan

            return prologue, body(False), body(True)

        NQK = 2 * KC
        NROWS = H * TPB
        NUNITS = H * 2
        EARLY = 30
        RING = (4, 5, 7)
        IN_RING = ("row", "turn_max", "turn_x", "project", "value", "out")

        def attention(name, causal):
            w, w_out = (wcau, wcau_out) if causal else (wfull, wfull_out)
            prologue, steady, final = attention_plan(causal)

            def ring_numbers(plan):
                out, n, d = [], 0, 0
                for step in plan:
                    out.append((n, d))
                    n += step[0] in IN_RING
                    d += step[0] in IN_RING and step[0] != "turn_x"
                return out, n, d

            _, ring_pro, read_pro = ring_numbers(prologue)
            _, ring_all, read_all = ring_numbers(steady)
            assert ring_pro % len(RING) == 0 and ring_all % len(RING) == 0

            with Semaphores(name) as sem, ExitStack() as bc:
                carve = carver()
                parts = [carve(NQK * T // 2, BF16).rearrange("p (n t) -> p n t", n=NQK) for _ in range(3)]
                rest = carve(NQK * T).rearrange("p (n t) -> p n t", n=NQK)
                v_aug = carve(TPB * H * SLOT).rearrange("p (s h d) -> p s h d", s=TPB, h=H)
                o_t = carve(NG * T).rearrange("p (g t) -> p g t", g=NG)
                turned = carve(T)
                den = carve(T // SLOT)
                row_max = carve(NG * 16).rearrange("p (g n) -> p g n", g=NG)
                shift_hi = carve(NG * P // 2, BF16).rearrange("p (g n) -> p g n", g=NG)
                shift_lo = carve(NG * P // 2, BF16).rearrange("p (g n) -> p g n", g=NG)

                mv_ready, rstd_ready, xn_ready = sem("mv_ready"), sem("rstd_ready"), sem("xn_ready")
                ring_full = sem("ring_full")
                ring_read = sem("ring_read")
                xnT_ready = sem("xnT_ready")
                part0, part1, part2 = sem("part0"), sem("part1"), sem("part2")
                stacked = [sem(f"stacked{c}") for c in range(KC)]
                aug_set, shift_ready = sem("aug_set"), sem("shift_ready")
                shifted = [sem(f"shifted{g}") for g in range(NG)]
                unit_psum, unit_exp, pv_psum, pv_read = sem("unit_psum"), sem("unit_exp"), sem("pv_psum"), sem("pv_read")
                o_ready, x_biased = sem("o_ready"), sem("x_biased")
                stack_turn = sem("stack_turn")
                block = bc.enter_context(nc.Block())

                def run(engine, steps):
                    steps(prologue, 0, 0, 0, [])
                    with engine.Fori(0, NBATCH - 1) as i:
                        steps(steady, i, i * ring_all + ring_pro, i * read_all + read_pro, steady)
                    i = NBATCH - 1
                    steps(final, i, i * ring_all + ring_pro, i * read_all + read_pro, steady)

                @block.gpsimd
                def _(pool):
                    pool.memset(kst[96:98, :], 1.0)
                    pool.drain()
                    pool.memset(v_aug[:, :, :, HD:SLOT], 1.0)
                    pool.drain().then_inc(aug_set, 1)

                    def steps(plan, i, ring0, read0, before):
                        for step in plan:
                            b = i + step[1]
                            if step[0] == "norm":
                                norm_rstd(pool, b, mv_ready, rstd_ready)
                            if step[0] == "second":
                                n = step[2]
                                pool.wait_ge(part1, NQK * b + (n + 1))
                                pool.tensor_tensor(parts[2][:, n, :], rest[:, n, :], parts[1][:, n, :],
                                                   ALU.subtract).then_inc(part2, 1)
                                if n == NQK - 1 and not causal:
                                    pool.wait_ge(xn_ready, TPB * b + TPB)
                                    xi = x_sb[:, bass.ds(b * TPB, TPB), :]
                                    pool.tensor_tensor(xi, xi, bias_o[:, :].unsqueeze(1).broadcast_to([P, TPB, C]),
                                                       ALU.add).then_inc(x_biased, 1)
                    run(pool, steps)

                @block.sync
                def _(sp):
                    def stack_chunk(n, count):
                        c, is_k = n // 2, n % 2
                        stack, order = (kst, PARTS_K) if is_k else (qst, PARTS_Q)
                        for part, done in ((0, part0), (1, part1), (2, part2)):
                            sp.wait_ge(done, count)
                            for slot, p in enumerate(order):
                                if p == part:
                                    sp.dma_start(stack[slot * HD:(slot + 1) * HD, c * 4096:(c + 1) * 4096],
                                                 parts[part][:, n, :]).then_inc(stacked[c], 16)

                    def store_shift(g, count):
                        sp.wait_ge(shift_ready, count)
                        for row, src in ((96, shift_hi), (97, shift_lo)):
                            sp.dma_start(qst[row:row + 1, g * 2048:(g + 1) * 2048],
                                         src[0:16, g, :]).then_inc(shifted[g], 16)

                    for n in range(NQK):
                        stack_chunk(n, n + 1)
                    store_shift(0, 1)
                    with sp.Fori(0, NBATCH - 1) as i:
                        chunk_done = [sp.snap(NQK * i + (NQK + n + 1)) for n in range(NQK)]
                        shift_done = [sp.snap(NG * i + (g + 1)) for g in range(1, NG + 1)]
                        half_done, all_done = sp.snap(NUNITS * i + NUNITS // 2), sp.snap(NUNITS * i + NUNITS)
                        store_shift(1, shift_done[0])
                        store_shift(2, shift_done[1])
                        sp.wait_ge(unit_psum, half_done)
                        sp.sem_inc(stack_turn, 1)
                        stack_chunk(0, chunk_done[0])
                        stack_chunk(1, chunk_done[1])
                        store_shift(3, shift_done[2])
                        store_shift(0, shift_done[3])
                        sp.wait_ge(unit_psum, all_done)
                        sp.sem_inc(stack_turn, 1)
                        stack_chunk(2, chunk_done[2])
                        stack_chunk(3, chunk_done[3])
                    for g in range(1, NG):
                        store_shift(g, NG * (NBATCH - 1) + g + 1)
                    for g in range(NG):
                        sp.wait_ge(shifted[g], 32 * NBATCH)

                @block.scalar
                def _(act):
                    def steps(plan, i, ring0, read0, before):
                        numbers, _, _ = ring_numbers(plan)
                        for step, (j, d) in zip(plan, numbers):
                            if step[0] == "turn_x":
                                act.wait_ge(ring_full, ring0 + (j + 1))
                                act.activation(xnT[:, step[2], :], pb[:, RING[j % 3], :], ACT.Copy).then_inc(xnT_ready, 1)
                            elif step[0] == "project":
                                n = step[2]
                                act.wait_ge(ring_full, ring0 + (j + 1))
                                if causal:
                                    act.activation(parts[0][:, n, :], pb[:, RING[j % 3], :], ACT.Copy).then_inc(part0, 1)
                                else:
                                    act.activation(parts[0][:, n, :], pb[:, RING[j % 3], :], ACT.Identity,
                                                   bias=bias_qk[:, n % 2, n // 2:n // 2 + 1]).then_inc(part0, 1)
                            elif step[0] == "second":
                                at = plan.index(("project", step[1], step[2]))
                                act.wait_ge(ring_read, read0 + (numbers[at][1] + 1))
                                n = step[2]
                                act.activation(parts[1][:, n, :], rest[:, n, :], ACT.Copy).then_inc(part1, 1)
                            elif step[0] == "unit":
                                u = step[1]
                                half, hh = (u // G) % 2, u % G
                                off, _, m = score_columns(causal, half)[-1]
                                act.wait_ge(unit_psum, NUNITS * i + (u + 1))
                                bank = 2 * (u % 2)
                                act.activation(probs[:, (u // G) % 2, hh, 0:off + m],
                                               pb[:, bank:bank + 2, :].rearrange("p k t -> p (k t)")[:, 0:off + m],
                                               ACT.Exp, scale=HD ** -0.5).then_inc(unit_exp, 1)
                    run(act, steps)

                @block.tensor
                def _(pe):
                    pe.sem_inc(pv_read, 1)
                    pe.wait_ge(aug_set, 1)

                    def ring_bank(j, ring0, read0, numbers, plan, before):
                        k, source, r0 = j - 3, plan, read0
                        if k < 0 and not before:
                            return RING[j % 3]
                        if k < 0:
                            items = [s for s in before if s[0] in IN_RING]
                            step, reads = items[k], None
                            after = sum(1 for s in items[len(items) + k + 1:] if s[0] != "turn_x")
                            assert step[0] != "turn_x"
                            pe.wait_ge(ring_read, read0 - after)
                        else:
                            at = [n for n, s in enumerate(plan) if s[0] in IN_RING][k]
                            if plan[at][0] == "turn_x":
                                pe.wait_ge(xnT_ready, KC * (before_batch[0] + plan[at][1]) + (plan[at][2] + 1))
                            else:
                                pe.wait_ge(ring_read, read0 + (numbers[at][1] + 1))
                        return RING[j % 3]

                    before_batch = [0]

                    def steps(plan, i, ring0, read0, before):
                        numbers, _, _ = ring_numbers(plan)
                        before_batch[0] = i
                        for step, (j, d) in zip(plan, numbers):
                            kind = step[0]
                            if kind in IN_RING:
                                bank = ring_bank(j, ring0, read0, numbers, plan, before)
                                b = i + step[1]
                            if kind == "row":
                                r = step[2]
                                h, t = r // TPB, r % TPB
                                if r % 32 == 0:
                                    pe.wait_ge(stacked[h // 8], 192 * b + 192)
                                width = P * (t + 1) if causal else T
                                last = pe.matmul(pb[:, bank, 0:width], qst_h[0:96, h, t * P:(t + 1) * P],
                                                 kst_h[0:96, h, 0:width], start=True, stop=not causal)
                                if causal:
                                    last = pe.matmul(pb[:, bank, t * P:(t + 1) * P], ident_bf[:, :], mask_ts[:, :],
                                                     start=False, stop=True)
                            elif kind == "turn_max":
                                g = step[2]
                                at = [n for n, s in enumerate(plan) if s == ("row", step[1], 16 * g + 15)]
                                if at:
                                    pe.wait_ge(ring_read, read0 + (numbers[at[0]][1] + 1))
                                last = pe.transpose(pb[0:16, bank, 0:P], row_max[:, g, :], ident[:, :])
                            elif kind == "turn_x":
                                k = step[2]
                                for t in range(TPB):
                                    pe.wait_ge(xn_ready, TPB * b + (t + 1))
                                    last = pe.transpose(pb[:, bank, t * P:(t + 1) * P], xn[:, t, k * P:(k + 1) * P],
                                                        ident[:, :])
                            elif kind == "project":
                                n = step[2]
                                pe.wait_ge(xnT_ready, KC * b + KC)
                                c, is_k = n // 2, n % 2
                                for k in range(KC):
                                    last = pe.matmul(pb[:, bank, :], w[:, k, is_k, c * P:(c + 1) * P], xnT[:, k, :],
                                                     start=(k == 0), stop=(k == KC - 1))
                            elif kind == "value":
                                for t in (2 * step[2], 2 * step[2] + 1):
                                    for k in range(KC):
                                        last = pe.matmul(pb[:, bank, (t % 2) * C:(t % 2 + 1) * C],
                                                         xnT[:, k, t * P:(t + 1) * P], w[:, k, 2, :],
                                                         start=(k == 0), stop=(k == KC - 1))
                            elif kind == "out":
                                pe.wait_ge(o_ready, NG * i + NG)
                                for t in (2 * step[2], 2 * step[2] + 1):
                                    for g in range(NG):
                                        last = pe.matmul(pb[:, bank, (t % 2) * C:(t % 2 + 1) * C],
                                                         o_t[:, g, t * P:(t + 1) * P], w_out[:, g, :],
                                                         start=(g == 0), stop=(g == NG - 1))
                            elif kind == "unit":
                                u = step[1]
                                g, half, hh = u // 8, (u // G) % 2, u % G
                                h = g * G + hh
                                if u % 8 == 0:
                                    pe.wait_ge(shifted[g], 32 * i + 32)
                                if u >= 2:
                                    pe.wait_ge(unit_exp, NUNITS * i + (u - 1))
                                flat = pb[:, 2 * (u % 2):2 * (u % 2) + 2, :].rearrange("p k t -> p (k t)")
                                for s, (off, q0, m) in enumerate(score_columns(causal, half)):
                                    diagonal = causal and q0 <= s * P
                                    last = pe.matmul(flat[:, off:off + m], kst_h[0:ROWS, h, s * P:(s + 1) * P],
                                                     qst_h[0:ROWS, h, q0:q0 + m], start=True, stop=not diagonal)
                                    if diagonal:
                                        at = off + s * P - q0
                                        last = pe.matmul(flat[:, at:at + P], ident_bf[:, :], mask_st[:, :],
                                                         start=False, stop=True)
                                last.then_inc(unit_psum, 1)
                            elif kind == "pv":
                                n, s = step[1], step[2]
                                g, half = n // 2, n % 2
                                cols = score_columns(causal, half)
                                off, q0, m = cols[s]
                                if s == 0:
                                    pe.wait_ge(unit_exp, NUNITS * i + G * (n + 1))
                                    if half == 0:
                                        pe.wait_ge(pv_read, NG * i + (g + 1))
                                for hh in range(G):
                                    end = pe.matmul(pb[hh * SLOT:(hh + 1) * SLOT, 6, q0:q0 + m],
                                                    v_aug[:, s, g * G + hh, :], probs[:, n % 2, hh, off:off + m],
                                                    start=(s == 0), stop=(s == len(cols) - 1))
                                if half == 1 and s == len(cols) - 1:
                                    end.then_inc(pv_psum, 1)
                            if kind in IN_RING:
                                last.then_inc(ring_full, 1)
                    run(pe, steps)

                @block.vector
                def _(dve):
                    dve.wait_ge(aug_set, 1)

                    def steps(plan, i, ring0, read0, before):
                        numbers, _, _ = ring_numbers(plan)
                        for step, (j, d) in zip(plan, numbers):
                            kind, bank = step[0], RING[j % 3]
                            if kind in IN_RING and kind != "turn_x":
                                b = i + step[1]
                                if kind == "project":
                                    dve.wait_ge(part0, NQK * b + (step[2] + 1))
                                    if before:
                                        dve.wait_ge(part2, NQK * b)
                                else:
                                    dve.wait_ge(ring_full, ring0 + (j + 1))
                            if kind == "norm":
                                norm_stats(dve, i + step[1], mv_ready, rstd_ready)
                                norm_apply(dve, i + step[1], xn_ready)
                            elif kind == "row":
                                r = step[2]
                                width = P * (r % TPB + 1) if causal else T
                                dve.tensor_reduce(row_max[:, r // 16, r % 16:r % 16 + 1], pb[:, bank, 0:width],
                                                  AX_X, ALU.max).then_inc(ring_read, 1)
                            elif kind == "turn_max":
                                g = step[2]
                                dve.tensor_scalar(shift_hi[0:16, g, :], pb[0:16, bank, 0:P], -1.0, None, ALU.mult)
                                dve.drain()
                                dve.scalar_tensor_tensor(shift_lo[0:16, g, :], pb[0:16, bank, 0:P], -1.0,
                                                         shift_hi[0:16, g, :], ALU.mult,
                                                         ALU.subtract).then_inc(ring_read, 1)
                                dve.drain().then_inc(shift_ready, 1)
                            elif kind == "project":
                                n = step[2]
                                if causal:
                                    dve.tensor_tensor(rest[:, n, :], pb[:, bank, :], parts[0][:, n, :],
                                                      ALU.subtract).then_inc(ring_read, 1)
                                else:
                                    dve.scalar_tensor_tensor(rest[:, n, :], pb[:, bank, :],
                                                             bias_qk[:, n % 2, n // 2:n // 2 + 1], parts[0][:, n, :],
                                                             ALU.add, ALU.subtract).then_inc(ring_read, 1)
                            elif kind == "value":
                                half = step[2]
                                src = pb[:, bank, :].rearrange("p (s h d) -> p s h d", s=2, h=H)
                                for t in range(2):
                                    dst = v_aug[:, 2 * half + t, :, 0:HD]
                                    if causal:
                                        last = dve.tensor_copy(dst, src[:, t, :, :])
                                    else:
                                        last = dve.tensor_tensor(dst, src[:, t, :, :],
                                                                 bias_v[:, :].rearrange("p (h d) -> p h d", h=H), ALU.add)
                                last.then_inc(ring_read, 1)
                            elif kind == "divide":
                                g = step[1]
                                dve.drain()
                                dve.wait_ge(pv_psum, NG * i + (g + 1))
                                dve.transpose(turned, pb[:, 6, :]).then_inc(pv_read, 1)
                                dve.drain()
                                t3 = turned.rearrange("p (b r) -> p b r", r=SLOT)
                                dve.reciprocal(den, t3[:, :, HD])
                                dve.drain()
                                dve.tensor_tensor(t3[:, :, 0:HD], t3[:, :, 0:HD],
                                                  den.unsqueeze(2).broadcast_to([P, T // SLOT, HD]), ALU.mult)
                                dve.drain()
                                dve.transpose(o_t[:, g, :], turned).then_inc(o_ready, 1)
                            elif kind == "out":
                                if not causal:
                                    dve.wait_ge(x_biased, i + 1)
                                xi = x_sb[:, bass.ds(i * TPB + 2 * step[2], 2), :].rearrange("p t c -> p (t c)")
                                dve.scalar_tensor_tensor(xi, pb[:, bank, :], 0.5 if causal else 1.0, xi,
                                                         ALU.mult, ALU.add).then_inc(ring_read, 1)
                    run(dve, steps)

        def sbuf_ring(bc, name, what, n):
            return bc.enter_context(nc.sbuf_tensor(f"{name}_{what}", [P, n, C], F32))

        def shifted_eq(v):
            return v

        def store_out():
            with ExitStack() as bc:
                stored = bc.enter_context(nc.semaphore("stored"))
                block = bc.enter_context(nc.Block())

                @block.sync
                def _(sp):
                    for b in range(NBATCH):
                        sp.dma_start(out[b * T:(b + 1) * T, :].rearrange("(t p) c -> p t c", p=P),
                                     x_sb[:, b * TPB:(b + 1) * TPB, :]).then_inc(stored, 16)
                    sp.wait_ge(stored, 16 * NBATCH)

        with Semaphores("prep") as sem, ExitStack() as bc:
            prepare(sem, bc)
        for n, layer in enumerate(layers):
            if layer == "ffn":
                ffn_route(f"r{n}")
                ffn_experts(f"e{n}")
            elif layer == "decay":
                decay_attention(f"d{n}")
            elif layer == "causal":
                attention(f"a{n}", True)
            elif layer == "full":
                attention(f"a{n}", False)
        store_out()


LAYERS = ("ffn", "decay", "ffn", "causal", "full", "causal")


def _laid_out(inp):
    import numpy as np
    H, HD, KC, P, E, C = 16, 16, 2, 128, 32, 256
    a = {k: np.asarray(v) for k, v in inp.items()}

    def chunked(w):
        return w.reshape(KC, P, -1).transpose(1, 0, 2)

    def head_minor(w):
        return w.reshape(C, 2, 8, HD).transpose(0, 1, 3, 2).reshape(C, C)

    def padded_rows(w):
        z = np.zeros((4, 4, 32, C), w.dtype)
        z[:, :, :HD] = w.reshape(4, 4, HD, C)
        return z.reshape(4, P, C).transpose(1, 0, 2)

    def every_partition(v):
        return np.broadcast_to(v.reshape(1, -1), (P, v.size))

    wa = a["L1_ffn_Wa"]
    q_std, k_std, v, q_low, k_low = np.split(wa, [128, 256, 512, 640], axis=1)

    def with_tail(std, low):
        return np.concatenate([std.reshape(C, H, 8), low.reshape(C, H, 8)], axis=2).reshape(C, C)

    def column_bias(b):
        return b.reshape(2, 8, HD).transpose(2, 1, 0).reshape(P, 2)

    laid = {
        "x_in": a["L0_attn_x"].reshape(-1, C),
        "dec_wqkv": chunked(a["L0_attn_w_qkv"]),
        "dec_wout": chunked(a["L0_attn_w_out"]),
        "dec_param": np.repeat(a["L0_attn_decay_param"], HD).reshape(KC, P).T,
        "ffn_w": chunked(a["L0_ffn_weight"].T).reshape(P, KC * C),
        "ffn_scale": every_partition(a["L0_ffn_scale"]),
        "ffn_masks": a["L0_ffn_expert_masks"].transpose(2, 0, 1).reshape(KC, P, E, C).transpose(1, 2, 0, 3).reshape(P, -1),
        "ffn_router": chunked(a["L0_ffn_router_w"].T),
        "full_wq": chunked(head_minor(a["L1_attn_wq"].T)),
        "full_wk": chunked(head_minor(a["L1_attn_wk"].T)),
        "full_wv": chunked(a["L1_attn_wv"].T),
        "full_wo": padded_rows(a["L1_attn_wo"].T),
        "full_bq": column_bias(a["L1_attn_bq"]),
        "full_bk": column_bias(a["L1_attn_bk"]),
        "full_bv": every_partition(a["L1_attn_bv"]),
        "full_bo": every_partition(a["L1_attn_bo"]),
        "cau_wq": chunked(head_minor(with_tail(q_std, q_low))),
        "cau_wk": chunked(head_minor(with_tail(k_std, k_low))),
        "cau_wv": chunked(v),
        "cau_wo": padded_rows(a["L1_ffn_Wp"]),
        "cau_std": every_partition(np.concatenate([a["L1_ffn_w_std"], a["L1_ffn_w_std"]])),
        "cau_rec": every_partition(np.concatenate([a["L1_ffn_w_rec"], a["L1_ffn_w_rec"]])),
    }
    return {k: np.ascontiguousarray(v) for k, v in laid.items()}


def kernel(**inputs):
    import numpy as _np
    import concourse.bacc as _bacc
    from concourse import mybir as _mybir
    from concourse.bass_utils import run_bass_kernel_spmd as _run

    nc = _bacc.Bacc("TRN2", target_bir_lowering=False, num_devices=1)
    arrays, args = {}, []
    for name, a in _laid_out(inputs).items():
        arrays[f"in_{name}"] = a
        args.append(nc.dram_tensor(f"in_{name}", a.shape, _mybir.dt.from_np(a.dtype), kind="ExternalInput").ap())
    out = nc.dram_tensor("out_x", (8 * 512, 256), _mybir.dt.from_np(_np.dtype("float32")), kind="ExternalOutput").ap()
    macaron_kernel(nc, *args, out, LAYERS)
    r = _run(nc, [arrays], core_ids=[0])
    return r.results[0]["out_x"].reshape(8, 512, 256)
```

```python
from contextlib import ExitStack

import concourse.bass as bass
from concourse import mybir

F32 = mybir.dt.float32
BF16 = mybir.dt.bfloat16
I32 = mybir.dt.int32
ALU = mybir.AluOpType
ACT = mybir.ActivationFunctionType
AX_X = mybir.AxisListType.X

P = 128
NBATCH, T, C = 8, 512, 256
TPB = T // P
NT = NBATCH * TPB
KC = C // P
H, HD = 16, 16
E = 32
NSLOT = 64
EPS = 1e-5
G = 4
NG = H // G
SLOT = 32
MASKED = -1.0e30
ROWS = 98
PARTS_Q = (0, 1, 2, 0, 1, 0)
PARTS_K = (0, 0, 0, 1, 1, 2)


def macaron_kernel(nc, x_in, dec_wqkv, dec_wout, dec_param, ffn_w, ffn_scale, ffn_masks, ffn_router,
                   full_wq, full_wk, full_wv, full_wo, full_bq, full_bk, full_bv, full_bo,
                   cau_wq, cau_wk, cau_wv, cau_wo, cau_std, cau_rec, out, layers):
    ctx = ExitStack()
    with ctx:
        def sb(name, shape, dt=F32):
            return ctx.enter_context(nc.sbuf_tensor(name, shape, dt))

        pb = ctx.enter_context(nc.psum_tensor("pb", [P, 8, 512], F32))

        xn_dram = nc.dram_tensor("xn_dram", [NT * P, C], F32).ap()
        slots_dram = nc.dram_tensor("slots_dram", [NSLOT * P, C], F32).ap()

        x_sb = sb("x_sb", [P, NT, C])
        xn = sb("xn", [P, TPB, C])
        xnT = sb("xnT", [P, KC, T])
        stats = sb("stats", [P, TPB, 6])
        mv = sb("mv", [P, TPB, 2])
        rstd = sb("rstd", [P, TPB])
        var_eps = sb("var_eps", [P, TPB])
        powers = sb("powers", [P, 64])
        ident = sb("ident", [P, P])
        ident_bf = sb("ident_bf", [P, P], BF16)
        mask_ts = sb("mask_ts", [P, P], BF16)
        mask_st = sb("mask_st", [P, P], BF16)
        arena = sb("arena", [P, E * KC * C])
        qst = arena[:, 0:4096].bitcast(BF16)
        kst = arena[:, 4096:8192].bitcast(BF16)
        qst_h = qst.rearrange("p (h t) -> p h t", h=H)
        kst_h = kst.rearrange("p (h t) -> p h t", h=H)
        probs = arena[:, 8192:16384].rearrange("p (r g n) -> p r g n", r=2, g=G)
        wdec = sb("wdec", [P, KC, 3 * C])
        wdec_out = sb("wdec_out", [P, KC, C])
        router = sb("router", [P, KC, E])
        scale_b = sb("scale_b", [P, C])
        wfull = sb("wfull", [P, KC, 3, C])
        wfull_out = sb("wfull_out", [P, NG // 2, C])
        wcau = sb("wcau", [P, KC, 3, C])
        wcau_out = sb("wcau_out", [P, NG // 2, C])
        bias_qk = sb("bias_qk", [P, 2, KC])
        bias_v = sb("bias_v", [P, C])
        bias_o = sb("bias_o", [P, C])
        wq = sb("wq", [P, KC * C])
        work = sb("work", [P, 12800])

        def carver():
            at = [0]

            def carve(words, dt=F32):
                piece = work[:, at[0]:at[0] + words]
                at[0] += words
                assert at[0] <= 12800
                return piece if dt == F32 else piece.bitcast(dt)
            return carve

        class Semaphores:

            def __init__(self, name):
                self.name, self.held = name, []

            def __call__(self, n):
                self.held.append(nc.alloc_semaphore(f"{self.name}_{n}"))
                return self.held[-1]

            def __enter__(self):
                return self

            def __exit__(self, *_):
                nc.clear_and_free_semaphores(self.held)
                nc.all_engine_barrier(sem_only=True)

        def norm_stats(dve, i, mv_ready, rstd_ready):
            for t in range(TPB):
                dve.bn_stats(stats[:, t, :], x_sb[:, bass.ds(i * TPB + t, 1), :])
            norm_mean(dve, mv_ready)

        def norm_mean(dve, mv_ready):
            dve.drain()
            for t in range(TPB):
                dve.bn_aggr(mv[:, t, :], stats[:, t, :])
            dve.drain()
            dve.tensor_scalar(var_eps[:, :], mv[:, :, 1], EPS, None, ALU.add).then_inc(mv_ready, 1)

        def norm_rstd(pool, i, mv_ready, rstd_ready):
            pool.wait_ge(mv_ready, i + 1)
            pool.tensor_tensor(rstd[:, :], var_eps[:, :], powers[:, 0:TPB], ALU.pow).then_inc(rstd_ready, 1)

        def norm_apply(dve, i, rstd_ready, xn_ready, tiles=range(4)):
            dve.wait_ge(rstd_ready, i + 1)
            for t in tiles:
                dve.tensor_scalar(xn[:, t, :], x_sb[:, bass.ds(i * TPB + t, 1), :].rearrange("p a c -> p (a c)"),
                                  mv[:, t, 0:1], rstd[:, t:t + 1],
                                  ALU.subtract, ALU.mult).then_inc(xn_ready, 1)

        def transpose_tokens(pe, i, xn_ready, xnT_psum, bank):
            for t in range(TPB):
                pe.wait_ge(xn_ready, i * TPB + (t + 1))
                for k in range(KC):
                    last = pe.transpose(pb[:, bank + k, t * P:(t + 1) * P], xn[:, t, k * P:(k + 1) * P], ident[:, :])
            last.then_inc(xnT_psum, 1)

        def prepare(sem, load, block_ctx):
            carve = carver()
            wq_f = wq[:, :]
            colscale = carve(2 * H)
            usev = carve(2 * H)
            raw = carve(KC * 2 * C).rearrange("p (k a n) -> p k a n", k=KC, a=2)
            tmp = carve(2 * 64)
            loaded_x = sem("loaded_x")
            loaded_ffn = sem("loaded_ffn")
            loaded_scales, loaded_cau = sem("loaded_scales"), sem("loaded_cau")
            loaded_router = sem("loaded_router")
            consts_zero = sem("consts_zero")
            consts_done = sem("consts_done")
            scales_ready = sem("scales_ready")
            block = block_ctx.enter_context(nc.Block())

            @block.sync
            def _(sp):
                sp.dma_start(wq_f, ffn_w).then_inc(loaded_ffn, 16)
                for b in range(NBATCH):
                    sp.dma_start(x_sb[:, b * TPB:(b + 1) * TPB, :],
                                 x_in[b * T:(b + 1) * T, :].rearrange("(t p) c -> p t c", p=P)).then_inc(loaded_x, 16)
                sp.wait_ge(loaded_x, 16 * NBATCH)
                sp.wait_ge(loaded_router, 16)

            @block.scalar
            def _(act):
                act.dma_start(colscale, cau_std).then_inc(loaded_scales, 16)
                act.dma_start(usev, cau_rec).then_inc(loaded_scales, 16)
                act.dma_start(raw[:, :, 0, :], cau_wq).then_inc(loaded_cau, 16)
                act.dma_start(raw[:, :, 1, :], cau_wk).then_inc(loaded_cau, 16)
                act.dma_start(router[:, :, :], ffn_router).then_inc(loaded_router, 16)
                for dst, src in ((wcau[:, :, 2, :], cau_wv), (wcau_out[:, :, :], cau_wo), (wdec[:, :, :], dec_wqkv),
                                 (wdec_out[:, :, :], dec_wout), (scale_b[:, :], ffn_scale), (wfull[:, :, 0, :], full_wq),
                                 (wfull[:, :, 1, :], full_wk), (wfull[:, :, 2, :], full_wv),
                                 (wfull_out[:, :, :], full_wo), (bias_qk[:, 0, :], full_bq),
                                 (bias_qk[:, 1, :], full_bk), (bias_v[:, :], full_bv), (bias_o[:, :], full_bo)):
                    act.dma_start(dst, src).then_inc(load.weights, 16)

            @block.gpsimd
            def _(pool):
                pool.memset(powers[:, 0:32], -0.5)
                pool.memset(powers[:, 32:64], 0.5)
                pool.wait_ge(loaded_scales, 32)
                pool.tensor_scalar(colscale[:, H:2 * H], usev[:, 0:H], 1e-8, None, ALU.max)
                pool.tensor_scalar(colscale[:, 0:H], colscale[:, 0:H], 1e-8, None, ALU.max)
                pool.drain()
                pool.tensor_tensor(colscale, colscale, powers[:, 32:64], ALU.pow).then_inc(scales_ready, 1)
                pool.memset(ident[:, :], 0.0).then_inc(consts_zero, 1)
                pool.memset(ident_bf[:, :], 0.0).then_inc(consts_zero, 1)
                pool.memset(mask_ts[:, :], 0.0).then_inc(consts_zero, 1)
                pool.memset(mask_st[:, :], 0.0).then_inc(consts_zero, 1)
                pool.wait_ge(consts_zero, 4)
                for m in (ident, ident_bf):
                    pool.affine_select(out=m[:, :], in_=m[:, :], compare_op=ALU.not_equal, fill=1.0, base=0,
                                       pattern=[[-1, P]], channel_multiplier=1).then_inc(consts_done, 1)
                pool.affine_select(out=mask_ts[:, :], in_=mask_ts[:, :], compare_op=ALU.is_ge, fill=MASKED, base=0,
                                   pattern=[[-1, P]], channel_multiplier=1).then_inc(consts_done, 1)
                pool.affine_select(out=mask_st[:, :], in_=mask_st[:, :], compare_op=ALU.is_ge, fill=MASKED, base=0,
                                   pattern=[[1, P]], channel_multiplier=-1).then_inc(consts_done, 1)

            @block.vector
            def _(dve):
                dve.wait_ge(loaded_ffn, 16)
                dve.tensor_scalar(wq_f, wq_f, 2.0, -1.0, ALU.mult, ALU.max)
                dve.drain()
                dve.tensor_scalar(wq_f, wq_f, 1.0, 12582912.0, ALU.min, ALU.add)
                dve.drain()
                dve.tensor_scalar(wq_f, wq_f, 12582912.0, None, ALU.subtract)
                dve.drain()
                dve.wait_ge(loaded_cau, 32)
                s_std, s_rec = colscale[:, 0:H], colscale[:, H:2 * H]
                use, keep = usev[:, 0:H], usev[:, H:2 * H]
                dve.wait_ge(scales_ready, 1)
                dve.tensor_scalar(use, use, 0.1, None, ALU.is_gt)
                dve.drain()
                dve.tensor_scalar(keep, use, -1.0, 1.0, ALU.mult, ALU.add)
                dve.drain()
                t0 = tmp[:, 0:64].rearrange("p (d h) -> p d h", d=8)
                t1 = tmp[:, 64:128].rearrange("p (d h) -> p d h", d=8)
                for k in range(KC):
                    for c in range(KC):
                        def head_vec(v):
                            return v[:, c * 8:(c + 1) * 8].unsqueeze(1).broadcast_to([P, 8, 8])
                        q = raw[:, k, 0, c * P:(c + 1) * P].rearrange("p (d h) -> p d h", d=HD)
                        kk = raw[:, k, 1, c * P:(c + 1) * P].rearrange("p (d h) -> p d h", d=HD)
                        for n, (own, other) in enumerate(((q, kk), (kk, q))):
                            dst = wcau[:, k, n, c * P:(c + 1) * P].rearrange("p (d h) -> p d h", d=HD)
                            dve.tensor_tensor(dst[:, 0:8, :], own[:, 0:8, :], head_vec(s_std), ALU.mult)
                            dve.tensor_tensor(t0, own[:, 8:16, :], head_vec(keep), ALU.mult)
                            dve.tensor_tensor(t1, other[:, 8:16, :], head_vec(use), ALU.mult)
                            dve.drain()
                            dve.tensor_tensor(t0, t0, t1, ALU.add)
                            dve.drain()
                            dve.tensor_tensor(dst[:, 8:16, :], t0, head_vec(s_rec), ALU.mult)
                            dve.drain()

        class Loads:

            def __init__(self, sem):
                self.masks = [sem(f"masks{n}") for n in range(8)]
                self.weights = sem("weights")
                self.experts_ready = sem("experts_ready")

            def expert_weights(self, pool):
                for n in range(8):
                    pool.wait_ge(self.masks[n], 16)
                    piece = arena[:, n * 2048:(n + 1) * 2048].rearrange("p (e n) -> p e n", e=4)
                    pool.tensor_tensor(piece, piece, wq[:, :].unsqueeze(1).broadcast_to([P, 4, KC * C]),
                                       ALU.mult).then_inc(self.experts_ready, 1)

        GR = 8

        def ffn(name, load):
            with Semaphores(name) as sem, ExitStack() as bc:
                carve = carver()

                def te(v):
                    return v.rearrange("p (t e) -> p t e", t=NT)

                logits = carve(NT * E)
                shifted = carve(NT * E)
                ex = carve(NT * E)
                cand_words = carve(3 * NT * E)
                cand = cand_words[:, 0:NT * E]
                gat_words = cand_words[:, NT * E:]
                totals = gat_words[:, 0:NT * E]
                running = gat_words[:, NT * E:]
                gate = carve(NT * E)
                onehot = carve(NT * E // 2, BF16)
                lo_words = carve(NT * P // 2)
                lo_hot = lo_words.bitcast(BF16).rearrange("p (t n) -> p t n", t=NT)
                hi_hot = ex.bitcast(BF16).rearrange("p (t n) -> p t n", t=NT)
                hi_both = cand_words[:, 0:2 * NT * E].bitcast(BF16).rearrange("p (t v n) -> p t v n", t=NT, v=2)
                hi_val, hi_pid = hi_both[:, :, 0, :], hi_both[:, :, 1, :]
                rev = carve(E)
                iota_p = carve(P)
                tile_no = carve(NT)
                part_no = carve(1)
                tri = carve(P // 2, BF16)
                ones = carve(P // 2, BF16)
                coef = carve(NT)
                best = carve(NT)
                pos = carve(NT)
                pos_i = carve(NT, I32)
                hi_i, lo_i = carve(NT, I32), carve(NT, I32)
                hi_f, lo_f = carve(NT), carve(NT)
                cnt, ntile, tend, base = carve(E), carve(E), carve(E), carve(E)
                cnt_i = carve(E, I32)
                ones_e = carve(E)
                owner_f = carve(NSLOT)
                packed = carve(NSLOT // 4)
                packed_i = carve(NSLOT // 4, I32)
                src_f, src_z = carve(NSLOT), carve(NSLOT)
                src_i = carve(NSLOT, I32)
                cmp = shifted
                gat = gat_words.rearrange("p (n c) -> p n c", n=GR)
                yout = lo_words.rearrange("p (n c) -> p n c", n=GR)
                gatT = shifted.rearrange("p (n k m) -> p n k m", n=4, k=KC)
                idx = carve(2 * GR, I32)
                xn2 = yout.rearrange("p (b t) c -> p b t c", b=2)
                xnT2 = gat_words.rearrange("p (b k t) -> p b k t", b=2, k=KC)
                stats2 = carve(2 * TPB * 6).rearrange("p (b t n) -> p b t n", b=2, t=TPB)
                mv2 = carve(2 * TPB * 2).rearrange("p (b t n) -> p b t n", b=2, t=TPB)
                var2 = carve(2 * TPB).rearrange("p (b t) -> p b t", b=2)
                rstd2 = carve(2 * TPB).rearrange("p (b t) -> p b t", b=2)
                mv_ready, rstd_ready, xn_ready = sem("mv_ready"), sem("rstd_ready"), sem("xn_ready")
                xn_stored = [sem("xn_stored0"), sem("xn_stored1")]
                xn_all = sem("xn_all")
                xnT_psum, xnT_ready, logits_psum, logits_ready = (sem("xnT_psum"), sem("xnT_ready"),
                                                                  sem("logits_psum"), sem("logits_ready"))
                by_expert = ex.rearrange("p (b t) -> p b t", b=2)
                expert_psum, expert_ready, logits_turn = sem("expert_psum"), sem("expert_ready"), sem("logits_turn")
                consts, shifted_ready, ex_ready, onehot_ready, counts_ready = (
                    sem("consts"), sem("shifted_ready"), sem("ex_ready"), sem("onehot_ready"), sem("counts_ready"))
                hots_ready, slots_ready, owner_ready = sem("hots_ready"), sem("slots_ready"), sem("owner_ready")
                gathered, gat_free = [sem(f"gathered{n}") for n in range(GR)], sem("gat_free")
                gatT_psum, gatT_ready, y_psum, y_ready, y_stored = (sem("gatT_psum"), sem("gatT_ready"), sem("y_psum"),
                                                                    sem("y_ready"), [sem(f"y_stored{n}") for n in range(GR)])
                back, back_free = [sem(f"back{n}") for n in range(GR)], sem("back_free")
                src_ready, src_copied, pos_copied = sem("src_ready"), sem("src_copied"), sem("pos_copied")
                y_all = sem("y_all")
                gather_turn = sem("gather_turn")
                block = bc.enter_context(nc.Block())

                @block.gpsimd
                def _(pool):
                    pool.iota(iota_p, [[1, P]], base=0, channel_multiplier=0, allow_small_or_imprecise_dtypes=True)
                    pool.iota(rev, [[-1, E]], base=E, channel_multiplier=0, allow_small_or_imprecise_dtypes=True)
                    pool.iota(tile_no, [[1, NT]], base=1, channel_multiplier=0, allow_small_or_imprecise_dtypes=True)
                    pool.iota(part_no, [[0, 1]], base=0, channel_multiplier=1, allow_small_or_imprecise_dtypes=True)
                    pool.memset(ones, 1.0)
                    pool.memset(ones_e, 1.0)
                    pool.memset(gate, 1.0)
                    pool.drain()
                    pool.memset(gate.rearrange("p (e t) -> p e t", e=E)[:, :, 0:1], 0.0)
                    pool.affine_select(out=tri, in_=ones, compare_op=ALU.is_ge, fill=0.0, base=-1,
                                       pattern=[[1, P]], channel_multiplier=-1)
                    pool.drain().then_inc(consts, 1)
                    def rstd_of(i, h):
                        pool.wait_ge(mv_ready, i + 1)
                        pool.tensor_tensor(rstd2[:, h, :], var2[:, h, :], powers[:, 0:TPB],
                                           ALU.pow).then_inc(rstd_ready, 1)
                    with pool.Fori(0, NBATCH // 2) as r:
                        for h in range(2):
                            rstd_of(r * 2 + h, h)
                    last_token = pool.to_reg(NT * P - 1)
                    last_slot = pool.to_reg(NSLOT * P - 1)
                    def gather(r, n, src, copied, dst_free, source, last_row, done):
                        if n % GR == 0:
                            pool.tensor_copy(idx[:, n:n + GR], src[:, bass.ds(r * (2 * GR) + n, GR)]).then_inc(copied, 1)
                            pool.wait_ge(copied, r * 2 + (n // GR + 1))
                            pool.sem_inc(gather_turn, 1)
                        pool.wait_ge(dst_free, r * (2 * GR) + (n + 1))
                        pool.sem_inc(gather_turn, 1)
                        pool.indirect_dma_start(gat[:, n % GR, :], None, source,
                                                bass.IndirectOffsetOnAxis(ap=idx[:, n:n + 1], axis=0),
                                                bounds_check=last_row, oob_is_err=False).then_inc(done[n % GR], 16)

                    if load:
                        load.expert_weights(pool)
                    pool.wait_ge(src_ready, 1)
                    pool.wait_ge(xn_all, 1)
                    with pool.Fori(0, NSLOT // (2 * GR)) as r:
                        for n in range(2 * GR):
                            gather(r, n, src_i, src_copied, gat_free, xn_dram, last_token, gathered)
                    pool.wait_ge(y_all, 1)
                    with pool.Fori(0, NT // (2 * GR)) as r:
                        for n in range(2 * GR):
                            gather(r, n, pos_i, pos_copied, back_free, slots_dram, last_slot, back)

                @block.vector
                def _(dve):
                    def stats_of(i, h):
                        for t in range(TPB):
                            dve.bn_stats(stats2[:, h, t, :], x_sb[:, bass.ds(i * TPB + t, 1), :])
                        dve.drain()
                        for t in range(TPB):
                            dve.bn_aggr(mv2[:, h, t, :], stats2[:, h, t, :])
                        dve.drain()
                        dve.tensor_scalar(var2[:, h, :], mv2[:, h, :, 1], EPS, None, ALU.add).then_inc(mv_ready, 1)

                    def apply_to(i, h, later):
                        dve.wait_ge(rstd_ready, i + 1)
                        if later:
                            dve.wait_ge(xnT_psum, i - 1)
                            dve.wait_ge(xn_stored[h], (i - h) * 8)
                        for t in range(TPB):
                            dve.tensor_scalar(xn2[:, h, t, :],
                                              x_sb[:, bass.ds(i * TPB + t, 1), :].rearrange("p a c -> p (a c)"),
                                              mv2[:, h, t, 0:1], rstd2[:, h, t:t + 1],
                                              ALU.subtract, ALU.mult).then_inc(xn_ready, 1)

                    stats_of(0, 0)
                    stats_of(1, 1)
                    apply_to(0, 0, False)
                    stats_of(2, 0)
                    apply_to(1, 1, False)
                    stats_of(3, 1)
                    apply_to(2, 0, True)
                    with dve.Fori(2, NBATCH // 2) as r:
                        stats_of(r * 2, 0)
                        apply_to(r * 2 - 1, 1, True)
                        stats_of(r * 2 + 1, 1)
                        apply_to(r * 2, 0, True)
                    apply_to(NBATCH - 1, 1, True)
                    dve.wait_ge(consts, 1)
                    dve.wait_ge(logits_ready, NBATCH)
                    lg = te(logits)
                    dve.tensor_reduce(best, lg, AX_X, ALU.max)
                    dve.drain()
                    dve.tensor_tensor(te(shifted), lg, best.unsqueeze(2).broadcast_to([P, NT, E]),
                                      ALU.subtract).then_inc(shifted_ready, 1)
                    dve.drain()
                    rev_b = rev.unsqueeze(1).broadcast_to([P, NT, E])
                    dve.tensor_scalar(cand, shifted, 0.0, None, ALU.is_ge)
                    dve.drain()
                    dve.tensor_tensor(te(cand), te(cand), rev_b, ALU.mult)
                    dve.drain()
                    dve.tensor_reduce(best, te(cand), AX_X, ALU.max)
                    dve.drain()
                    dve.tensor_tensor(te(onehot), rev_b, best.unsqueeze(2).broadcast_to([P, NT, E]),
                                      ALU.is_equal).then_inc(onehot_ready, 1)
                    dve.wait_ge(ex_ready, 1)
                    dve.tensor_reduce(pos, te(ex), AX_X, ALU.add)
                    dve.drain()
                    dve.reciprocal(coef, pos)
                    dve.drain()
                    dve.tensor_scalar(coef, coef, 0.5, None, ALU.mult)
                    dve.wait_ge(counts_ready, 1)
                    for half in range(2):
                        dve.tensor_copy(totals.rearrange("p (e t) -> p t e", e=E)[:, half * 16:(half + 1) * 16, :],
                                        pb[:, 2 + half, :].rearrange("p (t e) -> p t e", t=16))
                    dve.drain()
                    dve.tensor_tensor_scan(running, gate, totals, 0.0, ALU.mult, ALU.add)
                    dve.drain()
                    run_et = running.rearrange("p (e t) -> p e t", e=E)
                    dve.tensor_scalar(cnt_i, run_et[:, :, NT - 1], float(P - 1), None, ALU.add)
                    dve.drain()
                    dve.tensor_scalar(cnt_i, cnt_i, 7, None, ALU.arith_shift_right)
                    dve.drain()
                    dve.tensor_copy(ntile, cnt_i)
                    dve.drain()
                    dve.tensor_tensor_scan(tend, ones_e, ntile, 0.0, ALU.mult, ALU.add)
                    dve.drain()
                    dve.tensor_tensor(base, tend, ntile, ALU.subtract)
                    dve.drain()
                    dve.tensor_scalar(base, base, float(P), None, ALU.mult)
                    dve.tensor_tensor(running, running, totals, ALU.subtract)
                    dve.drain()
                    dve.tensor_tensor(run_et, run_et, base.unsqueeze(2).broadcast_to([P, E, NT]), ALU.add)
                    dve.drain()
                    run_te = running.rearrange("p (e t) -> p t e", e=E)
                    for half in range(2):
                        dve.tensor_tensor(te(cand)[:, half * 16:(half + 1) * 16, :],
                                          pb[:, half, :].rearrange("p (t e) -> p t e", t=16),
                                          run_te[:, half * 16:(half + 1) * 16, :], ALU.add)
                    dve.drain()
                    dve.tensor_tensor(cand, cand, onehot, ALU.mult)
                    dve.drain()
                    dve.tensor_reduce(pos, te(cand), AX_X, ALU.add)
                    dve.drain()
                    dve.tensor_copy(pos_i, pos)
                    dve.drain()
                    dve.tensor_scalar(hi_i, pos_i, 7, None, ALU.arith_shift_right)
                    dve.tensor_scalar(lo_i, pos_i, P - 1, None, ALU.bitwise_and)
                    dve.drain()
                    dve.tensor_copy(hi_f, hi_i)
                    dve.tensor_copy(lo_f, lo_i)
                    dve.drain()
                    dve.wait_ge(xn_all, 1)
                    dve.tensor_tensor(lo_hot, iota_p.unsqueeze(1).broadcast_to([P, NT, P]),
                                      lo_f.unsqueeze(2).broadcast_to([P, NT, P]), ALU.is_equal)
                    dve.tensor_tensor(hi_hot, iota_p[:, 0:NSLOT].unsqueeze(1).broadcast_to([P, NT, NSLOT]),
                                      hi_f.unsqueeze(2).broadcast_to([P, NT, NSLOT]), ALU.is_equal)
                    dve.drain()
                    dve.tensor_tensor(hi_val, hi_hot, tile_no.unsqueeze(2).broadcast_to([P, NT, NSLOT]), ALU.mult)
                    dve.tensor_scalar(hi_pid, hi_hot, part_no, None, ALU.mult)
                    dve.drain().then_inc(hots_ready, 1)
                    dve.wait_ge(slots_ready, 1)
                    dve.tensor_scalar(src_f, pb[:, 4, 0:NSLOT], float(P), -float(P), ALU.mult, ALU.add)
                    dve.tensor_scalar(src_z, pb[:, 4, 0:NSLOT], 0.0, 8192.0, ALU.is_equal, ALU.mult)
                    dve.drain()
                    dve.tensor_tensor(src_f, pb[:, 4, NSLOT:2 * NSLOT], src_f, ALU.add)
                    dve.drain()
                    dve.tensor_tensor(src_f, src_f, src_z, ALU.add)
                    dve.drain()
                    dve.tensor_copy(src_i, src_f).then_inc(src_ready, 1)
                    for half in range(2):
                        dve.tensor_tensor(te(cmp), iota_p[:, half * 32:(half + 1) * 32].unsqueeze(2).broadcast_to([P, 32, E]),
                                          tend.unsqueeze(1).broadcast_to([P, 32, E]), ALU.is_ge)
                        dve.drain()
                        dve.tensor_reduce(owner_f[:, half * 32:(half + 1) * 32], te(cmp), AX_X, ALU.add)
                        dve.drain()
                    dve.tensor_scalar(owner_f, owner_f, float(E - 1), None, ALU.min)
                    dve.drain()
                    of4 = owner_f.rearrange("p (q j) -> p q j", j=4)
                    dve.scalar_tensor_tensor(packed, of4[:, :, 3], float(E), of4[:, :, 2], ALU.mult, ALU.add)
                    dve.drain()
                    dve.scalar_tensor_tensor(packed, packed, float(E), of4[:, :, 1], ALU.mult, ALU.add)
                    dve.drain()
                    dve.scalar_tensor_tensor(packed, packed, float(E), of4[:, :, 0], ALU.mult, ALU.add)
                    dve.drain()
                    dve.tensor_copy(packed_i, packed).then_inc(owner_ready, 1)
                    def scale_round(r, first=False):
                        for n in range(GR):
                            dve.wait_ge(y_psum, r * GR + (n + 1))
                            if not first:
                                dve.wait_ge(y_stored[n], r * 16)
                            dve.tensor_tensor(yout[:, n, :], pb[:, 4 + n % 4, 0:C], scale_b[:, :],
                                              ALU.mult).then_inc(y_ready, 1)

                    if load:
                        dve.wait_ge(load.weights, 16 * 13)
                    scale_round(0, first=True)
                    with dve.Fori(1, NSLOT // GR) as r:
                        scale_round(r)
                    with dve.Fori(0, NT // GR) as r:
                        for n in range(GR):
                            dve.wait_ge(back[n], 16 * r + 16)
                            dve.scalar_tensor_tensor(x_sb[:, bass.ds(r * GR + n, 1), :].rearrange("p a c -> p (a c)"),
                                                     gat[:, n, :], coef[:, bass.ds(r * GR + n, 1)],
                                                     x_sb[:, bass.ds(r * GR + n, 1), :].rearrange("p a c -> p (a c)"),
                                                     ALU.mult, ALU.add).then_inc(back_free, 1)

                @block.scalar
                def _(act):
                    def copies(i, h):
                        act.wait_ge(xnT_psum, i + 1)
                        act.activation(xnT2[:, h, :, :].rearrange("p k t -> p (k t)"),
                                       pb[:, 2 * h:2 * h + 2, :].rearrange("p k t -> p (k t)"),
                                       ACT.Copy).then_inc(xnT_ready, 1)

                    def copy_logits(i, h):
                        act.wait_ge(logits_psum, i + 1)
                        act.activation(logits[:, bass.ds(i * (TPB * E), TPB * E)], pb[:, 6 + h, 0:TPB * E],
                                       ACT.Copy).then_inc(logits_ready, 1)

                    def copy_by_expert(i, h):
                        act.wait_ge(expert_psum, i + 1)
                        act.activation(by_expert[0:E, h, :], pb[0:E, 4 + h, :], ACT.Copy).then_inc(expert_ready, 1)

                    copies(0, 0)
                    copies(1, 1)
                    copy_by_expert(0, 0)
                    with act.Fori(1, NBATCH // 2) as r:
                        copies(r * 2, 0)
                        copy_logits(r * 2 - 2, 0)
                        copy_by_expert(r * 2 - 1, 1)
                        copies(r * 2 + 1, 1)
                        copy_logits(r * 2 - 1, 1)
                        copy_by_expert(r * 2, 0)
                    copy_logits(NBATCH - 2, 0)
                    copy_by_expert(NBATCH - 1, 1)
                    copy_logits(NBATCH - 1, 1)
                    act.wait_ge(shifted_ready, 1)
                    act.activation(ex, shifted, ACT.Exp).then_inc(ex_ready, 1)
                    with act.Fori(0, NSLOT // 4) as r:
                        for n in range(4):
                            act.wait_ge(gatT_psum, r * 4 + (n + 1))
                            act.activation(gatT[:, n, :, :].rearrange("p k t -> p (k t)"), pb[:, n, 0:C],
                                           ACT.Copy).then_inc(gatT_ready, 1)

                @block.tensor
                def _(pe):
                    def turn(i, h, later):
                        if later:
                            pe.wait_ge(xnT_ready, i - 1)
                        for t in range(TPB):
                            pe.wait_ge(xn_ready, i * TPB + (t + 1))
                            for k in range(KC):
                                last = pe.transpose(pb[:, 2 * h + k, t * P:(t + 1) * P],
                                                    xn2[:, h, t, k * P:(k + 1) * P], ident[:, :])
                        last.then_inc(xnT_psum, 1)

                    def route(i, h):
                        pe.wait_ge(xnT_ready, i + 1)
                        for k in range(KC):
                            last = pe.matmul(pb[0:E, 4 + h, :], router[:, k, :], xnT2[:, h, k, :],
                                             start=(k == 0), stop=(k == KC - 1))
                        last.then_inc(expert_psum, 1)

                    def turn_logits(i, h, later):
                        if later:
                            pe.wait_ge(logits_ready, i - 1)
                        pe.wait_ge(expert_ready, i + 1)
                        pe.sem_inc(logits_turn, 1)
                        for t in range(TPB):
                            last = pe.transpose(pb[:, 6 + h, t * E:(t + 1) * E], by_expert[0:E, h, t * P:(t + 1) * P],
                                                ident[0:E, 0:E])
                        last.then_inc(logits_psum, 1)

                    turn(0, 0, False)
                    turn(1, 1, False)
                    route(0, 0)
                    turn(2, 0, True)
                    turn_logits(0, 0, False)
                    route(1, 1)
                    turn(3, 1, True)
                    turn_logits(1, 1, False)
                    route(2, 0)
                    with pe.Fori(2, NBATCH // 2) as r:
                        turn(r * 2, 0, True)
                        turn_logits(r * 2 - 2, 0, True)
                        route(r * 2 - 1, 1)
                        turn(r * 2 + 1, 1, True)
                        turn_logits(r * 2 - 1, 1, True)
                        route(r * 2, 0)
                    turn_logits(NBATCH - 2, 0, True)
                    route(NBATCH - 1, 1)
                    turn_logits(NBATCH - 1, 1, True)
                    pe.sem_inc(gat_free, GR)
                    pe.wait_ge(onehot_ready, 1)
                    pe.wait_ge(consts, 1)
                    for half in range(2):
                        oh = onehot[:, half * 512:(half + 1) * 512]
                        pe.matmul(pb[:, half, :], tri, oh, start=True, stop=True)
                        last = pe.matmul(pb[:, 2 + half, :], ones, oh, start=True, stop=True)
                    last.then_inc(counts_ready, 1)
                    pe.wait_ge(hots_ready, 1)
                    for t in range(NT):
                        last = pe.matmul(pb[:, 4, 0:2 * NSLOT], lo_hot[:, t, :],
                                         hi_both[:, t, :, :].rearrange("p v n -> p (v n)"),
                                         start=(t == 0), stop=(t == NT - 1))
                    last.then_inc(slots_ready, 1)
                    pe.wait_ge(owner_ready, 1)
                    if load:
                        pe.wait_ge(load.experts_ready, 8)
                    with pe.Fori(0, NSLOT // (2 * GR)) as r:
                        def turn_tile(n):
                            pe.wait_ge(gathered[n % GR], 32 * r + (16 + n // GR * 16))
                            for k in range(KC):
                                last = pe.transpose(pb[:, n % 4, k * P:(k + 1) * P],
                                                    gat[:, n % GR, k * P:(k + 1) * P], ident[:, :])
                            last.then_inc(gatT_psum, 1)

                        turn_tile(0)
                        _, fours = nc.values_load_multi_w_load_instructions(
                            packed_i[0:1, bass.ds(r * (GR // 2), GR // 2)], engines=(mybir.EngineType.PE,), min_val=0,
                            max_val=E ** 4 - 1)
                        for n in range(2 * GR):
                            if n < 2 * GR - 1:
                                turn_tile(n + 1)
                            w0 = pe.snap(fours[n // 4] // E ** (n % 4) % E * (KC * C))
                            pe.wait_ge(gatT_ready, r * (2 * GR) + (n + 1))
                            pe.sem_inc(gat_free, 1)
                            pe.wait_ge(y_ready, r * (2 * GR) + (n + 1))
                            for k in range(KC):
                                last = pe.matmul(pb[:, 4 + n % 4, 0:C], gatT[:, n % 4, k, :],
                                                 arena[:, bass.ds(w0 + k * C, C)],
                                                 start=(k == 0), stop=(k == KC - 1))
                            last.then_inc(y_psum, 1)

                @block.sync
                def _(sp):
                    sp.sem_inc(back_free, GR)
                    sp.sem_inc(y_ready, 4)
                    def store_normed(b, h, ready):
                        sp.wait_ge(xn_ready, ready)
                        sp.dma_start(xn_dram[bass.ds(b * T, T), :].rearrange("(t p) c -> p t c", p=P),
                                     xn2[:, h, :, :]).then_inc(xn_stored[h], 16)

                    if load:
                        for b in range(NBATCH):
                            store_normed(b, b % 2, b * TPB + TPB)
                            sp.dma_start(arena[:, b * 2048:(b + 1) * 2048],
                                         ffn_masks[:, b * 2048:(b + 1) * 2048]).then_inc(load.masks[b], 16)
                    else:
                        with sp.Fori(0, NBATCH // 2) as r:
                            for h in range(2):
                                store_normed(r * 2 + h, h, r * (2 * TPB) + (h * TPB + TPB))
                    for h in range(2):
                        sp.wait_ge(xn_stored[h], 16 * (NBATCH // 2))
                    sp.sem_inc(xn_all, 1)
                    with sp.Fori(0, NSLOT // GR) as r:
                        for n in range(GR):
                            sp.wait_ge(y_ready, r * GR + (n + 5))
                            sp.dma_start(slots_dram[bass.ds((r * GR + n) * P, P), :], yout[:, n, :])\
                              .then_inc(y_stored[n], 16)
                    for n in range(GR):
                        sp.wait_ge(y_stored[n], 16 * (NSLOT // GR))
                    sp.sem_inc(y_all, 1)
                    if load:
                        sp.wait_ge(load.weights, 16 * 13)

        def decay_attention(name):
            with Semaphores(name) as sem, ExitStack() as bc:
                carve = carver()
                F = KC * T

                def kt(v):
                    return v.rearrange("p (k t) -> p k t", k=KC)

                decay = carve(F)
                heads = carve(H // KC)
                spread = carve(KC * P).rearrange("p (k m) -> p k m", k=KC)
                rate = carve(KC)
                relu_q, exp_q, relu_k, exp_k = carve(F), carve(F), carve(F), carve(F)
                kv, run_kv, run_k, qkv, mixed = carve(F), carve(F), carve(F), carve(F), carve(F)
                den = carve(TPB * H)
                rden_t = carve(T)
                param_loaded, rate_exp, consts = sem("param_loaded"), sem("rate_exp"), sem("consts")
                mv_ready, rstd_ready, xn_ready = sem("mv_ready"), sem("rstd_ready"), sem("xn_ready")
                xnT_psum, xnT_ready, q_psum, k_psum, v_psum = (sem("xnT_psum"), sem("xnT_ready"), sem("q_psum"),
                                                               sem("k_psum"), sem("v_psum"))
                q_read, k_read, v_read, k_used = sem("q_read"), sem("k_read"), sem("v_read"), sem("k_used")
                phi_ready, run_ready, qkv_ready, dots_ready = (sem("phi_ready"), sem("run_ready"), sem("qkv_ready"),
                                                               sem("dots_ready"))
                den_psum, rden_ready, turned_psum, turned_ready, spread_psum = (
                    sem("den_psum"), sem("rden_ready"), sem("turned_psum"), sem("turned_ready"), sem("spread_psum"))
                mixed_ready, o_psum, x_added = sem("mixed_ready"), sem("o_psum"), sem("x_added")
                block = bc.enter_context(nc.Block())

                def run(engine, body):
                    body(0, None, 1)
                    with engine.Fori(0, NBATCH - 2) as i:
                        body(i + 1, i, i + 2)
                    body(NBATCH - 1, NBATCH - 2, None)
                    body(None, NBATCH - 1, None)

                @block.sync
                def _(sp):
                    sp.dma_start(rate, dec_param).then_inc(param_loaded, 16)

                @block.gpsimd
                def _(pool):
                    pool.memset(heads, 1.0)
                    pool.memset(spread[:, :, :], 1.0)
                    pool.drain()
                    pool.affine_select(out=heads, in_=heads, compare_op=ALU.is_ge, fill=0.0, base=0,
                                       pattern=[[-HD, H // KC]], channel_multiplier=1)
                    pool.affine_select(out=spread[:, :, :], in_=spread[:, :, :], compare_op=ALU.is_ge, fill=0.0, base=0,
                                       pattern=[[P, KC], [1, P]], channel_multiplier=-HD)
                    pool.drain()
                    pool.affine_select(out=heads, in_=heads, compare_op=ALU.is_ge, fill=0.0, base=HD - 1,
                                       pattern=[[HD, H // KC]], channel_multiplier=-1)
                    pool.affine_select(out=spread[:, :, :], in_=spread[:, :, :], compare_op=ALU.is_ge, fill=0.0,
                                       base=HD - 1, pattern=[[-P, KC], [-1, P]], channel_multiplier=HD)
                    pool.drain().then_inc(consts, 1)
                    norm_rstd(pool, 0, mv_ready, rstd_ready)

                    def body(b, i, n):
                        if n is not None:
                            norm_rstd(pool, n, mv_ready, rstd_ready)
                        if b is not None:
                            pool.wait_ge(run_ready, b + 1)
                            pool.wait_ge(phi_ready, b + 1)
                            if i is not None:
                                pool.wait_ge(mixed_ready, i + 1)
                            pool.tensor_tensor(qkv, relu_q, run_kv, ALU.mult).then_inc(qkv_ready, 1)
                    run(pool, body)

                @block.scalar
                def _(act):
                    act.wait_ge(param_loaded, 16)
                    act.activation(rate, rate, ACT.Exp, scale=-1.0).then_inc(rate_exp, 1)

                    def copy_x(n):
                        act.wait_ge(xnT_psum, n + 1)
                        act.activation(xnT[:, :, :].rearrange("p k t -> p (k t)"),
                                       pb[:, 6:8, :].rearrange("p k t -> p (k t)"), ACT.Copy).then_inc(xnT_ready, 1)

                    def relu_exp(bank, got, rel, ex, read, b):
                        src = pb[:, bank:bank + 2, :].rearrange("p k t -> p (k t)")
                        act.wait_ge(got, b + 1)
                        act.activation(rel, src, ACT.Relu)
                        act.activation(ex, src, ACT.Exp).then_inc(read, 1)

                    def body(b, i, n):
                        if b is not None:
                            if i is not None:
                                act.wait_ge(k_used, i + 1)
                            relu_exp(4, k_psum, relu_k, exp_k, k_read, b)
                        if i is not None:
                            act.wait_ge(turned_psum, i + 1)
                            act.activation(rden_t[0:H, :], pb[0:H, 3, :], ACT.Copy).then_inc(turned_ready, 1)
                        if b is not None:
                            if i is not None:
                                act.wait_ge(qkv_ready, i + 1)
                            relu_exp(2, q_psum, relu_q, exp_q, q_read, b)
                        if n is not None:
                            copy_x(n)
                    copy_x(0)
                    run(act, body)

                @block.tensor
                def _(pe):
                    pe.wait_ge(consts, 1)

                    def project(bank, col, done):
                        for c in range(KC):
                            for k in range(KC):
                                last = pe.matmul(pb[:, bank + c, :], wdec[:, k, col + c * P:col + (c + 1) * P],
                                                 xnT[:, k, :], start=(k == 0), stop=(k == KC - 1))
                        last.then_inc(done, 1)

                    def body(b, i, n):
                        if i is not None:
                            pe.wait_ge(q_read, i + 1)
                            pe.wait_ge(dots_ready, i + 1)
                            for t in range(TPB):
                                for c in range(KC):
                                    at = t * H + c * (H // KC)
                                    last = pe.matmul(pb[:, 2, at:at + H // KC], kt(run_k)[:, c, t * P:(t + 1) * P], heads,
                                                     start=True, stop=True)
                            last.then_inc(den_psum, 1)
                        if b is not None:
                            pe.wait_ge(xnT_ready, b + 1)
                            if i is not None:
                                pe.wait_ge(k_read, i + 1)
                            project(4, C, k_psum)
                        if i is not None:
                            pe.wait_ge(rden_ready, i + 1)
                            for t in range(TPB):
                                last = pe.transpose(pb[0:H, 3, t * P:(t + 1) * P], den[:, t * H:(t + 1) * H], ident[:, :])
                            last.then_inc(turned_psum, 1)
                        if b is not None:
                            project(6, 2 * C, v_psum)
                        if i is not None:
                            pe.wait_ge(x_added, i + 1)
                            pe.wait_ge(turned_ready, i + 1)
                            for c in range(KC):
                                last = pe.matmul(pb[:, c, :], spread[0:H, c, :], rden_t[0:H, :], start=True, stop=True)
                            last.then_inc(spread_psum, 1)
                        if b is not None:
                            project(2, 0, q_psum)
                        if n is not None:
                            pe.wait_ge(v_read, b + 1)
                            transpose_tokens(pe, n, xn_ready, xnT_psum, 6)
                        if i is not None:
                            pe.wait_ge(mixed_ready, i + 1)
                            for t in range(TPB):
                                for c in range(KC):
                                    last = pe.matmul(pb[:, t // 2, (t % 2) * C:(t % 2 + 1) * C],
                                                     kt(mixed)[:, c, t * P:(t + 1) * P], wdec_out[:, c, :],
                                                     start=(c == 0), stop=(c == KC - 1))
                            last.then_inc(o_psum, 1)
                    pe.sem_inc(x_added, 1)
                    transpose_tokens(pe, 0, xn_ready, xnT_psum, 6)
                    run(pe, body)

                @block.vector
                def _(dve):
                    dve.wait_ge(rate_exp, 1)
                    dve.tensor_scalar(rate, rate, 1.0, None, ALU.add)
                    dve.drain()
                    dve.reciprocal(rate, rate)
                    dve.memset(decay, 1.0)
                    dve.drain()
                    for c in range(KC):
                        dve.tensor_scalar(kt(decay)[:, c, :], kt(decay)[:, c, :], rate[:, c:c + 1], None, ALU.mult)
                    dve.drain()
                    dve.memset(kt(decay)[:, :, 0:1], 0.0)
                    norm_stats(dve, 0, mv_ready, rstd_ready)
                    norm_apply(dve, 0, rstd_ready, xn_ready)

                    def body(b, i, n):
                        if n is not None:
                            norm_stats(dve, n, mv_ready, rstd_ready)
                        if i is not None:
                            dve.wait_ge(den_psum, i + 1)
                            dve.tensor_scalar(den, pb[:, 2, 0:TPB * H], 1e-6, None, ALU.max)
                            dve.drain()
                            dve.reciprocal(den, den).then_inc(rden_ready, 1)
                        if b is not None:
                            dve.wait_ge(k_read, b + 1)
                            dve.scalar_tensor_tensor(relu_k, exp_k, 1.0, relu_k, ALU.min, ALU.add)
                            dve.drain()
                            dve.tensor_tensor_scan(run_k, decay, relu_k, 0.0, ALU.mult, ALU.add)
                            dve.wait_ge(v_psum, b + 1)
                            dve.tensor_tensor(kv, pb[:, 6:8, :].rearrange("p k t -> p (k t)"), relu_k,
                                              ALU.mult).then_inc(v_read, 1)
                            dve.drain().then_inc(k_used, 1)
                            if i is not None:
                                dve.wait_ge(qkv_ready, i + 1)
                            dve.tensor_tensor_scan(run_kv, decay, kv, 0.0, ALU.mult, ALU.add).then_inc(run_ready, 1)
                        if n is not None:
                            dve.wait_ge(xnT_psum, b + 1)
                            norm_apply(dve, n, rstd_ready, xn_ready)
                        if i is not None:
                            dve.wait_ge(spread_psum, i + 1)
                            dve.wait_ge(qkv_ready, i + 1)
                            dve.tensor_tensor(mixed, qkv, pb[:, 0:2, :].rearrange("p k t -> p (k t)"),
                                              ALU.mult).then_inc(mixed_ready, 1)
                        if b is not None:
                            dve.wait_ge(q_read, b + 1)
                            dve.scalar_tensor_tensor(relu_q, exp_q, 1.0, relu_q, ALU.min, ALU.add).then_inc(phi_ready, 1)
                            dve.drain()
                            dve.tensor_tensor(run_k, run_k, relu_q, ALU.mult).then_inc(dots_ready, 1)
                        if i is not None:
                            dve.wait_ge(o_psum, i + 1)
                            xi = x_sb[:, bass.ds(i * TPB, TPB), :].rearrange("p t c -> p (t c)")
                            dve.tensor_tensor(xi, pb[:, 0:2, :].rearrange("p k t -> p (k t)"), xi,
                                              ALU.add).then_inc(x_added, 1)
                    run(dve, body)

        def score_columns(causal, half):
            if not causal:
                return [(s * 256, half * 256, 256) for s in range(TPB)]
            if half == 0:
                return [(0, 0, 256), (256, 128, 128)]
            return [(0, 256, 256), (256, 256, 256), (512, 256, 256), (768, 384, 128)]

        def attention_plan(causal):

            def rows_of(rows, offset):
                out = []
                for r in rows:
                    out.append(("row", offset, r))
                    if r % 16 == 1 and r > 16:
                        out.append(("turn_max", offset, r // 16 - 1))
                return out

            def values(s, offset):
                n, t = divmod(s - 5, TPB)
                t -= TPB - len(score_columns(causal, n % 2))
                out = []
                if 0 <= n < 2 * NG and t >= 0:
                    out.append(("pv", offset, n, t))
                    if n % 2 and t == TPB - 1:
                        out.append(("unload", offset, n // 2))
                return out

            def divisions(s, offset):
                out = []
                for late, kind in ((1, "divide"), (2, "turn_back")):
                    n, t = divmod(s - late - 5, TPB)
                    g = n // 2
                    if 0 <= n < 2 * NG and n % 2 and t == TPB - 1 and (g % 2 or kind == "divide"):
                        out.append((kind, offset, g))
                return out

            def slot(s, rows, now, coming):
                out = list(rows[:1])
                tail = s - NUNITS
                out += divisions(s, now) if now is not None else []
                out += divisions(tail, coming) if coming is not None else []
                if coming is not None and s == 14:
                    out += [("turn_x", coming, k) for k in range(KC)]
                if coming is not None and s in (15, 17, 19, 21):
                    out += [("rest", coming, (s - 15) // 2), ("second", coming, (s - 15) // 2)]
                out += values(s, now) if now is not None else []
                out += values(tail, coming) if coming is not None else []
                out += rows[1:]
                if s == 20 and now is not None:
                    out.append(("turn_max", now, NG - 1))
                if tail < 0 and now is not None:
                    out.append(("unit", now, s))
                if tail >= 0 and coming is not None:
                    out.append(("unit", coming, tail))
                if coming is not None:
                    if s in (10, 11):
                        out += [("stats", coming, 2 * s - 20), ("stats", coming, 2 * s - 19)]
                    if s == 11:
                        out.append(("mean", coming))
                    if s == 12:
                        out += [("normed", coming, 0), ("normed", coming, 2)]
                    if s in (14, 16, 18, 20):
                        out.append(("project", coming, (s - 14) // 2))
                    if now is not None and tail == 2:
                        out.append(("value", coming, 0, 2))
                    if now is not None and tail in (3, 4):
                        out.append(("value", coming, tail - 1, 1))
                if now is not None and tail in (7, 8, 9):
                    out.append(("out", now, tail - 7))
                if now is not None and tail == 9:
                    out.append(("out", now, TPB - 1))
                return out

            def rows_in(s, offset):
                first = 2 * (s + AHEAD) - LAG.get(s - 1, 0)
                end = 2 * (s + AHEAD + 1) - LAG.get(s, 0)
                return rows_of([r for r in range(first, end) if 0 <= r < NROWS], offset)

            prologue = [("stats", 0, t) for t in range(TPB)] + [("mean", 0), ("normed", 0, 0), ("normed", 0, 2)]
            prologue += [("turn_x", 0, k) for k in range(KC)]
            for n in range(NQK):
                prologue += [("project", 0, n), ("rest", 0, n)]
                if n:
                    prologue.append(("second", 0, n - 1))
            prologue += [("second", 0, NQK - 1), ("value", 0, 0, 2), ("value", 0, 2, 1), ("value", 0, 3, 1)]
            early = rows_of(range(2 * (HEAD + AHEAD)), 0)
            first = early.index(("turn_max", 0, 0)) + 1
            prologue += early[:first]
            left = early[first:]
            for s in range(HEAD):
                share = left[len(left) * s // HEAD:len(left) * (s + 1) // HEAD]
                prologue += slot(NUNITS + s, share, None, 0)

            steady = []
            for s in range(HEAD, HEAD + NUNITS):
                steady += slot(s, rows_in(s, 0) + rows_in(s - NUNITS, 1), 0, 1)
            final = []
            for s in range(HEAD, HEAD + NUNITS):
                final += slot(s, rows_in(s, 0), 0, None)
            return prologue, steady, final

        NQK = 2 * KC
        NROWS = H * TPB
        NUNITS = H * 2
        HEAD = 10
        AHEAD = 11
        LAG = {11: 1, 12: 2, 13: 2, 14: 1, 15: 1, 17: -1, 18: -2, 19: -2}
        RING = (4, 5, 7)
        IN_RING = ("row", "turn_max", "turn_x", "project", "value", "out")
        READS = ("row", "turn_max", "rest", "value", "out")

        def attention(name, causal, to_dram):
            w, w_out = (wcau, wcau_out) if causal else (wfull, wfull_out)
            prologue, steady, final = attention_plan(causal)

            def ring_numbers(plan):
                out, n, d = [], 0, 0
                for step in plan:
                    out.append((n, d))
                    n += step[0] in IN_RING
                    d += step[0] in READS
                return out, n, d

            def reads_through(plan, numbers, step):
                if step[0] == "project":
                    step = ("rest",) + step[1:]
                return numbers[plan.index(step)][1] + 1

            _, ring_pro, read_pro = ring_numbers(prologue)
            _, ring_all, read_all = ring_numbers(steady)
            assert ring_all % len(RING) == 0

            def bank_of(j, before):
                return RING[(j + (ring_pro if before else 0)) % len(RING)]

            with Semaphores(name) as sem, ExitStack() as bc:
                carve = carver()
                parts = [carve(NQK * T // 2, BF16).rearrange("p (n t) -> p n t", n=NQK) for _ in range(3)]
                rest = carve(NQK * T).rearrange("p (n t) -> p n t", n=NQK)
                v_aug = carve(TPB * H * SLOT).rearrange("p (s h d) -> p s h d", s=TPB, h=H)
                o_t = carve(NG // 2 * T).rearrange("p (g t) -> p g t", g=NG // 2)
                turned = carve(T)
                mixed = carve(T)
                den = carve(T // SLOT)
                row_max = carve(NG * 16).rearrange("p (g n) -> p g n", g=NG)
                shift_hi = carve(NG * P // 2, BF16).rearrange("p (g n) -> p g n", g=NG)
                shift_lo = carve(NG * P // 2, BF16).rearrange("p (g n) -> p g n", g=NG)

                mv_ready, rstd_ready, xn_ready = sem("mv_ready"), sem("rstd_ready"), sem("xn_ready")
                ring_full = sem("ring_full")
                ring_read = sem("ring_read")
                xnT_ready = sem("xnT_ready")
                part0, part1, part2 = sem("part0"), sem("part1"), sem("part2")
                stacked = [sem(f"stacked{c}") for c in range(KC)]
                aug_set, shift_ready = sem("aug_set"), sem("shift_ready")
                shifted = [sem(f"shifted{g}") for g in range(NG)]
                unit_psum, unit_exp, pv_psum, pv_read = sem("unit_psum"), sem("unit_exp"), sem("pv_psum"), sem("pv_read")
                o_ready, x_biased = sem("o_ready"), sem("x_biased")
                x_done = sem("x_done")
                stored = sem("stored")
                stack_turn = sem("stack_turn")
                block = bc.enter_context(nc.Block())

                def run(engine, steps):
                    steps(prologue, 0, 0, 0, [])
                    with engine.Fori(0, NBATCH - 1) as i:
                        steps(steady, i, i * ring_all + ring_pro, i * read_all + read_pro, steady)
                    i = NBATCH - 1
                    steps(final, i, i * ring_all + ring_pro, i * read_all + read_pro, steady)

                @block.gpsimd
                def _(pool):
                    pool.memset(kst[96:98, :], 1.0)
                    pool.drain()
                    pool.memset(v_aug[:, :, :, HD:SLOT], 1.0)
                    pool.drain().then_inc(aug_set, 1)

                    def steps(plan, i, ring0, read0, before):
                        for step in plan:
                            b = i + step[1]
                            if step[0] == "mean":
                                norm_rstd(pool, b, mv_ready, rstd_ready)
                            if step[0] == "second":
                                n = step[2]
                                pool.wait_ge(part1, NQK * b + (n + 1))
                                pool.tensor_tensor(parts[2][:, n, :], rest[:, n, :], parts[1][:, n, :],
                                                   ALU.subtract).then_inc(part2, 1)
                                if n == NQK - 1 and not causal:
                                    pool.wait_ge(xn_ready, TPB * b + TPB)
                                    xi = x_sb[:, bass.ds(b * TPB, TPB), :]
                                    pool.tensor_tensor(xi, xi, bias_o[:, :].unsqueeze(1).broadcast_to([P, TPB, C]),
                                                       ALU.add).then_inc(x_biased, 1)
                    run(pool, steps)

                @block.sync
                def _(sp):
                    def stack_chunk(n, count):
                        c, is_k = n // 2, n % 2
                        stack, order = (kst, PARTS_K) if is_k else (qst, PARTS_Q)
                        for part, done in ((0, part0), (1, part1), (2, part2)):
                            sp.wait_ge(done, count)
                            for slot, p in enumerate(order):
                                if p == part:
                                    sp.dma_start(stack[slot * HD:(slot + 1) * HD, c * 4096:(c + 1) * 4096],
                                                 parts[part][:, n, :]).then_inc(stacked[c], 16)

                    def store_shift(g, count):
                        sp.wait_ge(shift_ready, count)
                        for row, src in ((96, shift_hi), (97, shift_lo)):
                            sp.dma_start(qst[row:row + 1, g * 2048:(g + 1) * 2048],
                                         src[0:16, g, :]).then_inc(shifted[g], 16)

                    for n in range(NQK):
                        stack_chunk(n, n + 1)
                    store_shift(0, 1)

                    def iteration(i, keep, stores):
                        chunk_done = [keep(NQK * i + (NQK + n + 1)) for n in range(NQK)]
                        shift_done = [keep(NG * i + (g + 1)) for g in range(1, NG + 1)]
                        half_done, all_done = keep(NUNITS * i + NUNITS // 2), keep(NUNITS * i + NUNITS)
                        store_shift(1, shift_done[0])
                        store_shift(2, shift_done[1])
                        if stores:
                            store_x(i - 1, i)
                        sp.wait_ge(unit_psum, half_done)
                        sp.sem_inc(stack_turn, 1)
                        stack_chunk(0, chunk_done[0])
                        stack_chunk(1, chunk_done[1])
                        store_shift(3, shift_done[2])
                        store_shift(0, shift_done[3])
                        sp.wait_ge(unit_psum, all_done)
                        sp.sem_inc(stack_turn, 1)
                        stack_chunk(2, chunk_done[2])
                        stack_chunk(3, chunk_done[3])

                    def store_x(b, finished):
                        sp.wait_ge(x_done, finished)
                        sp.dma_start(out[bass.ds(b * T, T), :].rearrange("(t p) c -> p t c", p=P),
                                     x_sb[:, bass.ds(b * TPB, TPB), :]).then_inc(stored, 16)

                    if to_dram:
                        iteration(0, int, False)
                        with sp.Fori(1, NBATCH - 1) as i:
                            iteration(i, sp.snap, True)
                    else:
                        with sp.Fori(0, NBATCH - 1) as i:
                            iteration(i, sp.snap, False)
                    for g in range(1, NG):
                        store_shift(g, NG * (NBATCH - 1) + g + 1)
                    if to_dram:
                        store_x(NBATCH - 2, NBATCH - 1)
                        store_x(NBATCH - 1, NBATCH)
                        sp.wait_ge(stored, 16 * NBATCH)
                    for g in range(NG):
                        sp.wait_ge(shifted[g], 32 * NBATCH)

                @block.scalar
                def _(act):
                    def steps(plan, i, ring0, read0, before):
                        numbers, _, _ = ring_numbers(plan)
                        for step, (j, d) in zip(plan, numbers):
                            if step[0] == "turn_x":
                                act.wait_ge(ring_full, ring0 + (j + 1))
                                act.activation(xnT[:, step[2], :], pb[:, bank_of(j, before), :], ACT.Copy).then_inc(xnT_ready, 1)
                            elif step[0] == "project":
                                n = step[2]
                                act.wait_ge(ring_full, ring0 + (j + 1))
                                if causal:
                                    act.activation(parts[0][:, n, :], pb[:, bank_of(j, before), :], ACT.Copy).then_inc(part0, 1)
                                else:
                                    act.activation(parts[0][:, n, :], pb[:, bank_of(j, before), :], ACT.Identity,
                                                   bias=bias_qk[:, n % 2, n // 2:n // 2 + 1]).then_inc(part0, 1)
                            elif step[0] == "second":
                                act.wait_ge(ring_read, read0 + reads_through(plan, numbers, ("rest",) + step[1:]))
                                n = step[2]
                                act.activation(parts[1][:, n, :], rest[:, n, :], ACT.Copy).then_inc(part1, 1)
                            elif step[0] == "unit":
                                b, u = i + step[1], step[2]
                                half, hh = (u // G) % 2, u % G
                                off, _, m = score_columns(causal, half)[-1]
                                act.wait_ge(unit_psum, NUNITS * b + (u + 1))
                                bank = 2 * (u % 2)
                                act.activation(probs[:, (u // G) % 2, hh, 0:off + m],
                                               pb[:, bank:bank + 2, :].rearrange("p k t -> p (k t)")[:, 0:off + m],
                                               ACT.Exp, scale=HD ** -0.5).then_inc(unit_exp, 1)
                    run(act, steps)

                @block.tensor
                def _(pe):
                    pe.sem_inc(pv_read, 1)
                    pe.wait_ge(aug_set, 1)

                    def ring_bank(j, ring0, read0, numbers, plan, before):
                        k, source, r0 = j - 3, plan, read0
                        if k < 0 and not before:
                            return bank_of(j, before)
                        if k < 0:
                            items = [s for s in before if s[0] in IN_RING]
                            after = len(items[len(items) + k + 1:])
                            assert all(s[0] in READS for s in items[k:])
                            pe.wait_ge(ring_read, read0 - after)
                        else:
                            at = [n for n, s in enumerate(plan) if s[0] in IN_RING][k]
                            if plan[at][0] == "turn_x":
                                pe.wait_ge(xnT_ready, KC * (before_batch[0] + plan[at][1]) + (plan[at][2] + 1))
                            else:
                                pe.wait_ge(ring_read, read0 + reads_through(plan, numbers, plan[at]))
                        return bank_of(j, before)

                    before_batch = [0]

                    def steps(plan, i, ring0, read0, before):
                        numbers, _, _ = ring_numbers(plan)
                        before_batch[0] = i
                        for step, (j, d) in zip(plan, numbers):
                            kind = step[0]
                            if kind in IN_RING:
                                bank = ring_bank(j, ring0, read0, numbers, plan, before)
                                b = i + step[1]
                            if kind == "row":
                                r = step[2]
                                h, t = r // TPB, r % TPB
                                if r % 32 == 0:
                                    pe.wait_ge(stacked[h // 8], 192 * b + 192)
                                width = P * (t + 1) if causal else T
                                last = pe.matmul(pb[:, bank, 0:width], qst_h[0:96, h, t * P:(t + 1) * P],
                                                 kst_h[0:96, h, 0:width], start=True, stop=not causal)
                                if causal:
                                    last = pe.matmul(pb[:, bank, t * P:(t + 1) * P], ident_bf[:, :], mask_ts[:, :],
                                                     start=False, stop=True)
                            elif kind == "turn_max":
                                g = step[2]
                                row = ("row", step[1], 16 * g + 15)
                                if row in plan:
                                    pe.wait_ge(ring_read, read0 + reads_through(plan, numbers, row))
                                last = pe.transpose(pb[0:16, bank, 0:P], row_max[:, g, :], ident[:, :])
                            elif kind == "turn_x":
                                k = step[2]
                                for t in range(TPB):
                                    pe.wait_ge(xn_ready, TPB * b + (t + 1))
                                    last = pe.transpose(pb[:, bank, t * P:(t + 1) * P], xn[:, t, k * P:(k + 1) * P],
                                                        ident[:, :])
                            elif kind == "project":
                                n = step[2]
                                pe.wait_ge(xnT_ready, KC * b + KC)
                                c, is_k = n // 2, n % 2
                                for k in range(KC):
                                    last = pe.matmul(pb[:, bank, :], w[:, k, is_k, c * P:(c + 1) * P], xnT[:, k, :],
                                                     start=(k == 0), stop=(k == KC - 1))
                            elif kind == "value":
                                for n in range(step[3]):
                                    t = step[2] + n
                                    for k in range(KC):
                                        last = pe.matmul(pb[:, bank, n * C:(n + 1) * C],
                                                         xnT[:, k, t * P:(t + 1) * P], w[:, k, 2, :],
                                                         start=(k == 0), stop=(k == KC - 1))
                            elif kind == "out":
                                t = step[2]
                                pe.wait_ge(o_ready, NG // 2 * (b + 1))
                                for n in range(NG // 2):
                                    last = pe.matmul(pb[:, bank, 0:C], o_t[:, n, t * P:(t + 1) * P], w_out[:, n, :],
                                                     start=(n == 0), stop=(n == NG // 2 - 1))
                            elif kind == "unit":
                                b, u = i + step[1], step[2]
                                g, half, hh = u // 8, (u // G) % 2, u % G
                                h = g * G + hh
                                if u % 8 == 0:
                                    pe.wait_ge(shifted[g], 32 * b + 32)
                                if u >= 2 or before:
                                    pe.wait_ge(unit_exp, NUNITS * b + u - 1)
                                flat = pb[:, 2 * (u % 2):2 * (u % 2) + 2, :].rearrange("p k t -> p (k t)")
                                for s, (off, q0, m) in enumerate(score_columns(causal, half)):
                                    diagonal = causal and q0 <= s * P
                                    last = pe.matmul(flat[:, off:off + m], kst_h[0:ROWS, h, s * P:(s + 1) * P],
                                                     qst_h[0:ROWS, h, q0:q0 + m], start=True, stop=not diagonal)
                                    if diagonal:
                                        at = off + s * P - q0
                                        last = pe.matmul(flat[:, at:at + P], ident_bf[:, :], mask_st[:, :],
                                                         start=False, stop=True)
                                last.then_inc(unit_psum, 1)
                            elif kind == "pv":
                                b, n, s = i + step[1], step[2], step[3]
                                g, half = n // 2, n % 2
                                cols = score_columns(causal, half)
                                off, q0, m = cols[s]
                                if n < 2:
                                    value = ("value", step[1], 0, 2) if s < 2 else ("value", step[1], s, 1)
                                    if value in plan:
                                        pe.wait_ge(ring_read, read0 + reads_through(plan, numbers, value))
                                if s == 0:
                                    pe.wait_ge(unit_exp, NUNITS * b + G * (n + 1))
                                    if half == 0:
                                        pe.wait_ge(pv_read, NG * b + (g + 1))
                                for hh in range(G):
                                    end = pe.matmul(pb[hh * SLOT:(hh + 1) * SLOT, 6, q0:q0 + m],
                                                    v_aug[:, s, g * G + hh, :], probs[:, n % 2, hh, off:off + m],
                                                    start=(s == 0), stop=(s == len(cols) - 1))
                                if half == 1 and s == len(cols) - 1:
                                    end.then_inc(pv_psum, 1)
                            if kind in IN_RING:
                                last.then_inc(ring_full, 1)
                    run(pe, steps)

                @block.vector
                def _(dve):
                    dve.wait_ge(aug_set, 1)

                    def steps(plan, i, ring0, read0, before):
                        numbers, _, _ = ring_numbers(plan)
                        for step, (j, d) in zip(plan, numbers):
                            kind, bank = step[0], bank_of(j, before)
                            if kind in READS:
                                b = i + step[1]
                                if kind == "rest":
                                    dve.wait_ge(part0, NQK * b + (step[2] + 1))
                                    if before:
                                        dve.wait_ge(part2, NQK * b)
                                    bank = bank_of(numbers[plan.index(("project",) + step[1:])][0], before)
                                else:
                                    dve.wait_ge(ring_full, ring0 + (j + 1))
                            if kind == "stats":
                                dve.bn_stats(stats[:, step[2], :], x_sb[:, bass.ds((i + step[1]) * TPB + step[2], 1), :])
                            elif kind == "mean":
                                norm_mean(dve, mv_ready)
                            elif kind == "normed":
                                norm_apply(dve, i + step[1], rstd_ready, xn_ready, (step[2], step[2] + 1))
                            elif kind == "row":
                                r = step[2]
                                width = P * (r % TPB + 1) if causal else T
                                dve.tensor_reduce(row_max[:, r // 16, r % 16:r % 16 + 1], pb[:, bank, 0:width],
                                                  AX_X, ALU.max).then_inc(ring_read, 1)
                            elif kind == "turn_max":
                                g = step[2]
                                dve.tensor_scalar(shift_hi[0:16, g, :], pb[0:16, bank, 0:P], -1.0, None, ALU.mult)
                                dve.drain()
                                dve.scalar_tensor_tensor(shift_lo[0:16, g, :], pb[0:16, bank, 0:P], -1.0,
                                                         shift_hi[0:16, g, :], ALU.mult,
                                                         ALU.subtract).then_inc(ring_read, 1)
                                dve.drain().then_inc(shift_ready, 1)
                            elif kind == "rest":
                                n = step[2]
                                if causal:
                                    dve.tensor_tensor(rest[:, n, :], pb[:, bank, :], parts[0][:, n, :],
                                                      ALU.subtract).then_inc(ring_read, 1)
                                else:
                                    dve.scalar_tensor_tensor(rest[:, n, :], pb[:, bank, :],
                                                             bias_qk[:, n % 2, n // 2:n // 2 + 1], parts[0][:, n, :],
                                                             ALU.add, ALU.subtract).then_inc(ring_read, 1)
                            elif kind == "value":
                                src = pb[:, bank, :].rearrange("p (s h d) -> p s h d", s=2, h=H)
                                for t in range(step[3]):
                                    dst = v_aug[:, step[2] + t, :, 0:HD]
                                    if causal:
                                        last = dve.tensor_copy(dst, src[:, t, :, :])
                                    else:
                                        last = dve.tensor_tensor(dst, src[:, t, :, :],
                                                                 bias_v[:, :].rearrange("p (h d) -> p h d", h=H), ALU.add)
                                last.then_inc(ring_read, 1)
                            elif kind == "unload":
                                b, g = i + step[1], step[2]
                                dve.drain()
                                dve.wait_ge(pv_psum, NG * b + (g + 1))
                                dve.transpose(turned, pb[:, 6, :]).then_inc(pv_read, 1)
                            elif kind == "divide":
                                g = step[2]
                                dve.drain()
                                t3 = turned.rearrange("p (b r) -> p b r", r=SLOT)
                                dve.reciprocal(den, t3[:, :, HD])
                                dve.drain()
                                m3 = mixed.rearrange("p (b r) -> p b r", r=SLOT)
                                dve.tensor_tensor(m3[:, :, (g % 2) * HD:(g % 2 + 1) * HD], t3[:, :, 0:HD],
                                                  den.unsqueeze(2).broadcast_to([P, T // SLOT, HD]), ALU.mult)
                            elif kind == "turn_back":
                                g = step[2]
                                dve.drain()
                                dve.transpose(o_t[:, g // 2, :], mixed).then_inc(o_ready, 1)
                            elif kind == "out":
                                if not causal:
                                    dve.wait_ge(x_biased, b + 1)
                                xi = x_sb[:, bass.ds(b * TPB + step[2], 1), :].rearrange("p t c -> p (t c)")
                                dve.scalar_tensor_tensor(xi, pb[:, bank, 0:C], 0.5 if causal else 1.0, xi,
                                                         ALU.mult, ALU.add).then_inc(ring_read, 1)
                                if to_dram and step[2] == TPB - 1:
                                    dve.drain().then_inc(x_done, 1)
                    run(dve, steps)

        with Semaphores("load") as held:
            load = Loads(held)
            with Semaphores("prep") as sem, ExitStack() as bc:
                prepare(sem, load, bc)
            ffn("e0", load)
        for n, layer in list(enumerate(layers))[1:]:
            if layer == "ffn":
                ffn(f"e{n}", None)
            elif layer == "decay":
                decay_attention(f"d{n}")
            elif layer == "causal":
                attention(f"a{n}", True, n == len(layers) - 1)
            elif layer == "full":
                attention(f"a{n}", False, n == len(layers) - 1)


LAYERS = ("ffn", "decay", "ffn", "causal", "full", "causal")


def _laid_out(inp):
    import numpy as np
    H, HD, KC, P, E, C = 16, 16, 2, 128, 32, 256
    a = {k: np.asarray(v) for k, v in inp.items()}

    def chunked(w):
        return w.reshape(KC, P, -1).transpose(1, 0, 2)

    def head_minor(w):
        return w.reshape(C, 2, 8, HD).transpose(0, 1, 3, 2).reshape(C, C)

    def paired_rows(w):
        return w.reshape(2, 2, 4, HD, C).transpose(0, 2, 1, 3, 4).reshape(2, P, C).transpose(1, 0, 2)

    def every_partition(v):
        return np.broadcast_to(v.reshape(1, -1), (P, v.size))

    wa = a["L1_ffn_Wa"]
    q_std, k_std, v, q_low, k_low = np.split(wa, [128, 256, 512, 640], axis=1)

    def with_tail(std, low):
        return np.concatenate([std.reshape(C, H, 8), low.reshape(C, H, 8)], axis=2).reshape(C, C)

    def column_bias(b):
        return b.reshape(2, 8, HD).transpose(2, 1, 0).reshape(P, 2)

    laid = {
        "x_in": a["L0_attn_x"].reshape(-1, C),
        "dec_wqkv": chunked(a["L0_attn_w_qkv"]),
        "dec_wout": chunked(a["L0_attn_w_out"]),
        "dec_param": np.repeat(a["L0_attn_decay_param"], HD).reshape(KC, P).T,
        "ffn_w": chunked(a["L0_ffn_weight"].T).reshape(P, KC * C),
        "ffn_scale": every_partition(a["L0_ffn_scale"]),
        "ffn_masks": a["L0_ffn_expert_masks"].transpose(2, 0, 1).reshape(KC, P, E, C).transpose(1, 2, 0, 3).reshape(P, -1),
        "ffn_router": chunked(a["L0_ffn_router_w"].T),
        "full_wq": chunked(head_minor(a["L1_attn_wq"].T)),
        "full_wk": chunked(head_minor(a["L1_attn_wk"].T)),
        "full_wv": chunked(a["L1_attn_wv"].T),
        "full_wo": paired_rows(a["L1_attn_wo"].T),
        "full_bq": column_bias(a["L1_attn_bq"]),
        "full_bk": column_bias(a["L1_attn_bk"]),
        "full_bv": every_partition(a["L1_attn_bv"]),
        "full_bo": every_partition(a["L1_attn_bo"]),
        "cau_wq": chunked(head_minor(with_tail(q_std, q_low))),
        "cau_wk": chunked(head_minor(with_tail(k_std, k_low))),
        "cau_wv": chunked(v),
        "cau_wo": paired_rows(a["L1_ffn_Wp"]),
        "cau_std": every_partition(np.concatenate([a["L1_ffn_w_std"], a["L1_ffn_w_std"]])),
        "cau_rec": every_partition(np.concatenate([a["L1_ffn_w_rec"], a["L1_ffn_w_rec"]])),
    }
    return {k: np.ascontiguousarray(v) for k, v in laid.items()}


def kernel(**inputs):
    import numpy as _np
    import concourse.bacc as _bacc
    from concourse import mybir as _mybir
    from concourse.bass_utils import run_bass_kernel_spmd as _run

    nc = _bacc.Bacc("TRN2", target_bir_lowering=False, num_devices=1)
    arrays, args = {}, []
    for name, a in _laid_out(inputs).items():
        arrays[f"in_{name}"] = a
        args.append(nc.dram_tensor(f"in_{name}", a.shape, _mybir.dt.from_np(a.dtype), kind="ExternalInput").ap())
    out = nc.dram_tensor("out_x", (8 * 512, 256), _mybir.dt.from_np(_np.dtype("float32")), kind="ExternalOutput").ap()
    macaron_kernel(nc, *args, out, LAYERS)
    r = _run(nc, [arrays], core_ids=[0])
    return r.results[0]["out_x"].reshape(8, 512, 256)
```
